# Optimizing a Trainium2 kernel written in Bass

```python
import numpy as np
import jax
import jax.numpy as jnp

def _softmax(x, axis=-1):
    return jax.nn.softmax(x, axis=axis)
def _gelu(x):
    return jax.nn.gelu(x, approximate=True)
def _silu(x):
    return jax.nn.silu(x)
def _sigmoid(x):
    return jax.nn.sigmoid(x)
def _layernorm(x, axis=-1, eps=1e-5):
    m = jnp.mean(x, axis=axis, keepdims=True)
    v = jnp.var(x, axis=axis, keepdims=True)
    return (x - m) / jnp.sqrt(v + eps)
def _scatter_add(tgt, idx, src, axis=0):
    return tgt.at[idx].add(src)
def _segment_sum(src, seg, n):
    return jax.ops.segment_sum(src, seg, n)

kernel_name = 'mk_metaformer_d2_conv_nhwc128_02ee6d'

def setup_inputs(seed: int = 0):
    np.random.seed(seed)
    _w = jnp.asarray
    def _rec_inputs():
        import jax
        import jax.numpy as jnp
        _gk = jax.random.key(seed)
        x = 7.22e-05 + 1 * jax.random.normal(jax.random.fold_in(_gk, 1), (1, 256, 256, 128), jnp.float32)
        return x
    x = _rec_inputs()
    def _L0_conv_setup():
        import jax, jax.numpy as jnp
        import numpy as np
        H = 4
        C = 32
        CZ = 128
        N = 256
        B = 1
        EPS = 1e-05
        key = jax.random.key(seed)
        ks = jax.random.split(key, 8)
        hc = H * C
        return {'z': jax.random.normal(ks[0], (B, N, N, CZ), dtype=jnp.float32), 'ln_scale': jnp.ones((CZ,), dtype=jnp.float32), 'ln_bias': jnp.zeros((CZ,), dtype=jnp.float32), 'Wq': jax.random.normal(ks[1], (CZ, hc), dtype=jnp.float32) * 0.02, 'Wk': jax.random.normal(ks[2], (CZ, hc), dtype=jnp.float32) * 0.02, 'Wv': jax.random.normal(ks[3], (CZ, hc), dtype=jnp.float32) * 0.02, 'Wb': jax.random.normal(ks[4], (CZ, H), dtype=jnp.float32) * 0.02, 'Wg': jax.random.normal(ks[5], (CZ, hc), dtype=jnp.float32) * 0.02, 'Wo': jax.random.normal(ks[6], (hc, CZ), dtype=jnp.float32) * 0.02}
    _L0_conv_all = _L0_conv_setup()
    _L0_conv_in = {k: v for k, v in _L0_conv_all.items() if k in ('ln_scale', 'ln_bias', 'Wq', 'Wk', 'Wv', 'Wb', 'Wg', 'Wo', )}
    del _L0_conv_all

    def _L0_ffn_setup():
        import jax, jax.numpy as jnp
        import numpy as np
        BN_EPS = 1e-05
        key = jax.random.key(seed)
        k1, k2, k3 = jax.random.split(key, 3)
        B, T, I, H = (64, 2048, 128, 128)
        x = jax.random.normal(k1, (B, T, I), dtype=jnp.float32)
        W = jax.random.normal(k2, (H, I), dtype=jnp.float32) * (1.0 / np.sqrt(I))
        V = jnp.linalg.qr(jax.random.normal(k3, (H, H), dtype=jnp.float32))[0]
        gamma = jnp.ones((H,), dtype=jnp.float32)
        beta = jnp.zeros((H,), dtype=jnp.float32)
        return {'x': x, 'W': W, 'V': V, 'gamma': gamma, 'beta': beta}
    _L0_ffn_all = _L0_ffn_setup()
    _L0_ffn_in = {k: v for k, v in _L0_ffn_all.items() if k in ('W', 'V', 'gamma', 'beta', )}
    del _L0_ffn_all

    def _L1_conv_setup():
        import jax, jax.numpy as jnp
        import numpy as np
        N, H, W, C = (16, 128, 128, 128)
        OUT = 128
        EPS = 1e-05

        def _grid_mlp(x, gh, gw, Wg, bg):
            n, h, w, c = x.shape
            fh, fw = (h // gh, w // gw)
            u = x.reshape(n, gh, fh, gw, fw, c).transpose(0, 1, 3, 2, 4, 5).reshape(n, gh * gw, fh * fw, c)
            u = jnp.einsum('ngpc,kg->nkpc', u, Wg) + bg[:, None, None]
            u = u.reshape(n, gh, gw, fh, fw, c).transpose(0, 1, 3, 2, 4, 5).reshape(n, h, w, c)
            return u
        key = jax.random.key(seed)
        ks = jax.random.split(key, 11)
        s = lambda fan_in: 1.0 / np.sqrt(fan_in)
        return {'x': jax.random.normal(ks[0], (N, H, W, C), dtype=jnp.float32), 'ln_w': jnp.ones((C,), jnp.float32), 'ln_b': jnp.zeros((C,), jnp.float32), 'W1': jax.random.uniform(ks[1], (256, 256), jnp.float32, -s(256), s(256)), 'b1': jax.random.uniform(ks[2], (256,), jnp.float32, -s(256), s(256)), 'W2': jax.random.uniform(ks[3], (64, 64), jnp.float32, -s(64), s(64)), 'b2': jax.random.uniform(ks[4], (64,), jnp.float32, -s(64), s(64)), 'W3': jax.random.uniform(ks[5], (4, 4), jnp.float32, -s(4), s(4)), 'b3': jax.random.uniform(ks[6], (4,), jnp.float32, -s(4), s(4)), 'We': jax.random.uniform(ks[7], (OUT, C), jnp.float32, -s(C), s(C)), 'be': jax.random.uniform(ks[8], (OUT,), jnp.float32, -s(C), s(C))}
    _L1_conv_all = _L1_conv_setup()
    _L1_conv_in = {k: v for k, v in _L1_conv_all.items() if k in ('ln_w', 'ln_b', 'W1', 'b1', 'W2', 'b2', 'W3', 'b3', 'We', 'be', )}
    del _L1_conv_all

    def _L1_ffn_setup():
        import jax, jax.numpy as jnp
        import numpy as np
        B, N, D, C, E, K = (8, 8192, 128, 128, 8, 2)
        key = jax.random.key(seed)
        k0, k1, k2 = jax.random.split(key, 3)
        x = jax.random.normal(k0, (B, N, D), dtype=jnp.float32)
        router_w = jax.random.normal(k1, (D, E), dtype=jnp.float32) * 0.05
        router_b = jnp.zeros((E,), dtype=jnp.float32)
        expert_w = jax.random.normal(k2, (E, D, C), dtype=jnp.float32) * (1.0 / np.sqrt(D))
        expert_b = jnp.zeros((E, C), dtype=jnp.float32)
        return {'x': x, 'router_w': router_w, 'router_b': router_b, 'expert_w': expert_w, 'expert_b': expert_b}
    _L1_ffn_all = _L1_ffn_setup()
    _L1_ffn_in = {k: v for k, v in _L1_ffn_all.items() if k in ('router_w', 'router_b', 'expert_w', 'expert_b', )}
    del _L1_ffn_all

    return {
        "x": x,
        "L0_conv_ln_scale": _L0_conv_in["ln_scale"],
        "L0_conv_ln_bias": _L0_conv_in["ln_bias"],
        "L0_conv_Wq": _L0_conv_in["Wq"],
        "L0_conv_Wk": _L0_conv_in["Wk"],
        "L0_conv_Wv": _L0_conv_in["Wv"],
        "L0_conv_Wb": _L0_conv_in["Wb"],
        "L0_conv_Wg": _L0_conv_in["Wg"],
        "L0_conv_Wo": _L0_conv_in["Wo"],
        "L0_ffn_W": _L0_ffn_in["W"],
        "L0_ffn_V": _L0_ffn_in["V"],
        "L0_ffn_gamma": _L0_ffn_in["gamma"],
        "L0_ffn_beta": _L0_ffn_in["beta"],
        "L1_conv_ln_w": _L1_conv_in["ln_w"],
        "L1_conv_ln_b": _L1_conv_in["ln_b"],
        "L1_conv_W1": _L1_conv_in["W1"],
        "L1_conv_b1": _L1_conv_in["b1"],
        "L1_conv_W2": _L1_conv_in["W2"],
        "L1_conv_b2": _L1_conv_in["b2"],
        "L1_conv_W3": _L1_conv_in["W3"],
        "L1_conv_b3": _L1_conv_in["b3"],
        "L1_conv_We": _L1_conv_in["We"],
        "L1_conv_be": _L1_conv_in["be"],
        "L1_ffn_router_w": _L1_ffn_in["router_w"],
        "L1_ffn_router_b": _L1_ffn_in["router_b"],
        "L1_ffn_expert_w": _L1_ffn_in["expert_w"],
        "L1_ffn_expert_b": _L1_ffn_in["expert_b"],
    }

def reference(x, L0_conv_ln_scale, L0_conv_ln_bias, L0_conv_Wq, L0_conv_Wk, L0_conv_Wv, L0_conv_Wb, L0_conv_Wg, L0_conv_Wo, L0_ffn_W, L0_ffn_V, L0_ffn_gamma, L0_ffn_beta, L1_conv_ln_w, L1_conv_ln_b, L1_conv_W1, L1_conv_b1, L1_conv_W2, L1_conv_b2, L1_conv_W3, L1_conv_b3, L1_conv_We, L1_conv_be, L1_ffn_router_w, L1_ffn_router_b, L1_ffn_expert_w, L1_ffn_expert_b):
    import jax
    import jax.numpy as jnp
    def _L0_conv_ref(z, ln_scale, ln_bias, Wq, Wk, Wv, Wb, Wg, Wo):
        import jax, jax.numpy as jnp
        import numpy as np
        H = 4
        C = 32
        CZ = 128
        N = 256
        B = 1
        EPS = 1e-05
        b, n = (z.shape[0], z.shape[1])
        mu = jnp.mean(z, axis=-1, keepdims=True)
        var = jnp.mean(jnp.square(z - mu), axis=-1, keepdims=True)
        zn = (z - mu) * jax.lax.rsqrt(var + EPS) * ln_scale + ln_bias
        q = (zn @ Wq).reshape(b, n, n, H, C)
        k = (zn @ Wk).reshape(b, n, n, H, C)
        v = (zn @ Wv).reshape(b, n, n, H, C)
        bias = zn @ Wb
        g = jax.nn.sigmoid(zn @ Wg).reshape(b, n, n, H, C)
        scores = jnp.einsum('bijhd,bikhd->bijkh', q, k) * (1.0 / C ** 0.5)
        scores = scores + bias[:, None, :, :, :]
        a = jax.nn.softmax(scores, axis=-2)
        o = jnp.einsum('bijkh,bikhd->bijhd', a, v)
        o = (g * o).reshape(b, n, n, H * C)
        return o @ Wo

    def _L0_ffn_ref(x, W, V, gamma, beta):
        import jax, jax.numpy as jnp
        import numpy as np
        BN_EPS = 1e-05
        B, T, H = (x.shape[0], x.shape[1], W.shape[0])
        Wx = jnp.einsum('bti,hi->bth', x, W)
        flat = Wx.reshape(B * T, H)
        mean = jnp.mean(flat, axis=0)
        var = jnp.var(flat, axis=0)
        Wx = ((flat - mean) * jax.lax.rsqrt(var + BN_EPS) * gamma + beta).reshape(B, T, H)
        Vt = V.T

        def step(yt, wx_t):
            yt = jax.nn.sigmoid(wx_t + yt @ Vt)
            return (yt, yt)
        y0 = jnp.zeros((B, H), dtype=Wx.dtype)
        _, ys = jax.lax.scan(step, y0, jnp.swapaxes(Wx, 0, 1))
        return jnp.swapaxes(ys, 0, 1)

    def _L1_conv_ref(x, ln_w, ln_b, W1, b1, W2, b2, W3, b3, We, be):
        import jax, jax.numpy as jnp
        import numpy as np
        N, H, W, C = (16, 128, 128, 128)
        OUT = 128
        EPS = 1e-05

        def _grid_mlp(x, gh, gw, Wg, bg):
            n, h, w, c = x.shape
            fh, fw = (h // gh, w // gw)
            u = x.reshape(n, gh, fh, gw, fw, c).transpose(0, 1, 3, 2, 4, 5).reshape(n, gh * gw, fh * fw, c)
            u = jnp.einsum('ngpc,kg->nkpc', u, Wg) + bg[:, None, None]
            u = u.reshape(n, gh, gw, fh, fw, c).transpose(0, 1, 3, 2, 4, 5).reshape(n, h, w, c)
            return u
        mu = jnp.mean(x, axis=-1, keepdims=True)
        var = jnp.mean(jnp.square(x - mu), axis=-1, keepdims=True)
        xn = (x - mu) * jax.lax.rsqrt(var + EPS) * ln_w + ln_b
        u = jax.nn.gelu(xn, approximate=False)
        u = _grid_mlp(u, 16, 16, W1, b1)
        u = _grid_mlp(u, 8, 8, W2, b2)
        u = _grid_mlp(u, 2, 2, W3, b3)
        return jnp.einsum('nhwc,oc->nhwo', u, We) + be

    def _L1_ffn_ref(x, router_w, router_b, expert_w, expert_b):
        import jax, jax.numpy as jnp
        import numpy as np
        B, N, D, C, E, K = (8, 8192, 128, 128, 8, 2)
        router_probs = jax.nn.softmax(x @ router_w + router_b, axis=-1)
        top_p, top_i = jax.lax.top_k(router_probs, K)
        top_p = top_p / jnp.sum(top_p, axis=-1, keepdims=True)
        expert_out = jnp.einsum('bnd,edc->bnec', x, expert_w) + expert_b
        gathered = jnp.take_along_axis(expert_out, top_i[..., None], axis=2)
        return jnp.einsum('bnk,bnkc->bnc', top_p, gathered)

    def _gn(v, G=32, eps=1e-5):
        B_, H_, W_, C_ = v.shape
        g = v.reshape(B_, H_, W_, G, C_ // G)
        m = jnp.mean(g, axis=(1, 2, 4), keepdims=True)
        s = jnp.var(g, axis=(1, 2, 4), keepdims=True)
        return ((g - m) / jnp.sqrt(s + eps)).reshape(v.shape)

    def _ln_c(v, eps=1e-6):
        m = jnp.mean(v, axis=-1, keepdims=True)
        s = jnp.var(v, axis=-1, keepdims=True)
        return (v - m) / jnp.sqrt(s + eps)

    def _ln_t(v, eps=1e-5):
        m = jnp.mean(v, axis=-1, keepdims=True)
        s = jnp.var(v, axis=-1, keepdims=True)
        return (v - m) / jnp.sqrt(s + eps)

    def _to_tokens(v):
        B_, H_, W_, C_ = v.shape
        return v.reshape(B_, H_ * W_, C_)
    def _from_tokens(t, like):
        return t.reshape(like.shape)

    x = x + _L0_conv_ref(_ln_c(x), L0_conv_ln_scale, L0_conv_ln_bias, L0_conv_Wq, L0_conv_Wk, L0_conv_Wv, L0_conv_Wb, L0_conv_Wg, L0_conv_Wo)
    t = _to_tokens(x)
    t = t + _L0_ffn_ref(_ln_t(t), L0_ffn_W, L0_ffn_V, L0_ffn_gamma, L0_ffn_beta)
    x = _from_tokens(t, x)
    x = x + _L1_conv_ref(_ln_c(x), L1_conv_ln_w, L1_conv_ln_b, L1_conv_W1, L1_conv_b1, L1_conv_W2, L1_conv_b2, L1_conv_W3, L1_conv_b3, L1_conv_We, L1_conv_be)
    t = _to_tokens(x)
    t = t + _L1_ffn_ref(_ln_t(t), L1_ffn_router_w, L1_ffn_router_b, L1_ffn_expert_w, L1_ffn_expert_b)
    x = _from_tokens(t, x)
    return x


_drawn_inputs = setup_inputs


def setup_inputs(seed=0):
    import zlib

    import numpy as np

    out = dict(_drawn_inputs(seed))
    spreads = {'L0_conv_ln_scale': (1.0, 0.6),
     'L0_conv_ln_bias': (0.0, 0.279),
     'L0_ffn_gamma': (1.0, 0.2),
     'L0_ffn_beta': (0.0, 0.1),
     'L1_conv_ln_w': (1.0, 0.2),
     'L1_conv_ln_b': (0.0, 0.1),
     'L1_ffn_router_b': (0.0, 0.1),
     'L1_ffn_expert_b': (0.0, 0.1)}
    factors = {'L0_conv_Wq': 8.0, 'L0_conv_Wk': 8.0, 'L0_conv_Wb': 7.677, 'L0_conv_Wg': 8.0}
    for name, (base, spread) in spreads.items():
        noise = np.random.default_rng([zlib.crc32(name.encode()), seed]).standard_normal(out[name].shape)
        drawn = base * np.exp(spread * noise) if base else spread * noise
        out[name] = jnp.asarray(drawn.astype(out[name].dtype))
    for name, factor in factors.items():
        out[name] = (out[name] * factor).astype(out[name].dtype)
    return out
```

```python
from contextlib import ExitStack

import numpy as np

import concourse.bass as bass
from concourse import mybir

F32 = mybir.dt.float32
I32 = mybir.dt.int32
ACT = mybir.ActivationFunctionType
ALU = mybir.AluOpType
AX = mybir.AxisListType

P = 128
ROWS = 256
COLS = 256
TOK = ROWS * COLS
NT = COLS // P
HEADS, DH = 4, 32
EXPERTS = 8
EPS_LN, EPS_LNC, EPS_BN = 1e-5, 1e-6, 1e-5
TWICE_MUL, TWICE_ADD = 1.0 + EPS_LN, EPS_LN * EPS_LNC


SEG = 64
WARM = 16
LANES = TOK // SEG
G = 2
BATCH = G * P
NB = LANES // BATCH
STEPS = WARM + SEG
BLK = 16
NBLK = SEG // BLK
TOL = 2.0 ** -20


def need(engine, sem, rows, per=1):
    if isinstance(rows, int):
        if rows > 0:
            engine.wait_ge(sem, min(rows, ROWS) * per)
    else:
        engine.wait_ge(sem, rows * per if per > 1 else rows)


def settle(engine, passed):
    engine.sem_inc(passed, 1)


def inside(row, count=ROWS):
    return not isinstance(row, int) or 0 <= row < count


def pipeline(engine, body, first, last, loop_from, loop_to, unroll):
    for k in range(first, loop_from):
        body(k, k % unroll)
    with engine.Fori(0, (loop_to - loop_from) // unroll) as turn:
        for u in range(unroll):
            body(turn * unroll + (loop_from + u), (loop_from + u) % unroll)
    for k in range(loop_to, last):
        body(k, k % unroll)


QR = 4
QT = QR * NT


def norm_pass(nc, io, zt_d, bias_d):
    ctx = ExitStack()
    with ctx:
        def sb(name, shape, dt=F32):
            return ctx.enter_context(nc.sbuf_tensor(name, shape, dt))

        def sem(name):
            return ctx.enter_context(nc.semaphore(name))

        ident = sb("ident0", [P, P])
        wb = sb("wb", [P, DH])
        ln_cols = sb("ln_cols", [P, 2])
        mhalf = sb("mhalf0", [P, QT])
        x_t = [sb(f"x0_{u}", [P, QT, P]) for u in range(4)]
        stat = sb("stat0", [P, QT, 6])
        mv = [sb(f"mv0_{u}", [P, QT, 2]) for u in range(2)]
        v = sb("v0", [P, QT])
        rs = [sb(f"rs0_{u}", [P, QT]) for u in range(2)]
        xh = [sb(f"xh0_{u}", [P, QT, P]) for u in range(2)]
        zt = [sb(f"zt0_{u}", [P, QR * COLS]) for u in range(2)]
        bias = [sb(f"bias0_{u}", [P, COLS]) for u in range(2)]
        psT = [ctx.enter_context(nc.psum_tensor(f"psT0_{i}", [P, 2, 512], F32)) for i in range(2)]
        psB = [ctx.enter_context(nc.psum_tensor(f"psB0_{i}", [P, 512], F32)) for i in range(2)]

        w_in, setup, passed_pool, passed_dve = sem("w_in0"), sem("setup0"), sem("passed_pool0"), sem("passed_dve0")
        x_in = [sem(f"x_in0_{u}") for u in range(4)]
        stat_s, mv_s, v_s, rs_s, xh_s, tr_mm, zt_s, b_mm, b_s = (
            sem(n + "0") for n in ("stat_s", "mv_s", "v_s", "rs_s", "xh_s", "tr_mm", "zt_s", "b_mm", "b_s"))
        zt_out = [sem(f"zt_out0_{u}") for u in range(2)]
        b_out = [sem(f"b_out0_{u}") for u in range(2)]
        x_v = io["x"].rearrange("(m j p) c -> m p j c", j=QT, p=P)
        zt_v = zt_d.rearrange("p (m t) -> m p t", t=QR * COLS)
        b_v = bias_d.rearrange("(m r) h k -> m r h k", r=QR)
        N0 = ROWS // QR
        FIRST, LAST, LOOP0, LOOP1, U = -2, N0, 4, 60, 4

        def upto(engine, s, n, per=1):
            need(engine, s, min(n, N0) if isinstance(n, int) else n, per)

        block = ctx.enter_context(nc.Block())

        @block.sync
        def _(sp):
            for dst, src in ((ident[:], io["ident"]), (wb[:], io["WbPad"]), (ln_cols[:], io["ln_cols"])):
                sp.dma_start(dst, src).then_inc(w_in, 16)

            def body(m, u):
                if inside(m + 3, N0):
                    upto(sp, xh_s, m)
                    sp.dma_start(x_t[(u + 3) % 4][:], x_v[m + 3]).then_inc(x_in[(u + 3) % 4], 16)
                if inside(m, N0):
                    upto(sp, zt_s, m + 1)
                    sp.dma_start(zt_v[m], zt[u % 2][:]).then_inc(zt_out[u % 2], 16)
                    upto(sp, b_s, m + 1)
                    for r in range(QR):
                        sp.dma_start(b_v[m, r], bias[u % 2][DH * r:DH * r + HEADS, :]).then_inc(b_out[u % 2], 16)

            pipeline(sp, body, FIRST - 1, LAST, LOOP0, LOOP1, U)
            for u in range(2):
                sp.wait_ge(zt_out[u], 16 * N0 // 2)
                sp.wait_ge(b_out[u], 16 * QR * N0 // 2)

        @block.gpsimd
        def _(pool):
            pool.memset(mhalf[:], -0.5).then_inc(setup, 1)
            pool.wait_ge(setup, 1)

            def body(m, u):
                b = u % 2
                if inside(m + 2, N0):
                    upto(pool, mv_s, m + 3)
                    upto(pool, rs_s, m + 2)
                    settle(pool, passed_pool)
                    pool.tensor_scalar(v[:], mv[b][:, :, 1], TWICE_MUL, TWICE_ADD, ALU.mult, ALU.add).then_inc(v_s, 1)
                    upto(pool, v_s, m + 3)
                    upto(pool, xh_s, m + 1)
                    pool.tensor_tensor(rs[b][:], v[:], mhalf[:], ALU.pow).then_inc(rs_s, 1)

            pipeline(pool, body, FIRST, LAST, LOOP0, LOOP1, U)

        @block.vector
        def _(dve):
            def body(m, u):
                b, q = u % 2, (u + 2) % 4
                if inside(m + 2, N0):
                    dve.wait_ge(x_in[q], (m + 2 - q) * 4 + 16)
                    upto(dve, mv_s, m + 2)
                    for t in range(QT):
                        last = dve.bn_stats(stat[:, t, :], x_t[q][:, t, :])
                    last.then_inc(stat_s, 1)
                if inside(m, N0):
                    upto(dve, b_mm, m + 1)
                    upto(dve, b_out[b], m - b, 16 * QR // 2)
                    dve.tensor_scalar(bias[b][:], psB[b][:, 0:COLS], -1.0, None, ALU.mult).then_inc(b_s, 1)
                if inside(m + 2, N0):
                    upto(dve, stat_s, m + 3)
                    upto(dve, v_s, m + 1)
                    upto(dve, xh_s, m + 1)
                    settle(dve, passed_dve)
                    for t in range(QT):
                        last = dve.bn_aggr(mv[b][:, t, :], stat[:, t, :])
                    last.then_inc(mv_s, 1)
                    upto(dve, rs_s, m + 3)
                    upto(dve, mv_s, m + 3)
                    upto(dve, tr_mm, m + 1)
                    for t in range(QT):
                        last = dve.tensor_scalar(xh[b][:, t, :], x_t[q][:, t, :], mv[b][:, t, 0:1], rs[b][:, t:t + 1],
                                                 ALU.subtract, ALU.mult)
                    last.then_inc(xh_s, 1)

            pipeline(dve, body, FIRST, LAST, LOOP0, LOOP1, U)

        @block.scalar
        def _(act):
            act.wait_ge(w_in, 48)

            def body(m, u):
                a = (u + 1) % 2
                if inside(m + 1, N0):
                    upto(act, tr_mm, m + 2)
                    upto(act, zt_out[a], m + 1 - a, 8)
                    upto(act, b_mm, m)
                    for i in range(2):
                        last = act.activation(zt[a][:, i * 512:(i + 1) * 512], psT[a][:, i, :], ACT.Identity,
                                              bias=ln_cols[:, 1:2], scale=ln_cols[:, 0:1])
                    last.then_inc(zt_s, 1)

            pipeline(act, body, FIRST, LAST, LOOP0, LOOP1, U)

        @block.tensor
        def _(pe):
            pe.wait_ge(w_in, 48)

            def body(m, u):
                a = (u + 1) % 2
                if inside(m + 1, N0):
                    upto(pe, xh_s, m + 2)
                    upto(pe, zt_s, m)
                    for t in range(QT):
                        last = pe.transpose(psT[a][:, t // 4, (t % 4) * P:(t % 4 + 1) * P], xh[a][:, t, :], ident[:])
                    last.then_inc(tr_mm, 1)
                if inside(m, N0):
                    upto(pe, zt_s, m + 1)
                    upto(pe, b_s, m - 1)
                    for r in range(QR):
                        last = pe.matmul(psB[u % 2][DH * r:DH * (r + 1), 0:COLS], wb[:],
                                         zt[u % 2][:, r * COLS:(r + 1) * COLS], start=True, stop=True)
                    last.then_inc(b_mm, 1)

            pipeline(pe, body, FIRST, LAST, LOOP0, LOOP1, U)


def attention_pass(nc, io, zt_d, bias_d, t1_d, wx_d, bn_sb):
    ctx = ExitStack()
    with ctx:
        def sb(name, shape, dt=F32):
            return ctx.enter_context(nc.sbuf_tensor(name, shape, dt))

        def ps(name, shape):
            return ctx.enter_context(nc.psum_tensor(name, shape, F32))

        def sem(name):
            return ctx.enter_context(nc.semaphore(name))

        w_s = sb("w_s", [P, 4, P])
        wo_s = sb("wo_s", [P, P])
        wt_s = sb("wt_s", [P, P])
        ident = sb("ident", [P, P])
        half = sb("half", [P, DH])
        mhalf = sb("mhalf", [P, NT])
        bias = sb("bias", [P, NT, HEADS, COLS])
        pad = sb("pad", [P, WARM])

        x_t = [sb(f"x_t{u}", [P, NT, P]) for u in range(4)]
        zT = [sb(f"zT{u}", [P, COLS]) for u in range(4)]
        qT = [sb(f"qT{u}", [P, COLS]) for u in range(2)]
        kT = [sb(f"kT{u}", [P, COLS]) for u in range(2)]
        vv = [sb(f"vv{u}", [P, NT, P]) for u in range(2)]
        th = [sb(f"th{u}", [P, COLS]) for u in range(2)]
        score = [sb(f"score{u}", [P, NT, HEADS, COLS]) for u in range(2)]
        least = [sb(f"least{u}", [P, NT, HEADS]) for u in range(2)]
        prob = [sb(f"prob{u}", [P, NT, HEADS, COLS]) for u in range(2)]
        total = [sb(f"total{u}", [P, NT * HEADS]) for u in range(2)]
        rtotal = [sb(f"rtotal{u}", [P, NT * HEADS]) for u in range(2)]
        spread = [sb(f"spread{u}", [P, NT, P]) for u in range(2)]
        probT = [sb(f"probT{u}", [P, HEADS, NT, COLS]) for u in range(2)]
        gated = [sb(f"gated{u}", [P, COLS]) for u in range(2)]
        og = [sb(f"og{u}", [P, COLS]) for u in range(2)]
        t1 = [sb(f"t1_{u}", [P, NT, P]) for u in range(2)]
        stat2 = [sb(f"stat2_{u}", [P, NT, 6]) for u in range(2)]
        mv2 = [sb(f"mv2_{u}", [P, NT, 2]) for u in range(2)]
        v2 = [sb(f"v2_{u}", [P, NT]) for u in range(2)]
        rs2 = [sb(f"rs2_{u}", [P, NT]) for u in range(2)]
        yh = [sb(f"yh{u}", [P, NT, P]) for u in range(2)]
        yT = [sb(f"yT{u}", [P, COLS]) for u in range(2)]
        wx = [sb(f"wx{u}", [P, COLS]) for u in range(2)]
        wx_stat = sb("wx_stat", [P, ROWS, 6])

        psS = [ps(f"psS{i}", [P, 512]) for i in range(2)]
        psT = [ps(f"psT{i}", [P, 512]) for i in range(2)]
        psQK, psVG = ps("psQK", [P, 512]), ps("psVG", [P, 512])
        psO = ps("psO", [P, 512])
        psM = ps("psM", [P, 512])

        w_in, setup_d, pad_out, passed_pool, passed_dve = (
            sem(n) for n in ("w_in", "setup_d", "pad_out", "passed_pool", "passed_dve"))
        x_in = [sem(f"x_in{u}") for u in range(4)]
        z_in = [sem(f"z_in{u}") for u in range(4)]
        qk_mm, qk_s, vg_mm, vg_s, s_mm, score_s, prob_s, tr_mm, probT_s = (
            sem(n) for n in ("qk_mm", "qk_s", "vg_mm", "vg_s", "s_mm", "score_s", "prob_s", "tr_mm", "probT_s"))
        rtotal_s, spread_s, pv_mm, rt_mm, gated_s, og_s, out_mm = (
            sem(n) for n in ("rtotal_s", "spread_s", "pv_mm", "rt_mm", "gated_s", "og_s", "out_mm"))
        t1_s, stat2_s, mv2_s, v2_s, rs2_s, yh_s, yT_mm, yT_s, wx_mm, wx_s, wstat_s = (
            sem(n) for n in ("t1_s", "stat2_s", "mv2_s", "v2_s", "rs2_s", "yh_s", "yT_mm", "yT_s",
                             "wx_mm", "wx_s", "wstat_s"))
        t1_out = [sem(f"t1_out{u}") for u in range(2)]
        wx_out = [sem(f"wx_out{u}") for u in range(2)]

        x_v = io["x"].rearrange("(r j p) c -> r p j c", j=NT, p=P)
        z_v = zt_d.rearrange("p (r t) -> r p t", t=COLS)
        t1_v = t1_d.rearrange("(r j p) c -> r p j c", j=NT, p=P)
        wx_v = wx_d[:, WARM:WARM + TOK].rearrange("p (r t) -> r p t", t=COLS)

        FIRST, LAST, LOOP0, LOOP1, U = -1, ROWS + 3, 4, 248, 4
        UNITS = 4
        block = ctx.enter_context(nc.Block())

        @block.sync
        def _(sp):
            loads = [(w_s[:, i, :], io[n]) for i, n in enumerate(("Wq", "Wk", "Wv", "Wg"))]
            loads += [(wo_s[:], io["Wo"]), (wt_s[:], io["WT"]), (ident[:], io["ident"])]
            loads += [(bias[:, t], bias_d[t * P:(t + 1) * P]) for t in range(NT)]
            for dst, src in loads:
                sp.dma_start(dst, src).then_inc(w_in, 16)
            sp.wait_ge(setup_d, 3)
            sp.dma_start(wx_d[:, 0:WARM], pad[:]).then_inc(pad_out, 16)

            def body(k, u):
                if inside(k + 3):
                    need(sp, vg_mm, k)
                    sp.dma_start(zT[(u + 3) % 4][:], z_v[k + 3]).then_inc(z_in[(u + 3) % 4], 16)
                if inside(k + 1):
                    need(sp, t1_s, k - 2)
                    sp.dma_start(x_t[(u + 1) % 4][:], x_v[k + 1]).then_inc(x_in[(u + 1) % 4], 16)
                if inside(k - 3):
                    need(sp, wx_s, k - 2)
                    sp.dma_start(wx_v[k - 3], wx[(u - 3) % 2][:]).then_inc(wx_out[(u - 3) % 2], 16)
                if inside(k - 2):
                    need(sp, t1_s, k - 1)
                    sp.dma_start(t1_v[k - 2], t1[u % 2][:]).then_inc(t1_out[u % 2], 16)

            pipeline(sp, body, FIRST - 2, LAST, LOOP0, LOOP1, U)
            sp.wait_ge(pad_out, 16)
            for u in range(2):
                sp.wait_ge(t1_out[u], 16 * ROWS // 2)
                sp.wait_ge(wx_out[u], 16 * ROWS // 2)

        @block.gpsimd
        def _(pool):
            pool.memset(mhalf[:], -0.5).then_inc(setup_d, 1)
            pool.memset(half[:], 0.5).then_inc(setup_d, 1)
            pool.memset(pad[:], 0.0).then_inc(setup_d, 1)
            pool.wait_ge(setup_d, 3)

            def body(k, u):
                a, b = (u + 1) % 2, u % 2
                if inside(k - 1):
                    need(pool, rtotal_s, k)
                    need(pool, rt_mm, k - 2)
                    pool.tensor_tensor(
                        spread[a][:].rearrange("p t (h d) -> p (t h) d", h=HEADS),
                        rtotal[a][:].unsqueeze(2).to_broadcast([P, NT * HEADS, DH]),
                        half[:].unsqueeze(1).to_broadcast([P, NT * HEADS, DH]), ALU.mult).then_inc(spread_s, 1)
                if inside(k - 2):
                    need(pool, mv2_s, k - 1)
                    need(pool, rs2_s, k - 3)
                    settle(pool, passed_pool)
                    pool.tensor_scalar(v2[b][:], mv2[b][:, :, 1], 1.0, EPS_LN, ALU.mult, ALU.add).then_inc(v2_s, 1)
                    need(pool, v2_s, k - 1)
                    need(pool, yh_s, k - 3)
                    pool.tensor_tensor(rs2[b][:], v2[b][:], mhalf[:], ALU.pow).then_inc(rs2_s, 1)

            pipeline(pool, body, FIRST, LAST, LOOP0, LOOP1, U)

        @block.vector
        def _(dve):
            dve.wait_ge(w_in, 9 * 16)

            def body(k, u):
                a, b = (u + 1) % 2, u % 2
                if inside(k - 1):
                    need(dve, prob_s, k, UNITS)
                    need(dve, spread_s, k - 2)
                    dve.reciprocal(rtotal[a][:], total[a][:]).then_inc(rtotal_s, 1)
                for n in range(UNITS):
                    if inside(k):
                        dve.wait_ge(s_mm, k * UNITS + n + 1)
                        need(dve, prob_s, k - 1, UNITS)
                        settle(dve, passed_dve)
                        for t in range(NT):
                            last = dve.tensor_tensor_reduce(
                                out=score[b][:, t, n, :], in0=psS[n % 2][:, t * COLS:(t + 1) * COLS],
                                in1=bias[:, t, n, :], scale=1.0, scalar=3e38, op0=ALU.add, op1=ALU.min,
                                accum_out=least[b][:, t, n:n + 1])
                        last.then_inc(score_s, 1)
                    if inside(k - 1):
                        dve.wait_ge(tr_mm, (k - 1) * UNITS + n + 1)
                        need(dve, pv_mm, k - 2)
                        dve.tensor_copy(probT[a][:, n].rearrange("p t q -> p (t q)"), psT[n % 2][:]).then_inc(probT_s, 1)
                    if inside(k - 2):
                        if n == 1:
                            need(dve, out_mm, k - 1)
                            dve.wait_ge(x_in[(u - 2) % 4], (k - 2 - (u - 2) % 4) * 4 + 16)
                            need(dve, yh_s, k - 3)
                            need(dve, t1_out[b], k - 2 - b, 8)
                            dve.tensor_tensor(t1[b][:], psM[:, 0:COLS].rearrange("p (j c) -> p j c", j=NT),
                                              x_t[(u - 2) % 4][:], ALU.add).then_inc(t1_s, 1)
                        if n == 2:
                            need(dve, t1_s, k - 1)
                            need(dve, mv2_s, k - 3)
                            for j in range(NT):
                                last = dve.bn_stats(stat2[b][:, j, :], t1[b][:, j, :])
                            last.then_inc(stat2_s, 1)
                        if n == 3:
                            need(dve, stat2_s, k - 1)
                            need(dve, v2_s, k - 3)
                            need(dve, yh_s, k - 3)
                            settle(dve, passed_dve)
                            for j in range(NT):
                                last = dve.bn_aggr(mv2[b][:, j, :], stat2[b][:, j, :])
                            last.then_inc(mv2_s, 1)
                if inside(k - 3):
                    need(dve, wx_s, k - 2)
                    dve.bn_stats(wx_stat[:, bass.ds(k - 3, 1), :], wx[a][:]).then_inc(wstat_s, 1)
                if inside(k - 2):
                    need(dve, rs2_s, k - 1)
                    need(dve, mv2_s, k - 1)
                    need(dve, yT_mm, k - 3)
                    for j in range(NT):
                        last = dve.tensor_scalar(yh[b][:, j, :], t1[b][:, j, :], mv2[b][:, j, 0:1],
                                                 rs2[b][:, j:j + 1], ALU.subtract, ALU.mult)
                    last.then_inc(yh_s, 1)
                if inside(k - 1):
                    need(dve, rt_mm, k)
                    need(dve, vg_s, k)
                    need(dve, og_s, k - 2)
                    dve.scalar_tensor_tensor(gated[a][:], th[a][:], 1.0, psO[:, 0:COLS], ALU.add,
                                             ALU.mult).then_inc(gated_s, 1)
                    need(dve, gated_s, k)
                    need(dve, out_mm, k - 2)
                    dve.tensor_tensor(og[a][:], gated[a][:], psO[:, COLS:2 * COLS], ALU.mult).then_inc(og_s, 1)

            pipeline(dve, body, FIRST, LAST, LOOP0, LOOP1, U)
            dve.wait_ge(wstat_s, ROWS)
            dve.bn_aggr(bn_sb[:, 0:2], wx_stat[:].rearrange("p r s -> p (r s)")).then_inc(wstat_s, 1)

        @block.scalar
        def _(act):
            def body(k, u):
                a, b = (u + 1) % 2, u % 2
                if inside(k):
                    for n in range(UNITS):
                        act.wait_ge(score_s, k * UNITS + n + 1)
                        need(act, tr_mm, k - 1, UNITS)
                        need(act, rtotal_s, k - 1)
                        for t in range(NT):
                            last = act.activation(prob[b][:, t, n, :], score[b][:, t, n, :], ACT.Exp,
                                                  bias=least[b][:, t, n:n + 1], scale=-1.0,
                                                  accum_out=total[b][:, t * HEADS + n:t * HEADS + n + 1])
                        last.then_inc(prob_s, 1)
                if inside(k + 1):
                    need(act, qk_mm, k + 2)
                    need(act, s_mm, k, UNITS)
                    act.activation(qT[a][:], psQK[:, 0:COLS], ACT.Identity, scale=-(DH ** -0.5))
                    act.activation(kT[a][:], psQK[:, COLS:2 * COLS], ACT.Identity).then_inc(qk_s, 1)
                if inside(k):
                    need(act, vg_mm, k + 1)
                    need(act, pv_mm, k - 1)
                    need(act, gated_s, k - 1)
                    act.activation(vv[b][:].rearrange("p t c -> p (t c)"), psVG[:, 0:COLS], ACT.Identity)
                    act.activation(th[b][:], psVG[:, COLS:2 * COLS], ACT.Tanh, scale=0.5).then_inc(vg_s, 1)
                if inside(k - 2):
                    need(act, yT_mm, k - 1)
                    need(act, wx_mm, k - 3)
                    act.activation(yT[b][:], psM[:, 0:COLS], ACT.Identity).then_inc(yT_s, 1)
                    need(act, wx_mm, k - 1)
                    need(act, wstat_s, k - 3)
                    need(act, wx_out[b], k - 2 - b, 8)
                    act.activation(wx[b][:], psM[:, COLS:2 * COLS], ACT.Identity).then_inc(wx_s, 1)

            pipeline(act, body, FIRST, LAST, LOOP0, LOOP1, U)

        @block.tensor
        def _(pe):
            pe.wait_ge(w_in, 9 * 16)

            def body(k, u):
                a, b = (u + 1) % 2, u % 2
                if inside(k):
                    need(pe, qk_s, k + 1)
                for n in range(UNITS):
                    if inside(k):
                        if n >= 2 or not isinstance(k, int) or k > 0:
                            pe.wait_ge(score_s, k * UNITS + n - 1)
                        hs = slice(DH * n, DH * (n + 1))
                        for t in range(NT):
                            last = pe.matmul(psS[n % 2][:, t * COLS:(t + 1) * COLS], qT[b][hs, t * P:(t + 1) * P],
                                             kT[b][hs, :], start=True, stop=True)
                        last.then_inc(s_mm, 1)
                    if inside(k - 1):
                        if n == 0:
                            need(pe, prob_s, k, UNITS)
                        if n >= 2 or not isinstance(k, int) or k > 1:
                            pe.wait_ge(probT_s, (k - 1) * UNITS + n - 1)
                        for j in range(NT):
                            for t in range(NT):
                                last = pe.transpose(psT[n % 2][:, j * COLS + t * P:j * COLS + (t + 1) * P],
                                                    prob[a][:, t, n, j * P:(j + 1) * P], ident[:])
                        last.then_inc(tr_mm, 1)
                    if n == 1 and inside(k - 2):
                        need(pe, og_s, k - 1)
                        need(pe, wx_s, k - 2)
                        for j in range(NT):
                            last = pe.matmul(psM[:, j * P:(j + 1) * P], og[b][:, j * P:(j + 1) * P], wo_s[:],
                                             start=True, stop=True)
                        last.then_inc(out_mm, 1)
                if inside(k + 1):
                    q = (u + 1) % 4
                    pe.wait_ge(z_in[q], (k + 1 - q) * 4 + 16)
                    need(pe, qk_s, k + 1)
                    pe.matmul(psQK[:, 0:COLS], w_s[:, 0, :], zT[q][:], start=True, stop=True)
                    pe.matmul(psQK[:, COLS:2 * COLS], w_s[:, 1, :], zT[q][:], start=True, stop=True).then_inc(qk_mm, 1)
                if inside(k):
                    need(pe, vg_s, k)
                    for j in range(NT):
                        pe.matmul(psVG[:, j * P:(j + 1) * P], zT[u % 4][:, j * P:(j + 1) * P], w_s[:, 2, :],
                                  start=True, stop=True)
                    pe.matmul(psVG[:, COLS:2 * COLS], w_s[:, 3, :], zT[u % 4][:], start=True, stop=True).then_inc(vg_mm, 1)
                if inside(k - 1):
                    need(pe, probT_s, k, UNITS)
                    need(pe, og_s, k - 1)
                    for j in range(NT):
                        for h in range(HEADS):
                            hs = slice(DH * h, DH * (h + 1))
                            last = pe.matmul(psO[hs, 0:COLS], vv[a][:, j, hs], probT[a][:, h, j, :],
                                             start=j == 0, stop=j == NT - 1)
                    last.then_inc(pv_mm, 1)
                if inside(k - 2):
                    need(pe, yh_s, k - 1)
                    for j in range(NT):
                        last = pe.transpose(psM[:, j * P:(j + 1) * P], yh[b][:, j, :], ident[:])
                    last.then_inc(yT_mm, 1)
                if inside(k - 1):
                    need(pe, spread_s, k)
                    for t in range(NT):
                        last = pe.transpose(psO[:, COLS + t * P:COLS + (t + 1) * P], spread[a][:, t, :], ident[:])
                    last.then_inc(rt_mm, 1)
                if inside(k - 2):
                    need(pe, yT_s, k - 1)
                    pe.matmul(psM[:, COLS:2 * COLS], wt_s[:], yT[b][:], start=True, stop=True).then_inc(wx_mm, 1)

            pipeline(pe, body, FIRST, LAST, LOOP0, LOOP1, U)


def recurrence_pass(nc, io, t1_d, wx_d, t2_d, bn_sb):
    ctx = ExitStack()
    with ctx:
        def sb(name, shape, dt=F32):
            return ctx.enter_context(nc.sbuf_tensor(name, shape, dt))

        def ps(name, shape):
            return ctx.enter_context(nc.psum_tensor(name, shape, F32))

        def sem(name):
            return ctx.enter_context(nc.semaphore(name))

        vt_s = sb("vt_s", [P, P])
        ident = sb("ident_r", [P, P])
        gb = sb("gb", [P, 2])
        mhalf = sb("mhalf_r", [P, 1])
        var_e = sb("var_e", [P, 1])
        rstd = sb("rstd", [P, 1])
        am = sb("am", [P, 1])
        bn_a = sb("bn_a", [P, 1])
        bn_b = sb("bn_b", [P, 1])
        wxb = [sb(f"wxb{i}", [P, WARM + BATCH * SEG]) for i in range(2)]
        y = [sb(f"y{g}", [P, BLK, P]) for g in range(G)]
        pre = [sb(f"pre{g}", [P, 2, P]) for g in range(G)]
        t1b = [[sb(f"t1b{g}{i}", [P, BLK, P]) for i in range(2)] for g in range(G)]
        warm_mask = sb("warm_mask", [P, LANES])
        end_mask = sb("end_mask", [P, 1])
        starts = sb("starts", [P, LANES])
        ends = sb("ends", [P, 1 + LANES])
        guess = [sb(f"guess{g}", [P, P]) for g in range(G)]
        off = sb("off", [P, LANES])
        off2 = sb("off2", [P, LANES])
        off_max = sb("off_max", [P, 1])
        off_bad = sb("off_bad", [P, 1])
        ones = sb("ones_r", [P, 1])
        again = sb("again", [1, 1], I32)

        psY = [ps(f"psY{g}", [P, 512]) for g in range(G)]
        psT = [[ps(f"psT{g}{i}", [P, 4, P]) for i in range(2)] for g in range(G)]
        psF = ps("psF", [P, 512])

        c_in, c_ready, bn_c, bn_p = sem("c_in"), sem("c_ready"), sem("bn_c"), sem("bn_p")
        wx_in = [sem(f"wx_in{i}") for i in range(2)]
        wx_free = sem("wx_free")
        mm = [sem(f"mm{g}") for g in range(G)]
        pre_s = [sem(f"pre_s{g}") for g in range(G)]
        y_s = [sem(f"y_s{g}") for g in range(G)]
        guess_s = [sem(f"guess_s{g}") for g in range(G)]
        start_s = [sem(f"start_s{g}") for g in range(G)]
        begin_s = [sem(f"begin_s{g}") for g in range(G)]
        end_s = sem("end_s")
        tr = [sem(f"tr{g}") for g in range(G)]
        t2_s = [sem(f"t2_s{g}") for g in range(G)]
        t1_in = [[sem(f"t1_in{g}{i}") for i in range(2)] for g in range(G)]
        t2_out = [[sem(f"t2_out{g}{i}") for i in range(2)] for g in range(G)]
        off_s, bad_s, sum_mm, again_s, seen = sem("off_s"), sem("bad_s"), sem("sum_mm"), sem("again_s"), sem("seen")
        passed_r = {e: sem("passed_" + e + "2") for e in ("sp", "act", "pe", "dve")}
        CREDIT_OUT, CREDIT_T2 = 16, 2

        t1_v = t1_d.rearrange("(b g p k s) c -> b g k p s c", g=G, p=P, k=NBLK, s=BLK)
        t2_v = t2_d.rearrange("(b g p k s) c -> b g k p s c", g=G, p=P, k=NBLK, s=BLK)
        block = ctx.enter_context(nc.Block())

        def passes(engine, one_pass, passed):
            with engine.register("n_pass") as n_pass, engine.register("go_on") as go_on:
                engine.reg_mov(n_pass, 0)
                engine.reg_mov(go_on, 1)
                with engine.While(lambda: go_on):
                    n = engine.snap(n_pass)
                    one_pass(n)
                    engine.wait_ge(again_s, n + 1)
                    settle(engine, passed)
                    engine.reg_load(go_on, again[0:1, 0:1])
                    engine.drain().then_inc(seen, 1)
                    engine.reg_add(n_pass, n_pass, 1)

        @block.sync
        def _(sp):
            for dst, src in ((vt_s[:], io["VT"]), (ident[:], io["ident"]), (gb[:], io["bn_cols"])):
                sp.dma_start(dst, src).then_inc(c_in, 16)
            for g in range(G):
                for i in range(2):
                    sp.nop().then_inc(t2_out[g][i], CREDIT_OUT)

            def one_pass(n):
                def load_t1(b, k, g):
                    sp.wait_ge(t2_out[g][k % 2], (n * NB + b) * (8 * NBLK) + (k // 2) * 16 + CREDIT_OUT)
                    sp.dma_start(t1b[g][k % 2][:], t1_v[b, g, k]).then_inc(t1_in[g][k % 2], 16)

                with sp.Fori(0, NB // 2) as pair:
                    for i in range(2):
                        b = pair * 2 + i
                        sp.wait_ge(wx_free, n * NB + b + 1)
                        sp.dma_start(wxb[i][:], wx_d[:, bass.ds(b * (BATCH * SEG), WARM + BATCH * SEG)]
                                     ).then_inc(wx_in[i], 16)
                        for k in range(2):
                            for g in range(G):
                                load_t1(b, k, g)
                        for k in range(NBLK):
                            for g in range(G):
                                sp.wait_ge(t2_s[g], ((n * NB + b) * NBLK + (k + 1)) * 4 + CREDIT_T2)
                                sp.dma_start(t2_v[b, g, k], t1b[g][k % 2][:]).then_inc(t2_out[g][k % 2], 16)
                            if k + 2 < NBLK:
                                for g in range(G):
                                    load_t1(b, k + 2, g)
                for g in range(G):
                    for i in range(2):
                        sp.wait_ge(t2_out[g][i], (n + 1) * (NB * NBLK * 8) + CREDIT_OUT)

            passes(sp, one_pass, passed_r["sp"])

        @block.gpsimd
        def _(pool):
            pool.memset(mhalf[:], -0.5).then_inc(bn_p, 1)
            pool.tensor_scalar(var_e[:], bn_sb[:, 1:2], 1.0, EPS_BN, ALU.mult, ALU.add).then_inc(bn_p, 1)
            pool.wait_ge(bn_p, 2)
            pool.tensor_tensor(rstd[:], var_e[:], mhalf[:], ALU.pow).then_inc(bn_p, 1)

        @block.vector
        def _(dve):
            dve.nop().then_inc(wx_free, 2)
            for g in range(G):
                dve.nop().then_inc(t2_s[g], CREDIT_T2)
            dve.memset(ones[:], 1.0)
            dve.memset(warm_mask[:], 1.0).then_inc(bn_c, 1)
            dve.memset(end_mask[:], 0.0)
            dve.memset(ends[:], 0.0).then_inc(bn_c, 1)
            dve.wait_ge(bn_c, 1)
            dve.memset(warm_mask[:, 0:1], 0.0)
            for g in range(G):
                last = dve.memset(y[g][:, BLK - 1, :], 0.0)
            last.then_inc(bn_c, 1)
            dve.wait_ge(c_in, 48)
            dve.wait_ge(bn_p, 3)
            dve.tensor_tensor(bn_a[:], gb[:, 0:1], rstd[:], ALU.mult).then_inc(bn_c, 1)
            dve.wait_ge(bn_c, 4)
            dve.tensor_tensor(am[:], bn_a[:], bn_sb[:, 0:1], ALU.mult).then_inc(bn_c, 1)
            dve.wait_ge(bn_c, 5)
            dve.tensor_tensor(bn_b[:], gb[:, 1:2], am[:], ALU.subtract).then_inc(c_ready, 1)
            dve.wait_ge(c_ready, 1)

            def one_pass(n):
                with dve.Fori(0, NB // 2) as pair:
                    for i in range(2):
                        b = pair * 2 + i
                        nb = n * NB + b
                        base = nb * STEPS
                        wv = wxb[i][:]
                        dve.wait_ge(wx_in[i], n * (NB // 2 * 16) + pair * 16 + 16)

                        def step(s, j, g, now):
                            dve.wait_ge(mm[g], base + now + 1)
                            dve.scalar_tensor_tensor(
                                pre[g][:, j % 2, :],
                                wv[:, bass.ds(s + g * P * SEG, P, SEG)] if not isinstance(s, int)
                                else wv[:, s + g * P * SEG:s + g * P * SEG + (P - 1) * SEG + 1:SEG],
                                bn_a[:, 0:1], psY[g][:, 0:P], ALU.mult, ALU.add).then_inc(pre_s[g], 1)

                        for j in range(WARM):
                            for g in range(G):
                                step(j, j, g, j)
                        for g in range(G):
                            lanes = bass.ds(b * BATCH + g * P, P)
                            dve.wait_ge(y_s[g], base + WARM)
                            dve.tensor_tensor(guess[g][:], y[g][:, BLK - 1, :], warm_mask[:, lanes],
                                              ALU.mult).then_inc(guess_s[g], 1)
                        for g in range(G):
                            lanes = bass.ds(b * BATCH + g * P, P)
                            dve.wait_ge(guess_s[g], nb + 1)
                            dve.scalar_tensor_tensor(starts[:, lanes], ends[:, lanes], end_mask[:, 0:1], guess[g][:],
                                                     ALU.mult, ALU.add).then_inc(start_s[g], 1)
                        for g in range(G):
                            lanes = bass.ds(b * BATCH + g * P, P)
                            dve.wait_ge(start_s[g], nb + 1)
                            dve.tensor_scalar(y[g][:, BLK - 1, :], starts[:, lanes], 1.0, None,
                                              ALU.mult).then_inc(begin_s[g], 1)
                        with dve.Fori(0, NBLK // 2) as k2:
                            for ki in range(2):
                                k = k2 * 2 + ki
                                for g in range(G):
                                    dve.wait_ge(t1_in[g][ki], nb * (8 * NBLK) + k2 * 16 + 16)
                                for j in range(BLK):
                                    for g in range(G):
                                        step(k * BLK + (WARM + j), j, g, k * BLK + (WARM + j))
                                    if j % 4 == 1 and j > 4:
                                        add_states(nb, k, ki, (j - 5) // 4)
                                add_states(nb, k, ki, 3)
                        for g in range(G):
                            dve.wait_ge(y_s[g], base + STEPS)
                            last = dve.tensor_scalar(ends[:, bass.ds(b * BATCH + g * P + 1, P)], y[g][:, BLK - 1, :], 1.0,
                                                     None, ALU.mult)
                        last.then_inc(wx_free, 1)
                dve.wait_ge(wx_free, (n + 1) * NB + 2)
                dve.tensor_tensor(off[:], starts[:], ends[:, 0:LANES], ALU.subtract).then_inc(off_s, 1)
                dve.wait_ge(off_s, n * 3 + 1)
                dve.tensor_tensor(off2[:], off[:], off[:], ALU.mult).then_inc(off_s, 1)
                dve.wait_ge(off_s, n * 3 + 2)
                dve.tensor_reduce(off_max[:], off2[:], AX.X, ALU.max).then_inc(off_s, 1)
                dve.wait_ge(off_s, n * 3 + 3)
                dve.tensor_scalar(off_bad[:], off_max[:], TOL * TOL, None, ALU.is_gt).then_inc(bad_s, 1)
                dve.memset(warm_mask[:], 0.0)
                dve.memset(end_mask[:], 1.0)
                dve.wait_ge(sum_mm, n + 1)
                dve.tensor_copy(again[0:1, 0:1], psF[0:1, 0:1]).then_inc(again_s, 1)
                dve.wait_ge(seen, n * 4 + 3)

            def add_states(nb, k, ki, quad):
                for g in range(G):
                    dve.wait_ge(tr[g], (nb * NBLK + k) * 4 + quad + 1)
                    part = t1b[g][ki][:, 4 * quad:4 * quad + 4, :]
                    dve.tensor_tensor(part, psT[g][quad % 2][:], part, ALU.add).then_inc(t2_s[g], 1)

            passes(dve, one_pass, passed_r["dve"])

        @block.scalar
        def _(act):
            act.wait_ge(c_ready, 1)

            def one_pass(n):
                with act.Fori(0, NB) as b:
                    base = (n * NB + b) * STEPS
                    with act.Fori(0, STEPS, BLK) as s0:
                        for j in range(BLK):
                            for g in range(G):
                                act.wait_ge(pre_s[g], base + s0 + (j + 1))
                                act.activation(y[g][:, j, :], pre[g][:, j % 2, :], ACT.Sigmoid,
                                               bias=bn_b[:, 0:1]).then_inc(y_s[g], 1)

            passes(act, one_pass, passed_r["act"])

        @block.tensor
        def _(pe):
            pe.wait_ge(c_in, 48)
            pe.wait_ge(bn_c, 3)

            def one_pass(n):
                with pe.Fori(0, NB) as b:
                    nb = n * NB + b
                    base = nb * STEPS

                    def step(j, g):
                        pe.matmul(psY[g][:, 0:P], vt_s[:], y[g][:, (j - 1) % BLK, :], start=True,
                                  stop=True).then_inc(mm[g], 1)

                    def transposes(k, quad):
                        for g in range(G):
                            pe.wait_ge(t2_s[g], (nb * NBLK + k) * 4 + quad + 1)
                            for q in range(4):
                                last = pe.transpose(psT[g][quad % 2][:, q, :], y[g][:, 4 * quad + q, :], ident[:])
                            last.then_inc(tr[g], 1)

                    pe.wait_ge(wx_free, nb + 2)
                    for j in range(WARM):
                        for g in range(G):
                            if j:
                                pe.wait_ge(y_s[g], base + j)
                            step(j, g)
                    with pe.Fori(0, NBLK) as k:
                        for j in range(BLK):
                            for g in range(G):
                                if j == 0:
                                    pe.wait_ge(begin_s[g], nb + 1)
                                pe.wait_ge(y_s[g], base + k * BLK + (WARM + j))
                                step(j, g)
                            if j % 4 == 0 and j:
                                transposes(k, j // 4 - 1)
                        for g in range(G):
                            pe.wait_ge(y_s[g], base + k * BLK + (WARM + BLK))
                        transposes(k, 3)
                pe.wait_ge(bad_s, n + 1)
                pe.matmul(psF[0:1, 0:1], off_bad[:], ones[:], start=True, stop=True).then_inc(sum_mm, 1)

            passes(pe, one_pass, passed_r["pe"])


HALVES = 2
WID = 4
TILES = HALVES * WID
NM = ROWS // WID
ROUTE, GAP = 15, 8
FX = 16


def mixer_pass(nc, io, t2_d, out_d):
    ctx = ExitStack()
    with ctx:
        def sb(name, shape, dt=F32):
            return ctx.enter_context(nc.sbuf_tensor(name, shape, dt))

        def ps(name, shape):
            return ctx.enter_context(nc.psum_tensor(name, shape, F32))

        def sem(name):
            return ctx.enter_context(nc.semaphore(name))

        ident = sb("ident_m", [P, P])
        ln_w, ln_b, be = sb("ln_w", [P, P]), sb("ln_b", [P, P]), sb("be", [P, P])
        w1 = sb("w1", [P, 2, COLS])
        w2 = sb("w2", [P, 2, COLS])
        w3t = sb("w3t", [P, 2, COLS])
        b12 = sb("b12", [P, 4])
        b12w = sb("b12w", [P, 4, P])
        b3 = sb("b3", [P, COLS])
        w32 = sb("w32", [P, 2, COLS])
        mix = sb("mix", [P, 2, COLS])
        mix_b = sb("mix_b", [P, COLS])
        wet = sb("wet", [P, P])
        rw, rb, dec = sb("rw", [P, EXPERTS]), sb("rb", [P, EXPERTS]), sb("dec", [P, EXPERTS])
        ew = sb("ew", [P, EXPERTS * P])
        eb = sb("eb", [TILES * EXPERTS, TILES * P])
        mhalf = sb("mhalf_m", [P, TILES])

        t2 = [sb(f"t2_{u}", [P, TILES, P]) for u in range(4)]
        t2e = [sb(f"t2e{u}", [P, TILES, P]) for u in range(2)]
        statc = sb("statc", [P, TILES, 6])
        mvc = [sb(f"mvc{u}", [P, TILES, 2]) for u in range(2)]
        vc = sb("vc", [P, TILES])
        rsc = [sb(f"rsc{u}", [P, TILES]) for u in range(2)]
        xc = sb("xc", [P, TILES, P])
        xw = sb("xw", [P, TILES, P])
        xb = [sb(f"xb{u}", [P, TILES, P]) for u in range(2)]
        ug = [sb(f"ug{u}", [P, TILES, P]) for u in range(2)]
        mT = [sb(f"mT{u}", [P, WID, COLS]) for u in range(2)]
        t3 = [sb(f"t3_{u}", [P, TILES, P]) for u in range(2)]
        state = sb("state", [P, TILES, 6])
        mve = sb("mve", [P, TILES, 2])
        ve = sb("ve", [P, TILES])
        rse = sb("rse", [P, TILES])
        xe = [sb(f"xe{u}", [P, TILES, P]) for u in range(2)]
        xeT = [sb(f"xeT{u}", [P, TILES, P]) for u in range(2)]
        logit = sb("logit", [P, TILES, EXPERTS])
        logit2 = sb("logit2", [P, TILES, EXPERTS])
        is_max = sb("is_max", [P, TILES, EXPERTS])
        order = sb("order", [P, TILES, EXPERTS])
        pick = [sb(f"pick{i}", [P, TILES, EXPERTS]) for i in range(2)]
        share = [sb(f"share{i}", [P, TILES, EXPERTS]) for i in range(2)]
        top = [sb(f"top{i}", [P, TILES]) for i in range(2)]
        first = sb("first", [P, TILES])
        gap = sb("gap", [P, TILES])
        th = sb("th", [P, TILES])
        wgt = [sb(f"wgt{i}", [P, TILES]) for i in range(2)]
        gate = [sb(f"gate{u}", [P, TILES, EXPERTS]) for u in range(2)]
        gateT = [sb(f"gateT{u}", [TILES * EXPERTS, P]) for u in range(2)]
        acc = [sb(f"acc{u}", [P, TILES, P]) for u in range(2)]

        psC = ps("psC", [P, 2, 512])
        psD = ps("psD", [P, 2, 512])
        psE = [ps(f"psE{i}", [P, 2, 512]) for i in range(2)]

        w_in, fold, fold_v, ready = sem("w_in3"), sem("fold3"), sem("fold_v3"), sem("ready3")
        t2_in = [sem(f"t2_in{u}") for u in range(4)]
        statc_s, mvc_s, vc_s, rsc_s, t2e_s, xc_s, xw_s, xb_s, ug_s = (
            sem(n) for n in ("statc_s", "mvc_s", "vc_s", "rsc_s", "t2e_s", "xc_s", "xw_s", "xb_s", "ug_s"))
        mix_mm, mT_s, we_mm, t3_s = sem("mix_mm"), sem("mT_s"), sem("we_mm"), sem("t3_s")
        state_s, mve_s, ve_s, rse_s, xe_s, xeT_mm, xeT_s = (
            sem(n) for n in ("state_s", "mve_s", "ve_s", "rse_s", "xe_s", "xeT_mm", "xeT_s"))
        route_mm, logit_s, route_s, th_s, gateT_mm, gateT_s, eb_mm, acc_s = (
            sem(n) for n in ("route_mm", "logit_s", "route_s", "th_s", "gateT_mm", "gateT_s",
                             "eb_mm", "acc_s"))
        ex_mm, ex_s = sem("ex_mm"), sem("ex_s")
        out_s = [sem(f"out_s{u}") for u in range(2)]
        passed_pool, passed_dve, passed_pe = sem("passed_pool3"), sem("passed_dve3"), sem("passed_pe3")

        def view(d):
            return d.rearrange("(h g n v) c -> h g n v c", h=HALVES, g=8, v=FX)

        t2_v, out_v = view(t2_d), view(out_d)
        FIRST, LAST, LOOP0, LOOP1, U = -2, NM, 4, 60, 4
        PAIRS = TILES // 2

        def place(v, m, q, h):
            n = m * 4 - q * 4
            s = slice(n, n + FX) if isinstance(n, int) else bass.ds(n, FX)
            return v[h, :, s, q * WID:(q + 1) * WID, :]

        def need(engine, s, batches, per=1):
            if isinstance(batches, int):
                if batches > 0:
                    engine.wait_ge(s, min(batches, NM) * per)
            else:
                engine.wait_ge(s, batches * per if per > 1 else batches)

        block = ctx.enter_context(nc.Block())

        @block.sync
        def _(sp):
            loads = [(ident[:], io["ident"]), (ln_w[:], io["ln_w"]), (ln_b[:], io["ln_b"]), (be[:], io["be"]),
                     (w1[:], io["W1"].rearrange("(t p) g -> p t g", t=2)),
                     (w2[:], io["W2e"].rearrange("(t p) g -> p t g", t=2)),
                     (w3t[:], io["W3eT"].rearrange("(t p) g -> p t g", t=2)),
                     (b12[:], io["b12"]), (b3[:], io["b3"]), (wet[:], io["WeT"]), (rw[:], io["rw"]),
                     (rb[:], io["rb"]), (dec[:], io["dec"]), (ew[:], io["ew"]), (eb[:], io["eb"])]
            for dst, src in loads:
                sp.dma_start(dst, src).then_inc(w_in, 16)

            def body(m, u):
                if inside(m + 2, NM):
                    q = (u + 2) % 4
                    need(sp, xc_s, m - 1)
                    need(sp, t2e_s, m - 1)
                    for h in range(HALVES):
                        dst = t2[q][:, h * WID:(h + 1) * WID, :]
                        sp.dma_start(dst, place(t2_v, m + 2, q, h)).then_inc(t2_in[q], 16)
                if inside(m - 1, NM):
                    q = (u - 1) % 4
                    need(sp, ex_s, m, TILES * EXPERTS)
                    for h in range(HALVES):
                        src = acc[q % 2][:, h * WID:(h + 1) * WID, :]
                        sp.dma_start(place(out_v, m - 1, q, h), src).then_inc(out_s[q % 2], 16)

            pipeline(sp, body, FIRST - 1, LAST + 1, LOOP0, LOOP1, U)
            for u in range(2):
                sp.wait_ge(out_s[u], 32 * NM // 2)

        @block.gpsimd
        def _(pool):
            pool.memset(mhalf[:], -0.5).then_inc(ready, 1)
            pool.wait_ge(ready, 1)
            pool.wait_ge(w_in, 15 * 16)

            def body(m, u):
                if inside(m + 1, NM):
                    need(pool, mve_s, m + 2)
                    need(pool, rse_s, m + 1)
                    settle(pool, passed_pool)
                    pool.tensor_scalar(ve[:], mve[:, :, 1], 1.0, EPS_LN, ALU.mult, ALU.add).then_inc(ve_s, 1)
                    need(pool, ve_s, m + 2)
                    need(pool, xe_s, m + 1)
                    pool.tensor_tensor(rse[:], ve[:], mhalf[:], ALU.pow).then_inc(rse_s, 1)
                if inside(m + 2, NM):
                    b, q = u % 2, (u + 2) % 4
                    need(pool, mvc_s, m + 3)
                    need(pool, rsc_s, m + 2)
                    settle(pool, passed_pool)
                    pool.tensor_scalar(vc[:], mvc[b][:, :, 1], TWICE_MUL, TWICE_ADD, ALU.mult, ALU.add).then_inc(vc_s, 1)
                    need(pool, vc_s, m + 3)
                    need(pool, xc_s, m + 1)
                    pool.tensor_tensor(rsc[b][:], vc[:], mhalf[:], ALU.pow).then_inc(rsc_s, 1)
                    need(pool, t3_s, m + 1)
                    pool.tensor_tensor(t2e[b][:], t2[q][:], be[:].unsqueeze(1).to_broadcast([P, TILES, P]),
                                       ALU.add).then_inc(t2e_s, 1)

            pipeline(pool, body, FIRST, LAST, LOOP0, LOOP1, U)

        @block.vector
        def _(dve):
            dve.wait_ge(w_in, 15 * 16)
            for i in range(4):
                last = dve.tensor_copy(b12w[:, i, :], b12[:, i:i + 1].to_broadcast([P, P]))
            last.then_inc(fold_v, 1)
            dve.wait_ge(fold, 1)
            dve.tensor_copy(w32[:].rearrange("p t g -> p (t g)"), psC[:, 0, :]).then_inc(fold_v, 1)
            dve.wait_ge(fold, 2)
            dve.tensor_copy(mix[:].rearrange("p t g -> p (t g)"), psD[:, 0, :]).then_inc(fold_v, 1)
            dve.tensor_tensor(mix_b[:], psD[:, 1, 0:COLS], b3[:], ALU.add).then_inc(fold_v, 1)
            dve.wait_ge(fold_v, 4)

            def norm_in(m, u):
                b, q = u % 2, (u + 2) % 4
                dve.wait_ge(t2_in[q], (m + 2 - q) * 8 + 32)
                for t in range(TILES):
                    last = dve.bn_stats(statc[:, t, :], t2[q][:, t, :])
                last.then_inc(statc_s, 1)
                need(dve, statc_s, m + 3)
                need(dve, vc_s, m + 1)
                settle(dve, passed_dve)
                for t in range(TILES):
                    last = dve.bn_aggr(mvc[b][:, t, :], statc[:, t, :])
                last.then_inc(mvc_s, 1)
                need(dve, rsc_s, m + 3)
                need(dve, mvc_s, m + 3)
                for t in range(TILES):
                    last = dve.tensor_scalar(xc[:, t, :], t2[q][:, t, :], mvc[b][:, t, 0:1], rsc[b][:, t:t + 1],
                                             ALU.subtract, ALU.mult)
                last.then_inc(xc_s, 1)
                need(dve, xc_s, m + 3)
                dve.tensor_tensor(xw[:], xc[:], ln_w[:].unsqueeze(1).to_broadcast([P, TILES, P]), ALU.mult).then_inc(xw_s, 1)
                need(dve, xw_s, m + 3)
                need(dve, ug_s, m + 1)
                dve.tensor_tensor(xb[b][:], xw[:], ln_b[:].unsqueeze(1).to_broadcast([P, TILES, P]), ALU.add).then_inc(xb_s, 1)

            def route(m, a, n):
                wide = [P, TILES, EXPERTS]
                over = lambda v: v[:].unsqueeze(2).to_broadcast(wide)
                if n:
                    dve.wait_ge(route_s, m * ROUTE + n)
                if n in (0, 6):
                    i = n // 6
                    if n == 0:
                        need(dve, logit_s, m + 1)
                    ins = dve.tensor_reduce(top[i][:], (logit2 if i else logit)[:], AX.X, ALU.max)
                elif n in (1, 8):
                    i = n // 8
                    ins = dve.tensor_tensor(is_max[:], (logit2 if i else logit)[:], over(top[i]), ALU.is_equal)
                elif n in (2, 9):
                    ins = dve.tensor_tensor(order[:], is_max[:], dec[:].unsqueeze(1).to_broadcast(wide), ALU.mult)
                elif n in (3, 10):
                    ins = dve.tensor_reduce(first[:], order[:], AX.X, ALU.max)
                elif n in (4, 11):
                    ins = dve.tensor_tensor(pick[n // 11][:], order[:], over(first), ALU.is_equal)
                elif n == 5:
                    ins = dve.scalar_tensor_tensor(logit2[:], pick[0][:], -3e38, logit[:], ALU.mult, ALU.add)
                elif n == GAP - 1:
                    need(dve, th_s, m)
                    ins = dve.tensor_tensor(gap[:], top[0][:], top[1][:], ALU.subtract)
                elif n == 12:
                    need(dve, th_s, m + 1)
                    for i, sign in ((0, 0.5), (1, -0.5)):
                        ins = dve.tensor_scalar(wgt[i][:], th[:], sign, 0.5, ALU.mult, ALU.add)
                elif n == 13:
                    for i in range(2):
                        ins = dve.tensor_tensor(share[i][:], pick[i][:], over(wgt[i]), ALU.mult)
                else:
                    need(dve, gateT_mm, m - 1)
                    ins = dve.tensor_tensor(gate[a][:], share[0][:], share[1][:], ALU.add)
                ins.then_inc(route_s, 1)

            def body(m, u):
                a, b = (u + 1) % 2, u % 2
                for p in range(PAIRS):
                    if p == 3 and not inside(m, NM) and inside(m + 1, NM):
                        for n in range(ROUTE):
                            route(m + 1, a, n)
                    if inside(m, NM):
                        for e in range(EXPERTS):
                            for i in range(2):
                                t = 2 * p + i
                                if p == 3 and 2 * e + i < ROUTE and inside(m + 1, NM):
                                    route(m + 1, a, 2 * e + i)
                                if e % 4 == 0:
                                    dve.wait_ge(ex_mm, (m * PAIRS + p) * 4 + (2 if e else 0) + i + 1)
                                if p == 0 and e == 0 and i == 0:
                                    need(dve, acc_s, m + 1)
                                    need(dve, route_s, m + 1, ROUTE)
                                if e:
                                    dve.wait_ge(ex_s, (m * PAIRS + p) * 2 * EXPERTS + 2 * (e - 1) + i + 1)
                                dve.scalar_tensor_tensor(
                                    acc[b][:, t, :], psE[i][:, e // 4, (e % 4) * P:(e % 4 + 1) * P],
                                    gate[b][:, t, e:e + 1], acc[b][:, t, :], ALU.mult, ALU.add).then_inc(ex_s, 1)
                    if inside(m + 1, NM):
                        if p == 0:
                            need(dve, mix_mm, m + 2)
                            need(dve, we_mm, m)
                            dve.tensor_tensor(mT[a][:], psC[:].rearrange("p k (w g) -> p (k w) g", w=2),
                                              mix_b[:].unsqueeze(1).to_broadcast([P, WID, COLS]), ALU.add).then_inc(mT_s, 1)
                        if p == 1:
                            need(dve, we_mm, m + 2)
                            need(dve, t2e_s, m + 2)
                            dve.tensor_tensor(t3[a][:].rearrange("p t c -> p (t c)"), psD[:].rearrange("p k n -> p (k n)"),
                                              t2e[a][:].rearrange("p t c -> p (t c)"), ALU.add).then_inc(t3_s, 1)
                            need(dve, t3_s, m + 2)
                            for t in range(TILES):
                                last = dve.bn_stats(state[:, t, :], t3[a][:, t, :])
                            last.then_inc(state_s, 1)
                            need(dve, state_s, m + 2)
                            need(dve, ve_s, m + 1)
                            settle(dve, passed_dve)
                            for t in range(TILES):
                                last = dve.bn_aggr(mve[:, t, :], state[:, t, :])
                            last.then_inc(mve_s, 1)
                            need(dve, mve_s, m + 2)
                            need(dve, rse_s, m + 2)
                            need(dve, xeT_mm, m)
                            for t in range(TILES):
                                last = dve.tensor_scalar(xe[a][:, t, :], t3[a][:, t, :], mve[:, t, 0:1], rse[:, t:t + 1],
                                                         ALU.subtract, ALU.mult)
                            last.then_inc(xe_s, 1)
                        if p == 2:
                            need(dve, route_mm, m + 2)
                            dve.tensor_tensor(logit[:], psD[:, 0, 0:TILES * EXPERTS].rearrange("p (t e) -> p t e", t=TILES),
                                              rb[:].unsqueeze(1).to_broadcast([P, TILES, EXPERTS]), ALU.add).then_inc(logit_s, 1)
                        if p == 3:
                            if inside(m + 2, NM):
                                norm_in(m, u)
                            need(dve, eb_mm, m + 2)
                            need(dve, out_s[a], m + 1 - a, 16)
                            dve.tensor_tensor(acc[a][:].rearrange("p t c -> p (t c)"), psD[:].rearrange("p k n -> p (k n)"),
                                              t3[a][:].rearrange("p t c -> p (t c)"), ALU.add).then_inc(acc_s, 1)
                    elif p == 3 and inside(m + 2, NM):
                        norm_in(m, u)

            pipeline(dve, body, FIRST, LAST, LOOP0, LOOP1, U)

        @block.scalar
        def _(act):
            def body(m, u):
                a, b = (u + 1) % 2, u % 2
                if inside(m + 1, NM):
                    for i in range(2):
                        need(act, xeT_mm, m + 2)
                        need(act, ex_mm, m, 4 * PAIRS)
                        last = act.activation(xeT[a][:, i * WID:(i + 1) * WID].rearrange("p t c -> p (t c)"), psC[:, i, :],
                                              ACT.Identity)
                    last.then_inc(xeT_s, 1)
                    act.wait_ge(route_s, (m + 1) * ROUTE + GAP)
                    act.activation(th[:], gap[:], ACT.Tanh, scale=0.5).then_inc(th_s, 1)
                if inside(m + 2, NM):
                    need(act, xb_s, m + 3)
                    need(act, mix_mm, m + 1)
                    act.activation(ug[b][:], xb[b][:], ACT.Gelu).then_inc(ug_s, 1)
                if inside(m + 1, NM):
                    need(act, gateT_mm, m + 2)
                    need(act, eb_mm, m)
                    act.activation(gateT[a][:], psC[0:TILES * EXPERTS, 0, 0:P], ACT.Identity).then_inc(gateT_s, 1)

            pipeline(act, body, FIRST, LAST, LOOP0, LOOP1, U)

        @block.tensor
        def _(pe):
            pe.wait_ge(w_in, 15 * 16)
            pe.wait_ge(fold_v, 1)
            for o in range(2):
                for t in range(2):
                    last = pe.matmul(psC[:, 0, o * COLS:(o + 1) * COLS], w2[:, t, o * P:(o + 1) * P], w3t[:, t, :],
                                     start=t == 0, stop=t == 1)
            last.then_inc(fold, 1)
            pe.wait_ge(fold_v, 2)
            for o in range(2):
                for t in range(2):
                    pe.matmul(psD[:, 0, o * COLS:(o + 1) * COLS], w1[:, t, o * P:(o + 1) * P], w32[:, t, :],
                              start=t == 0, stop=t == 1)
            for i in range(4):
                last = pe.matmul(psD[:, 1, 0:COLS], b12w[:, i, :], (w32 if i < 2 else w3t)[:, i % 2, :],
                                 start=i == 0, stop=i == 3)
            last.then_inc(fold, 1)
            pe.wait_ge(fold_v, 4)

            def body(m, u):
                a, b = (u + 1) % 2, u % 2
                for p in range(PAIRS):
                    if inside(m, NM):
                        for half in range(2):
                            for i in range(2):
                                t = 2 * p + i
                                if isinstance(m, int) and m == 0 and p == 0:
                                    pass
                                else:
                                    pe.wait_ge(ex_s, ((m * PAIRS + p) - 1) * 2 * EXPERTS + 8 * half + 7 + i)
                                if p == 0 and half == 0 and i == 0:
                                    need(pe, xeT_s, m + 1)
                                pe.matmul(psE[i][:, half, :], xeT[b][:, t, :], ew[:, half * 512:(half + 1) * 512],
                                          start=True, stop=True).then_inc(ex_mm, 1)
                    if inside(m + 1, NM):
                        if p == 0:
                            need(pe, ug_s, m + 2)
                            need(pe, gateT_s, m + 1)
                            for w in range(WID):
                                for h in range(HALVES):
                                    last = pe.matmul(psC[:, w // 2, (w % 2) * COLS:(w % 2 + 1) * COLS],
                                                     ug[a][:, h * WID + w, :], mix[:, h, :], start=h == 0, stop=h == 1)
                            last.then_inc(mix_mm, 1)
                        if p == 1:
                            need(pe, mT_s, m + 2)
                            need(pe, acc_s, m + 1)
                            for h in range(HALVES):
                                for w in range(WID):
                                    last = pe.matmul(psD[:, h, w * P:(w + 1) * P], mT[a][:, w, h * P:(h + 1) * P], wet[:],
                                                     start=True, stop=True)
                            last.then_inc(we_mm, 1)
                        if p == 2:
                            need(pe, xe_s, m + 2)
                            for t in range(TILES):
                                last = pe.transpose(psC[:, t // 4, (t % 4) * P:(t % 4 + 1) * P], xe[a][:, t, :], ident[:])
                            last.then_inc(xeT_mm, 1)
                            need(pe, xeT_s, m + 2)
                            for t in range(TILES):
                                last = pe.matmul(psD[:, 0, t * EXPERTS:(t + 1) * EXPERTS], xeT[a][:, t, :], rw[:],
                                                 start=True, stop=True)
                            last.then_inc(route_mm, 1)
                        if p == 3:
                            need(pe, route_s, m + 2, ROUTE)
                            settle(pe, passed_pe)
                            pe.transpose(psC[0:TILES * EXPERTS, 0, 0:P], gate[a][:].rearrange("p t e -> p (t e)"),
                                         ident[:]).then_inc(gateT_mm, 1)
                            need(pe, gateT_s, m + 2)
                            need(pe, logit_s, m + 2)
                            for h in range(2):
                                last = pe.matmul(psD[:, h, :], gateT[a][:], eb[:, h * 512:(h + 1) * 512], start=True, stop=True)
                            last.then_inc(eb_mm, 1)

            pipeline(pe, body, FIRST, LAST, LOOP0, LOOP1, U)


def metaformer(nc, io, out_d):
    zt_d = nc.dram_tensor("zt_scratch", [P, TOK], F32, kind="Internal").ap()
    bias_d = nc.dram_tensor("bias_scratch", [ROWS, HEADS, COLS], F32, kind="Internal").ap()
    t1_d = nc.dram_tensor("t1_scratch", [TOK, P], F32, kind="Internal").ap()
    t2_d = nc.dram_tensor("t2_scratch", [TOK, P], F32, kind="Internal").ap()
    wx_d = nc.dram_tensor("wx_scratch", [P, WARM + TOK], F32, kind="Internal").ap()
    with nc.sbuf_tensor("bn_sb", [P, 2], F32) as bn_sb:
        norm_pass(nc, io, zt_d, bias_d)
        attention_pass(nc, io, zt_d, bias_d, t1_d, wx_d, bn_sb)
        recurrence_pass(nc, io, t1_d, wx_d, t2_d, bn_sb)
        mixer_pass(nc, io, t2_d, out_d)


def layouts(a):
    f = np.float32
    rows = lambda v: np.ascontiguousarray(np.broadcast_to(v, (P, v.shape[-1])))
    io = {"x": a["x"].reshape(TOK, P)}
    for n in ("Wq", "Wk", "Wv", "Wg", "Wo"):
        io[n] = a["L0_conv_" + n]
    io["WbPad"] = np.zeros((P, DH), f)
    io["WbPad"][:, :HEADS] = a["L0_conv_Wb"]
    io["ln_cols"] = np.stack([a["L0_conv_ln_scale"], a["L0_conv_ln_bias"]], axis=1)
    io["WT"], io["VT"] = a["L0_ffn_W"].T, a["L0_ffn_V"].T
    io["bn_cols"] = np.stack([a["L0_ffn_gamma"], a["L0_ffn_beta"]], axis=1)
    io["ln_w"], io["ln_b"], io["be"] = rows(a["L1_conv_ln_w"]), rows(a["L1_conv_ln_b"]), rows(a["L1_conv_be"])
    io["W1"] = a["L1_conv_W1"]
    w2 = np.zeros((8, 2, 8, 2, 8, 2, 8, 2), f)
    w3t = np.zeros((2, 8, 2, 8, 2, 8, 2, 8), f)
    for i in range(2):
        for j in range(2):
            w2[:, i, :, j, :, i, :, j] = a["L1_conv_W2"].reshape(8, 8, 8, 8)
    for i in range(8):
        for j in range(8):
            w3t[:, i, :, j, :, i, :, j] = a["L1_conv_W3"].T.reshape(2, 2, 2, 2)
    io["W2e"], io["W3eT"] = w2.reshape(COLS, COLS), w3t.reshape(COLS, COLS)
    b2 = np.broadcast_to(a["L1_conv_b2"].reshape(8, 1, 8, 1), (8, 2, 8, 2)).reshape(COLS)
    b3 = np.broadcast_to(a["L1_conv_b3"].reshape(2, 1, 2, 1), (2, 8, 2, 8)).reshape(COLS)
    io["b12"] = np.stack([a["L1_conv_b1"][:P], a["L1_conv_b1"][P:], b2[:P], b2[P:]], axis=1)
    io["b3"] = rows(b3)
    io["WeT"] = a["L1_conv_We"].T
    io["rw"], io["rb"] = a["L1_ffn_router_w"], rows(a["L1_ffn_router_b"])
    io["ew"] = a["L1_ffn_expert_w"].transpose(1, 0, 2).reshape(P, EXPERTS * P)
    eb = np.zeros((TILES, EXPERTS, TILES, P), f)
    for t in range(TILES):
        eb[t, :, t, :] = a["L1_ffn_expert_b"]
    io["eb"] = eb.reshape(TILES * EXPERTS, TILES * P)
    io["ident"] = np.eye(P, dtype=f)
    io["dec"] = rows(np.arange(EXPERTS, 0, -1).astype(f))
    return {n: np.ascontiguousarray(v) for n, v in io.items()}


def kernel(**inputs):
    import concourse.bacc as bacc
    from concourse.bass_utils import run_bass_kernel_spmd

    arrays = layouts({n: np.asarray(v) for n, v in inputs.items()})
    nc = bacc.Bacc("TRN2", target_bir_lowering=False, num_devices=1)
    io = {n: nc.dram_tensor("in_" + n, v.shape, F32, kind="ExternalInput").ap() for n, v in arrays.items()}
    out = nc.dram_tensor("out", (TOK, P), F32, kind="ExternalOutput").ap()
    metaformer(nc, io, out)
    r = run_bass_kernel_spmd(nc, [{"in_" + n: v for n, v in arrays.items()}], core_ids=[0])
    return r.results[0]["out"].reshape(1, ROWS, COLS, P)
```

```python
from contextlib import ExitStack

import numpy as np

import concourse.bass as bass
from concourse import mybir

F32 = mybir.dt.float32
F32R = mybir.dt.float32r
I32 = mybir.dt.int32
ACT = mybir.ActivationFunctionType
ALU = mybir.AluOpType
AX = mybir.AxisListType

P = 128
ROWS = 256
COLS = 256
TOK = ROWS * COLS
NT = COLS // P
HEADS, DH = 4, 32
EXPERTS = 8
EPS_LN, EPS_LNC, EPS_BN = 1e-5, 1e-6, 1e-5
TWICE_MUL, TWICE_ADD = 1.0 + EPS_LN, EPS_LN * EPS_LNC


SEG = 64
WARM = 16
LANES = TOK // SEG
G = 2
BATCH = G * P
NB = LANES // BATCH
STEPS = WARM + SEG
BLK = 16
NBLK = SEG // BLK
TOL = 2.0 ** -20


def need(engine, sem, rows, per=1):
    if isinstance(rows, int):
        if rows > 0:
            engine.wait_ge(sem, min(rows, ROWS) * per)
    else:
        engine.wait_ge(sem, rows * per if per > 1 else rows)


def settle(engine, passed):
    engine.sem_inc(passed, 1)


def inside(row, count=ROWS):
    return not isinstance(row, int) or 0 <= row < count


def pipeline(engine, body, first, last, loop_from, loop_to, unroll):
    for k in range(first, loop_from):
        body(k, k % unroll)
    with engine.Fori(0, (loop_to - loop_from) // unroll) as turn:
        for u in range(unroll):
            body(turn * unroll + (loop_from + u), (loop_from + u) % unroll)
    for k in range(loop_to, last):
        body(k, k % unroll)


QR = 4
QT = QR * NT


def norm_pass(nc, io, zt_d, bias_d):
    ctx = ExitStack()
    with ctx:
        def sb(name, shape, dt=F32):
            return ctx.enter_context(nc.sbuf_tensor(name, shape, dt))

        def sem(name):
            return ctx.enter_context(nc.semaphore(name))

        ident = sb("ident0", [P, P])
        wb = sb("wb", [P, DH])
        ln_cols = sb("ln_cols", [P, 2])
        mhalf = sb("mhalf0", [P, QT])
        x_t = [sb(f"x0_{u}", [P, QT, P]) for u in range(4)]
        stat = sb("stat0", [P, QT, 6])
        mv = [sb(f"mv0_{u}", [P, QT, 2]) for u in range(2)]
        v = sb("v0", [P, QT])
        rs = [sb(f"rs0_{u}", [P, QT]) for u in range(2)]
        xh = [sb(f"xh0_{u}", [P, QT, P]) for u in range(2)]
        zt = [sb(f"zt0_{u}", [P, QR * COLS]) for u in range(2)]
        bias = [sb(f"bias0_{u}", [P, COLS]) for u in range(2)]
        psT = [ctx.enter_context(nc.psum_tensor(f"psT0_{i}", [P, 2, 512], F32)) for i in range(2)]
        psB = [ctx.enter_context(nc.psum_tensor(f"psB0_{i}", [P, 512], F32)) for i in range(2)]

        w_in, setup, passed_pool, passed_dve = sem("w_in0"), sem("setup0"), sem("passed_pool0"), sem("passed_dve0")
        x_in = [sem(f"x_in0_{u}") for u in range(4)]
        stat_s, mv_s, v_s, rs_s, xh_s, tr_mm, zt_s, b_mm, b_s = (
            sem(n + "0") for n in ("stat_s", "mv_s", "v_s", "rs_s", "xh_s", "tr_mm", "zt_s", "b_mm", "b_s"))
        zt_out = [sem(f"zt_out0_{u}") for u in range(2)]
        b_out = [sem(f"b_out0_{u}") for u in range(2)]
        x_v = io["x"].rearrange("(m j p) c -> m p j c", j=QT, p=P)
        zt_v = zt_d.rearrange("p (m t) -> m p t", t=QR * COLS)
        b_v = bias_d.rearrange("(m r) h k -> m r h k", r=QR)
        N0 = ROWS // QR
        FIRST, LAST, LOOP0, LOOP1, U = -2, N0, 4, 60, 4

        def upto(engine, s, n, per=1):
            need(engine, s, min(n, N0) if isinstance(n, int) else n, per)

        block = ctx.enter_context(nc.Block())

        @block.sync
        def _(sp):
            for dst, src in ((ident[:], io["ident"]), (wb[:], io["WbPad"]), (ln_cols[:], io["ln_cols"])):
                sp.dma_start(dst, src).then_inc(w_in, 16)

            def body(m, u):
                if inside(m + 3, N0):
                    upto(sp, xh_s, m)
                    sp.dma_start(x_t[(u + 3) % 4][:], x_v[m + 3]).then_inc(x_in[(u + 3) % 4], 16)
                if inside(m, N0):
                    upto(sp, zt_s, m + 1)
                    sp.dma_start(zt_v[m], zt[u % 2][:]).then_inc(zt_out[u % 2], 16)
                    upto(sp, b_s, m + 1)
                    for r in range(QR):
                        sp.dma_start(b_v[m, r], bias[u % 2][DH * r:DH * r + HEADS, :]).then_inc(b_out[u % 2], 16)

            pipeline(sp, body, FIRST - 1, LAST, LOOP0, LOOP1, U)
            for u in range(2):
                sp.wait_ge(zt_out[u], 16 * N0 // 2)
                sp.wait_ge(b_out[u], 16 * QR * N0 // 2)

        @block.gpsimd
        def _(pool):
            pool.memset(mhalf[:], -0.5).then_inc(setup, 1)
            pool.wait_ge(setup, 1)

            def body(m, u):
                b = u % 2
                if inside(m + 2, N0):
                    upto(pool, mv_s, m + 3)
                    upto(pool, rs_s, m + 2)
                    settle(pool, passed_pool)
                    pool.tensor_scalar(v[:], mv[b][:, :, 1], TWICE_MUL, TWICE_ADD, ALU.mult, ALU.add).then_inc(v_s, 1)
                    upto(pool, v_s, m + 3)
                    upto(pool, xh_s, m + 1)
                    pool.tensor_tensor(rs[b][:], v[:], mhalf[:], ALU.pow).then_inc(rs_s, 1)

            pipeline(pool, body, FIRST, LAST, LOOP0, LOOP1, U)

        @block.vector
        def _(dve):
            def body(m, u):
                b, q = u % 2, (u + 2) % 4
                if inside(m + 2, N0):
                    dve.wait_ge(x_in[q], (m + 2 - q) * 4 + 16)
                    upto(dve, mv_s, m + 2)
                    for t in range(QT):
                        last = dve.bn_stats(stat[:, t, :], x_t[q][:, t, :])
                    last.then_inc(stat_s, 1)
                if inside(m, N0):
                    upto(dve, b_mm, m + 1)
                    upto(dve, b_out[b], m - b, 16 * QR // 2)
                    dve.tensor_scalar(bias[b][:], psB[b][:, 0:COLS], -1.0, None, ALU.mult).then_inc(b_s, 1)
                if inside(m + 2, N0):
                    upto(dve, stat_s, m + 3)
                    upto(dve, v_s, m + 1)
                    upto(dve, xh_s, m + 1)
                    settle(dve, passed_dve)
                    for t in range(QT):
                        last = dve.bn_aggr(mv[b][:, t, :], stat[:, t, :])
                    last.then_inc(mv_s, 1)
                    upto(dve, rs_s, m + 3)
                    upto(dve, mv_s, m + 3)
                    upto(dve, tr_mm, m + 1)
                    for t in range(QT):
                        last = dve.tensor_scalar(xh[b][:, t, :], x_t[q][:, t, :], mv[b][:, t, 0:1], rs[b][:, t:t + 1],
                                                 ALU.subtract, ALU.mult)
                    last.then_inc(xh_s, 1)

            pipeline(dve, body, FIRST, LAST, LOOP0, LOOP1, U)

        @block.scalar
        def _(act):
            act.wait_ge(w_in, 48)

            def body(m, u):
                a = (u + 1) % 2
                if inside(m + 1, N0):
                    upto(act, tr_mm, m + 2)
                    upto(act, zt_out[a], m + 1 - a, 8)
                    upto(act, b_mm, m)
                    for i in range(2):
                        last = act.activation(zt[a][:, i * 512:(i + 1) * 512], psT[a][:, i, :], ACT.Identity,
                                              bias=ln_cols[:, 1:2], scale=ln_cols[:, 0:1])
                    last.then_inc(zt_s, 1)

            pipeline(act, body, FIRST, LAST, LOOP0, LOOP1, U)

        @block.tensor
        def _(pe):
            pe.wait_ge(w_in, 48)

            def body(m, u):
                a = (u + 1) % 2
                if inside(m + 1, N0):
                    upto(pe, xh_s, m + 2)
                    upto(pe, zt_s, m)
                    for t in range(QT):
                        last = pe.transpose(psT[a][:, t // 4, (t % 4) * P:(t % 4 + 1) * P], xh[a][:, t, :], ident[:])
                    last.then_inc(tr_mm, 1)
                if inside(m, N0):
                    upto(pe, zt_s, m + 1)
                    upto(pe, b_s, m - 1)
                    for r in range(QR):
                        last = pe.matmul(psB[u % 2][DH * r:DH * (r + 1), 0:COLS], wb[:],
                                         zt[u % 2][:, r * COLS:(r + 1) * COLS], start=True, stop=True)
                    last.then_inc(b_mm, 1)

            pipeline(pe, body, FIRST, LAST, LOOP0, LOOP1, U)


def attention_pass(nc, io, zt_d, bias_d, t1_d, wx_d, bn_sb):
    ctx = ExitStack()
    with ctx:
        def sb(name, shape, dt=F32):
            return ctx.enter_context(nc.sbuf_tensor(name, shape, dt))

        def ps(name, shape):
            return ctx.enter_context(nc.psum_tensor(name, shape, F32))

        def sem(name):
            return ctx.enter_context(nc.semaphore(name))

        w_s = sb("w_s", [P, 4, P])
        wo_s = sb("wo_s", [P, P])
        wt_s = sb("wt_s", [P, P])
        ident = sb("ident", [P, P])
        half = sb("half", [P, DH])
        mhalf = sb("mhalf", [P, NT])
        bias = sb("bias", [P, NT, HEADS, COLS])
        pad = sb("pad", [P, WARM])

        x_t = [sb(f"x_t{u}", [P, NT, P]) for u in range(4)]
        zT = [sb(f"zT{u}", [P, COLS]) for u in range(4)]
        qT = [sb(f"qT{u}", [P, COLS]) for u in range(2)]
        kT = [sb(f"kT{u}", [P, COLS]) for u in range(2)]
        vv = [sb(f"vv{u}", [P, NT, P]) for u in range(2)]
        th = [sb(f"th{u}", [P, COLS]) for u in range(2)]
        score = [sb(f"score{u}", [P, NT, HEADS, COLS]) for u in range(2)]
        least = [sb(f"least{u}", [P, NT, HEADS]) for u in range(2)]
        prob = [sb(f"prob{u}", [P, NT, HEADS, COLS]) for u in range(2)]
        total = [sb(f"total{u}", [P, NT * HEADS]) for u in range(2)]
        rtotal = [sb(f"rtotal{u}", [P, NT * HEADS]) for u in range(2)]
        spread = [sb(f"spread{u}", [P, NT, P]) for u in range(2)]
        probT = [sb(f"probT{u}", [P, HEADS, NT, COLS]) for u in range(2)]
        gated = [sb(f"gated{u}", [P, COLS]) for u in range(2)]
        og = [sb(f"og{u}", [P, COLS]) for u in range(2)]
        t1 = [sb(f"t1_{u}", [P, NT, P]) for u in range(2)]
        stat2 = [sb(f"stat2_{u}", [P, NT, 6]) for u in range(2)]
        mv2 = [sb(f"mv2_{u}", [P, NT, 2]) for u in range(2)]
        v2 = [sb(f"v2_{u}", [P, NT]) for u in range(2)]
        rs2 = [sb(f"rs2_{u}", [P, NT]) for u in range(2)]
        yh = [sb(f"yh{u}", [P, NT, P]) for u in range(2)]
        yT = [sb(f"yT{u}", [P, COLS]) for u in range(2)]
        wx = [sb(f"wx{u}", [P, COLS]) for u in range(2)]
        wx_stat = sb("wx_stat", [P, ROWS, 6])

        psS = [ps(f"psS{i}", [P, 512]) for i in range(2)]
        psT = [ps(f"psT{i}", [P, 512]) for i in range(2)]
        psQK, psVG = ps("psQK", [P, 512]), ps("psVG", [P, 512])
        psO = ps("psO", [P, 512])
        psM = ps("psM", [P, 512])

        w_in, setup_d, pad_out, passed_pool, passed_dve = (
            sem(n) for n in ("w_in", "setup_d", "pad_out", "passed_pool", "passed_dve"))
        x_in = [sem(f"x_in{u}") for u in range(4)]
        z_in = [sem(f"z_in{u}") for u in range(4)]
        qk_mm, qk_s, vg_mm, vg_s, s_mm, score_s, prob_s, tr_mm, probT_s = (
            sem(n) for n in ("qk_mm", "qk_s", "vg_mm", "vg_s", "s_mm", "score_s", "prob_s", "tr_mm", "probT_s"))
        rtotal_s, spread_s, pv_mm, rt_mm, gated_s, og_s, out_mm = (
            sem(n) for n in ("rtotal_s", "spread_s", "pv_mm", "rt_mm", "gated_s", "og_s", "out_mm"))
        t1_s, stat2_s, mv2_s, v2_s, rs2_s, yh_s, yT_mm, yT_s, wx_mm, wx_s, wstat_s = (
            sem(n) for n in ("t1_s", "stat2_s", "mv2_s", "v2_s", "rs2_s", "yh_s", "yT_mm", "yT_s",
                             "wx_mm", "wx_s", "wstat_s"))
        t1_out = [sem(f"t1_out{u}") for u in range(2)]
        wx_out = [sem(f"wx_out{u}") for u in range(2)]

        x_v = io["x"].rearrange("(r j p) c -> r p j c", j=NT, p=P)
        z_v = zt_d.rearrange("p (r t) -> r p t", t=COLS)
        t1_v = t1_d.rearrange("(r j p) c -> r p j c", j=NT, p=P)
        wx_v = wx_d[:, WARM:WARM + TOK].rearrange("p (r t) -> r p t", t=COLS)

        FIRST, LAST, LOOP0, LOOP1, U = -1, ROWS + 3, 4, 248, 4
        UNITS = 4
        block = ctx.enter_context(nc.Block())

        @block.sync
        def _(sp):
            loads = [(w_s[:, i, :], io[n]) for i, n in enumerate(("Wq", "Wk", "Wv", "Wg"))]
            loads += [(wo_s[:], io["Wo"]), (wt_s[:], io["WT"]), (ident[:], io["ident"])]
            loads += [(bias[:, t], bias_d[t * P:(t + 1) * P]) for t in range(NT)]
            for dst, src in loads:
                sp.dma_start(dst, src).then_inc(w_in, 16)
            sp.wait_ge(setup_d, 3)
            sp.dma_start(wx_d[:, 0:WARM], pad[:]).then_inc(pad_out, 16)

            def body(k, u):
                if inside(k + 3):
                    need(sp, vg_mm, k)
                    sp.dma_start(zT[(u + 3) % 4][:], z_v[k + 3]).then_inc(z_in[(u + 3) % 4], 16)
                if inside(k + 1):
                    need(sp, t1_s, k - 2)
                    sp.dma_start(x_t[(u + 1) % 4][:], x_v[k + 1]).then_inc(x_in[(u + 1) % 4], 16)
                if inside(k - 3):
                    need(sp, wx_s, k - 2)
                    sp.dma_start(wx_v[k - 3], wx[(u - 3) % 2][:]).then_inc(wx_out[(u - 3) % 2], 16)
                if inside(k - 2):
                    need(sp, t1_s, k - 1)
                    sp.dma_start(t1_v[k - 2], t1[u % 2][:]).then_inc(t1_out[u % 2], 16)

            pipeline(sp, body, FIRST - 2, LAST, LOOP0, LOOP1, U)
            sp.wait_ge(pad_out, 16)
            for u in range(2):
                sp.wait_ge(t1_out[u], 16 * ROWS // 2)
                sp.wait_ge(wx_out[u], 16 * ROWS // 2)

        @block.gpsimd
        def _(pool):
            pool.memset(mhalf[:], -0.5).then_inc(setup_d, 1)
            pool.memset(half[:], 0.5).then_inc(setup_d, 1)
            pool.memset(pad[:], 0.0).then_inc(setup_d, 1)
            pool.wait_ge(setup_d, 3)

            def body(k, u):
                a, b = (u + 1) % 2, u % 2
                if inside(k - 1):
                    need(pool, rtotal_s, k)
                    need(pool, rt_mm, k - 2)
                    pool.tensor_tensor(
                        spread[a][:].rearrange("p t (h d) -> p (t h) d", h=HEADS),
                        rtotal[a][:].unsqueeze(2).to_broadcast([P, NT * HEADS, DH]),
                        half[:].unsqueeze(1).to_broadcast([P, NT * HEADS, DH]), ALU.mult).then_inc(spread_s, 1)
                if inside(k - 2):
                    need(pool, mv2_s, k - 1)
                    need(pool, rs2_s, k - 3)
                    settle(pool, passed_pool)
                    pool.tensor_scalar(v2[b][:], mv2[b][:, :, 1], 1.0, EPS_LN, ALU.mult, ALU.add).then_inc(v2_s, 1)
                    need(pool, v2_s, k - 1)
                    need(pool, yh_s, k - 3)
                    pool.tensor_tensor(rs2[b][:], v2[b][:], mhalf[:], ALU.pow).then_inc(rs2_s, 1)

            pipeline(pool, body, FIRST, LAST, LOOP0, LOOP1, U)

        @block.vector
        def _(dve):
            dve.wait_ge(w_in, 9 * 16)

            def body(k, u):
                a, b = (u + 1) % 2, u % 2
                if inside(k - 1):
                    need(dve, prob_s, k, UNITS)
                    need(dve, spread_s, k - 2)
                    dve.reciprocal(rtotal[a][:], total[a][:]).then_inc(rtotal_s, 1)
                for n in range(UNITS):
                    if inside(k):
                        dve.wait_ge(s_mm, k * UNITS + n + 1)
                        need(dve, prob_s, k - 1, UNITS)
                        settle(dve, passed_dve)
                        for t in range(NT):
                            last = dve.tensor_tensor_reduce(
                                out=score[b][:, t, n, :], in0=psS[n % 2][:, t * COLS:(t + 1) * COLS],
                                in1=bias[:, t, n, :], scale=1.0, scalar=3e38, op0=ALU.add, op1=ALU.min,
                                accum_out=least[b][:, t, n:n + 1])
                        last.then_inc(score_s, 1)
                    if inside(k - 1):
                        dve.wait_ge(tr_mm, (k - 1) * UNITS + n + 1)
                        need(dve, pv_mm, k - 2)
                        dve.tensor_copy(probT[a][:, n].rearrange("p t q -> p (t q)"), psT[n % 2][:]).then_inc(probT_s, 1)
                    if inside(k - 2):
                        if n == 1:
                            need(dve, out_mm, k - 1)
                            dve.wait_ge(x_in[(u - 2) % 4], (k - 2 - (u - 2) % 4) * 4 + 16)
                            need(dve, yh_s, k - 3)
                            need(dve, t1_out[b], k - 2 - b, 8)
                            dve.tensor_tensor(t1[b][:], psM[:, 0:COLS].rearrange("p (j c) -> p j c", j=NT),
                                              x_t[(u - 2) % 4][:], ALU.add).then_inc(t1_s, 1)
                        if n == 2:
                            need(dve, t1_s, k - 1)
                            need(dve, mv2_s, k - 3)
                            for j in range(NT):
                                last = dve.bn_stats(stat2[b][:, j, :], t1[b][:, j, :])
                            last.then_inc(stat2_s, 1)
                        if n == 3:
                            need(dve, stat2_s, k - 1)
                            need(dve, v2_s, k - 3)
                            need(dve, yh_s, k - 3)
                            settle(dve, passed_dve)
                            for j in range(NT):
                                last = dve.bn_aggr(mv2[b][:, j, :], stat2[b][:, j, :])
                            last.then_inc(mv2_s, 1)
                if inside(k - 3):
                    need(dve, wx_s, k - 2)
                    dve.bn_stats(wx_stat[:, bass.ds(k - 3, 1), :], wx[a][:]).then_inc(wstat_s, 1)
                if inside(k - 2):
                    need(dve, rs2_s, k - 1)
                    need(dve, mv2_s, k - 1)
                    need(dve, yT_mm, k - 3)
                    for j in range(NT):
                        last = dve.tensor_scalar(yh[b][:, j, :], t1[b][:, j, :], mv2[b][:, j, 0:1],
                                                 rs2[b][:, j:j + 1], ALU.subtract, ALU.mult)
                    last.then_inc(yh_s, 1)
                if inside(k - 1):
                    need(dve, rt_mm, k)
                    need(dve, vg_s, k)
                    need(dve, og_s, k - 2)
                    dve.scalar_tensor_tensor(gated[a][:], th[a][:], 1.0, psO[:, 0:COLS], ALU.add,
                                             ALU.mult).then_inc(gated_s, 1)
                    need(dve, gated_s, k)
                    need(dve, out_mm, k - 2)
                    dve.tensor_tensor(og[a][:], gated[a][:], psO[:, COLS:2 * COLS], ALU.mult).then_inc(og_s, 1)

            pipeline(dve, body, FIRST, LAST, LOOP0, LOOP1, U)
            dve.wait_ge(wstat_s, ROWS)
            dve.bn_aggr(bn_sb[:, 0:2], wx_stat[:].rearrange("p r s -> p (r s)")).then_inc(wstat_s, 1)

        @block.scalar
        def _(act):
            def body(k, u):
                a, b = (u + 1) % 2, u % 2
                if inside(k):
                    for n in range(UNITS):
                        act.wait_ge(score_s, k * UNITS + n + 1)
                        need(act, tr_mm, k - 1, UNITS)
                        need(act, rtotal_s, k - 1)
                        for t in range(NT):
                            last = act.activation(prob[b][:, t, n, :], score[b][:, t, n, :], ACT.Exp,
                                                  bias=least[b][:, t, n:n + 1], scale=-1.0,
                                                  accum_out=total[b][:, t * HEADS + n:t * HEADS + n + 1])
                        last.then_inc(prob_s, 1)
                if inside(k + 1):
                    need(act, qk_mm, k + 2)
                    need(act, s_mm, k, UNITS)
                    act.activation(qT[a][:], psQK[:, 0:COLS], ACT.Identity, scale=-(DH ** -0.5))
                    act.activation(kT[a][:], psQK[:, COLS:2 * COLS], ACT.Identity).then_inc(qk_s, 1)
                if inside(k):
                    need(act, vg_mm, k + 1)
                    need(act, pv_mm, k - 1)
                    need(act, gated_s, k - 1)
                    act.activation(vv[b][:].rearrange("p t c -> p (t c)"), psVG[:, 0:COLS], ACT.Identity)
                    act.activation(th[b][:], psVG[:, COLS:2 * COLS], ACT.Tanh, scale=0.5).then_inc(vg_s, 1)
                if inside(k - 2):
                    need(act, yT_mm, k - 1)
                    need(act, wx_mm, k - 3)
                    act.activation(yT[b][:], psM[:, 0:COLS], ACT.Identity).then_inc(yT_s, 1)
                    need(act, wx_mm, k - 1)
                    need(act, wstat_s, k - 3)
                    need(act, wx_out[b], k - 2 - b, 8)
                    act.activation(wx[b][:], psM[:, COLS:2 * COLS], ACT.Identity).then_inc(wx_s, 1)

            pipeline(act, body, FIRST, LAST, LOOP0, LOOP1, U)

        @block.tensor
        def _(pe):
            pe.wait_ge(w_in, 9 * 16)

            def body(k, u):
                a, b = (u + 1) % 2, u % 2
                if inside(k):
                    need(pe, qk_s, k + 1)
                for n in range(UNITS):
                    if inside(k):
                        if n >= 2 or not isinstance(k, int) or k > 0:
                            pe.wait_ge(score_s, k * UNITS + n - 1)
                        hs = slice(DH * n, DH * (n + 1))
                        for t in range(NT):
                            last = pe.matmul(psS[n % 2][:, t * COLS:(t + 1) * COLS], qT[b][hs, t * P:(t + 1) * P],
                                             kT[b][hs, :], start=True, stop=True)
                        last.then_inc(s_mm, 1)
                    if inside(k - 1):
                        if n == 0:
                            need(pe, prob_s, k, UNITS)
                        if n >= 2 or not isinstance(k, int) or k > 1:
                            pe.wait_ge(probT_s, (k - 1) * UNITS + n - 1)
                        for j in range(NT):
                            for t in range(NT):
                                last = pe.transpose(psT[n % 2][:, j * COLS + t * P:j * COLS + (t + 1) * P],
                                                    prob[a][:, t, n, j * P:(j + 1) * P], ident[:])
                        last.then_inc(tr_mm, 1)
                    if n == 1 and inside(k - 2):
                        need(pe, og_s, k - 1)
                        need(pe, wx_s, k - 2)
                        for j in range(NT):
                            last = pe.matmul(psM[:, j * P:(j + 1) * P], og[b][:, j * P:(j + 1) * P], wo_s[:],
                                             start=True, stop=True)
                        last.then_inc(out_mm, 1)
                if inside(k + 1):
                    q = (u + 1) % 4
                    pe.wait_ge(z_in[q], (k + 1 - q) * 4 + 16)
                    need(pe, qk_s, k + 1)
                    pe.matmul(psQK[:, 0:COLS], w_s[:, 0, :], zT[q][:], start=True, stop=True)
                    pe.matmul(psQK[:, COLS:2 * COLS], w_s[:, 1, :], zT[q][:], start=True, stop=True).then_inc(qk_mm, 1)
                if inside(k):
                    need(pe, vg_s, k)
                    for j in range(NT):
                        pe.matmul(psVG[:, j * P:(j + 1) * P], zT[u % 4][:, j * P:(j + 1) * P], w_s[:, 2, :],
                                  start=True, stop=True)
                    pe.matmul(psVG[:, COLS:2 * COLS], w_s[:, 3, :], zT[u % 4][:], start=True, stop=True).then_inc(vg_mm, 1)
                if inside(k - 1):
                    need(pe, probT_s, k, UNITS)
                    need(pe, og_s, k - 1)
                    for j in range(NT):
                        for h in range(HEADS):
                            hs = slice(DH * h, DH * (h + 1))
                            last = pe.matmul(psO[hs, 0:COLS], vv[a][:, j, hs], probT[a][:, h, j, :],
                                             start=j == 0, stop=j == NT - 1)
                    last.then_inc(pv_mm, 1)
                if inside(k - 2):
                    need(pe, yh_s, k - 1)
                    for j in range(NT):
                        last = pe.transpose(psM[:, j * P:(j + 1) * P], yh[b][:, j, :], ident[:])
                    last.then_inc(yT_mm, 1)
                if inside(k - 1):
                    need(pe, spread_s, k)
                    for t in range(NT):
                        last = pe.transpose(psO[:, COLS + t * P:COLS + (t + 1) * P], spread[a][:, t, :], ident[:])
                    last.then_inc(rt_mm, 1)
                if inside(k - 2):
                    need(pe, yT_s, k - 1)
                    pe.matmul(psM[:, COLS:2 * COLS], wt_s[:], yT[b][:], start=True, stop=True).then_inc(wx_mm, 1)

            pipeline(pe, body, FIRST, LAST, LOOP0, LOOP1, U)


def recurrence_pass(nc, io, t1_d, wx_d, t2_d, bn_sb):
    ctx = ExitStack()
    with ctx:
        def sb(name, shape, dt=F32):
            return ctx.enter_context(nc.sbuf_tensor(name, shape, dt))

        def ps(name, shape):
            return ctx.enter_context(nc.psum_tensor(name, shape, F32))

        def sem(name):
            return ctx.enter_context(nc.semaphore(name))

        vt_s = sb("vt_s", [P, P])
        ident = sb("ident_r", [P, P])
        gb = sb("gb", [P, 2])
        mhalf = sb("mhalf_r", [P, 1])
        var_e = sb("var_e", [P, 1])
        rstd = sb("rstd", [P, 1])
        am = sb("am", [P, 1])
        bn_a = sb("bn_a", [P, 1])
        bn_b = sb("bn_b", [P, 1])
        wxb = [sb(f"wxb{i}", [P, WARM + BATCH * SEG]) for i in range(2)]
        y = [sb(f"y{g}", [P, BLK, P]) for g in range(G)]
        pre = [sb(f"pre{g}", [P, 2, P]) for g in range(G)]
        t1b = [[sb(f"t1b{g}{i}", [P, BLK, P]) for i in range(2)] for g in range(G)]
        warm_mask = sb("warm_mask", [P, LANES])
        end_mask = sb("end_mask", [P, 1])
        starts = sb("starts", [P, LANES])
        ends = sb("ends", [P, 1 + LANES])
        guess = [sb(f"guess{g}", [P, P]) for g in range(G)]
        off = sb("off", [P, LANES])
        off2 = sb("off2", [P, LANES])
        off_max = sb("off_max", [P, 1])
        off_bad = sb("off_bad", [P, 1])
        ones = sb("ones_r", [P, 1])
        again = sb("again", [1, 1], I32)

        psY = [ps(f"psY{g}", [P, 512]) for g in range(G)]
        psT = [[ps(f"psT{g}{i}", [P, 4, P]) for i in range(2)] for g in range(G)]
        psF = ps("psF", [P, 512])

        c_in, c_ready, bn_c, bn_p = sem("c_in"), sem("c_ready"), sem("bn_c"), sem("bn_p")
        wx_in = [sem(f"wx_in{i}") for i in range(2)]
        wx_free = sem("wx_free")
        mm = [sem(f"mm{g}") for g in range(G)]
        pre_s = [sem(f"pre_s{g}") for g in range(G)]
        y_s = [sem(f"y_s{g}") for g in range(G)]
        guess_s = [sem(f"guess_s{g}") for g in range(G)]
        start_s = [sem(f"start_s{g}") for g in range(G)]
        begin_s = [sem(f"begin_s{g}") for g in range(G)]
        end_s = sem("end_s")
        tr = [sem(f"tr{g}") for g in range(G)]
        t2_s = [sem(f"t2_s{g}") for g in range(G)]
        t1_in = [[sem(f"t1_in{g}{i}") for i in range(2)] for g in range(G)]
        t2_out = [[sem(f"t2_out{g}{i}") for i in range(2)] for g in range(G)]
        off_s, bad_s, sum_mm, again_s, seen = sem("off_s"), sem("bad_s"), sem("sum_mm"), sem("again_s"), sem("seen")
        passed_r = {e: sem("passed_" + e + "2") for e in ("sp", "act", "pe", "dve")}
        CREDIT_OUT, CREDIT_T2 = 16, 2

        t1_v = t1_d.rearrange("(b g p k s) c -> b g k p s c", g=G, p=P, k=NBLK, s=BLK)
        t2_v = t2_d.rearrange("(b g p k s) c -> b g k p s c", g=G, p=P, k=NBLK, s=BLK)
        block = ctx.enter_context(nc.Block())

        def passes(engine, one_pass, passed):
            with engine.register("n_pass") as n_pass, engine.register("go_on") as go_on:
                engine.reg_mov(n_pass, 0)
                engine.reg_mov(go_on, 1)
                with engine.While(lambda: go_on):
                    n = engine.snap(n_pass)
                    one_pass(n)
                    engine.wait_ge(again_s, n + 1)
                    settle(engine, passed)
                    engine.reg_load(go_on, again[0:1, 0:1])
                    engine.drain().then_inc(seen, 1)
                    engine.reg_add(n_pass, n_pass, 1)

        @block.sync
        def _(sp):
            for dst, src in ((vt_s[:], io["VT"]), (ident[:], io["ident"]), (gb[:], io["bn_cols"])):
                sp.dma_start(dst, src).then_inc(c_in, 16)
            for g in range(G):
                for i in range(2):
                    sp.nop().then_inc(t2_out[g][i], CREDIT_OUT)

            def one_pass(n):
                def load_t1(b, k, g):
                    sp.wait_ge(t2_out[g][k % 2], (n * NB + b) * (8 * NBLK) + (k // 2) * 16 + CREDIT_OUT)
                    sp.dma_start(t1b[g][k % 2][:], t1_v[b, g, k]).then_inc(t1_in[g][k % 2], 16)

                with sp.Fori(0, NB // 2) as pair:
                    for i in range(2):
                        b = pair * 2 + i
                        sp.wait_ge(wx_free, n * NB + b + 1)
                        sp.dma_start(wxb[i][:], wx_d[:, bass.ds(b * (BATCH * SEG), WARM + BATCH * SEG)]
                                     ).then_inc(wx_in[i], 16)
                        for k in range(2):
                            for g in range(G):
                                load_t1(b, k, g)
                        for k in range(NBLK):
                            for g in range(G):
                                sp.wait_ge(t2_s[g], ((n * NB + b) * NBLK + (k + 1)) * 4 + CREDIT_T2)
                                sp.dma_start(t2_v[b, g, k], t1b[g][k % 2][:]).then_inc(t2_out[g][k % 2], 16)
                            if k + 2 < NBLK:
                                for g in range(G):
                                    load_t1(b, k + 2, g)
                for g in range(G):
                    for i in range(2):
                        sp.wait_ge(t2_out[g][i], (n + 1) * (NB * NBLK * 8) + CREDIT_OUT)

            passes(sp, one_pass, passed_r["sp"])

        @block.gpsimd
        def _(pool):
            pool.memset(mhalf[:], -0.5).then_inc(bn_p, 1)
            pool.tensor_scalar(var_e[:], bn_sb[:, 1:2], 1.0, EPS_BN, ALU.mult, ALU.add).then_inc(bn_p, 1)
            pool.wait_ge(bn_p, 2)
            pool.tensor_tensor(rstd[:], var_e[:], mhalf[:], ALU.pow).then_inc(bn_p, 1)

        @block.vector
        def _(dve):
            dve.nop().then_inc(wx_free, 2)
            for g in range(G):
                dve.nop().then_inc(t2_s[g], CREDIT_T2)
            dve.memset(ones[:], 1.0)
            dve.memset(warm_mask[:], 1.0).then_inc(bn_c, 1)
            dve.memset(end_mask[:], 0.0)
            dve.memset(ends[:], 0.0).then_inc(bn_c, 1)
            dve.wait_ge(bn_c, 1)
            dve.memset(warm_mask[:, 0:1], 0.0)
            for g in range(G):
                last = dve.memset(y[g][:, BLK - 1, :], 0.0)
            last.then_inc(bn_c, 1)
            dve.wait_ge(c_in, 48)
            dve.wait_ge(bn_p, 3)
            dve.tensor_tensor(bn_a[:], gb[:, 0:1], rstd[:], ALU.mult).then_inc(bn_c, 1)
            dve.wait_ge(bn_c, 4)
            dve.tensor_tensor(am[:], bn_a[:], bn_sb[:, 0:1], ALU.mult).then_inc(bn_c, 1)
            dve.wait_ge(bn_c, 5)
            dve.tensor_tensor(bn_b[:], gb[:, 1:2], am[:], ALU.subtract).then_inc(c_ready, 1)
            dve.wait_ge(c_ready, 1)

            def one_pass(n):
                with dve.Fori(0, NB // 2) as pair:
                    for i in range(2):
                        b = pair * 2 + i
                        nb = n * NB + b
                        base = nb * STEPS
                        wv = wxb[i][:]
                        dve.wait_ge(wx_in[i], n * (NB // 2 * 16) + pair * 16 + 16)

                        def step(s, j, g, now):
                            dve.wait_ge(mm[g], base + now + 1)
                            dve.scalar_tensor_tensor(
                                pre[g][:, j % 2, :],
                                wv[:, bass.ds(s + g * P * SEG, P, SEG)] if not isinstance(s, int)
                                else wv[:, s + g * P * SEG:s + g * P * SEG + (P - 1) * SEG + 1:SEG],
                                bn_a[:, 0:1], psY[g][:, 0:P], ALU.mult, ALU.add).then_inc(pre_s[g], 1)

                        for j in range(WARM):
                            for g in range(G):
                                step(j, j, g, j)
                        for g in range(G):
                            lanes = bass.ds(b * BATCH + g * P, P)
                            dve.wait_ge(y_s[g], base + WARM)
                            dve.tensor_tensor(guess[g][:], y[g][:, BLK - 1, :], warm_mask[:, lanes],
                                              ALU.mult).then_inc(guess_s[g], 1)
                        for g in range(G):
                            lanes = bass.ds(b * BATCH + g * P, P)
                            dve.wait_ge(guess_s[g], nb + 1)
                            dve.scalar_tensor_tensor(starts[:, lanes], ends[:, lanes], end_mask[:, 0:1], guess[g][:],
                                                     ALU.mult, ALU.add).then_inc(start_s[g], 1)
                        for g in range(G):
                            lanes = bass.ds(b * BATCH + g * P, P)
                            dve.wait_ge(start_s[g], nb + 1)
                            dve.tensor_scalar(y[g][:, BLK - 1, :], starts[:, lanes], 1.0, None,
                                              ALU.mult).then_inc(begin_s[g], 1)
                        with dve.Fori(0, NBLK // 2) as k2:
                            for ki in range(2):
                                k = k2 * 2 + ki
                                for g in range(G):
                                    dve.wait_ge(t1_in[g][ki], nb * (8 * NBLK) + k2 * 16 + 16)
                                for j in range(BLK):
                                    for g in range(G):
                                        step(k * BLK + (WARM + j), j, g, k * BLK + (WARM + j))
                                    if j % 4 == 1 and j > 4:
                                        add_states(nb, k, ki, (j - 5) // 4)
                                add_states(nb, k, ki, 3)
                        for g in range(G):
                            dve.wait_ge(y_s[g], base + STEPS)
                            last = dve.tensor_scalar(ends[:, bass.ds(b * BATCH + g * P + 1, P)], y[g][:, BLK - 1, :], 1.0,
                                                     None, ALU.mult)
                        last.then_inc(wx_free, 1)
                dve.wait_ge(wx_free, (n + 1) * NB + 2)
                dve.tensor_tensor(off[:], starts[:], ends[:, 0:LANES], ALU.subtract).then_inc(off_s, 1)
                dve.wait_ge(off_s, n * 3 + 1)
                dve.tensor_tensor(off2[:], off[:], off[:], ALU.mult).then_inc(off_s, 1)
                dve.wait_ge(off_s, n * 3 + 2)
                dve.tensor_reduce(off_max[:], off2[:], AX.X, ALU.max).then_inc(off_s, 1)
                dve.wait_ge(off_s, n * 3 + 3)
                dve.tensor_scalar(off_bad[:], off_max[:], TOL * TOL, None, ALU.is_gt).then_inc(bad_s, 1)
                dve.memset(warm_mask[:], 0.0)
                dve.memset(end_mask[:], 1.0)
                dve.wait_ge(sum_mm, n + 1)
                dve.tensor_copy(again[0:1, 0:1], psF[0:1, 0:1]).then_inc(again_s, 1)
                dve.wait_ge(seen, n * 4 + 3)

            def add_states(nb, k, ki, quad):
                for g in range(G):
                    dve.wait_ge(tr[g], (nb * NBLK + k) * 4 + quad + 1)
                    part = t1b[g][ki][:, 4 * quad:4 * quad + 4, :]
                    dve.tensor_tensor(part, psT[g][quad % 2][:], part, ALU.add).then_inc(t2_s[g], 1)

            passes(dve, one_pass, passed_r["dve"])

        @block.scalar
        def _(act):
            act.wait_ge(c_ready, 1)

            def one_pass(n):
                with act.Fori(0, NB) as b:
                    base = (n * NB + b) * STEPS
                    with act.Fori(0, STEPS, BLK) as s0:
                        for j in range(BLK):
                            for g in range(G):
                                act.wait_ge(pre_s[g], base + s0 + (j + 1))
                                act.activation(y[g][:, j, :], pre[g][:, j % 2, :], ACT.Sigmoid,
                                               bias=bn_b[:, 0:1]).then_inc(y_s[g], 1)

            passes(act, one_pass, passed_r["act"])

        @block.tensor
        def _(pe):
            pe.wait_ge(c_in, 48)
            pe.wait_ge(bn_c, 3)

            def one_pass(n):
                with pe.Fori(0, NB) as b:
                    nb = n * NB + b
                    base = nb * STEPS

                    def step(j, g):
                        pe.matmul(psY[g][:, 0:P], vt_s[:], y[g][:, (j - 1) % BLK, :], start=True,
                                  stop=True).then_inc(mm[g], 1)

                    def transposes(k, quad):
                        for g in range(G):
                            pe.wait_ge(t2_s[g], (nb * NBLK + k) * 4 + quad + 1)
                            for q in range(4):
                                last = pe.transpose(psT[g][quad % 2][:, q, :], y[g][:, 4 * quad + q, :], ident[:])
                            last.then_inc(tr[g], 1)

                    pe.wait_ge(wx_free, nb + 2)
                    for j in range(WARM):
                        for g in range(G):
                            if j:
                                pe.wait_ge(y_s[g], base + j)
                            step(j, g)
                    with pe.Fori(0, NBLK) as k:
                        for j in range(BLK):
                            for g in range(G):
                                if j == 0:
                                    pe.wait_ge(begin_s[g], nb + 1)
                                pe.wait_ge(y_s[g], base + k * BLK + (WARM + j))
                                step(j, g)
                            if j % 4 == 0 and j:
                                transposes(k, j // 4 - 1)
                        for g in range(G):
                            pe.wait_ge(y_s[g], base + k * BLK + (WARM + BLK))
                        transposes(k, 3)
                pe.wait_ge(bad_s, n + 1)
                pe.matmul(psF[0:1, 0:1], off_bad[:], ones[:], start=True, stop=True).then_inc(sum_mm, 1)

            passes(pe, one_pass, passed_r["pe"])


HALVES = 2
WID = 4
TILES = HALVES * WID
NM = ROWS // WID
FOLDED = 4
ROUTE, GAP = 15, 8
FX = 16


def mixer_pass(nc, io, t2_d, out_d):
    ctx = ExitStack()
    with ctx:
        def sb(name, shape, dt=F32):
            return ctx.enter_context(nc.sbuf_tensor(name, shape, dt))

        def ps(name, shape):
            return ctx.enter_context(nc.psum_tensor(name, shape, F32))

        def sem(name):
            return ctx.enter_context(nc.semaphore(name))

        ident = sb("ident_m", [P, P])
        ln_w, ln_b, be = sb("ln_w", [P, P]), sb("ln_b", [P, P]), sb("be", [P, P])
        w1 = sb("w1", [P, 2, COLS])
        w2 = sb("w2", [P, 2, COLS])
        w3t = sb("w3t", [P, 2, COLS])
        b12 = sb("b12", [P, 4])
        b12w = sb("b12w", [P, 4, P])
        b3 = sb("b3", [P, COLS])
        w32 = sb("w32", [P, 2, COLS])
        mix = sb("mix", [P, 2, COLS])
        mix_b = sb("mix_b", [P, COLS])
        out_b = sb("out_b", [P, HALVES, P])
        wet = sb("wet", [P, P])
        rw, rb, dec = sb("rw", [P, EXPERTS]), sb("rb", [P, EXPERTS]), sb("dec", [P, EXPERTS])
        rwh, rwl = sb("rwh", [P, EXPERTS], F32R), sb("rwl", [P, EXPERTS], F32R)
        ew = sb("ew", [P, EXPERTS * P])
        ewh, ewl = sb("ewh", [P, EXPERTS * P], F32R), sb("ewl", [P, EXPERTS * P], F32R)
        eb = sb("eb", [TILES * EXPERTS, TILES * P])
        mhalf, minus = sb("mhalf_m", [P, TILES]), sb("minus_m", [P, TILES])

        t2 = [sb(f"t2_{u}", [P, TILES, P]) for u in range(4)]
        t2e = [sb(f"t2e{u}", [P, TILES, P]) for u in range(2)]
        statc = sb("statc", [P, TILES, 6])
        mvc = sb("mvc", [P, TILES, 2])
        vc, nmc = sb("vc", [P, TILES]), sb("nmc", [P, TILES])
        rsc = [sb(f"rsc{u}", [P, TILES]) for u in range(2)]
        bsc = [sb(f"bsc{u}", [P, TILES]) for u in range(2)]
        xc = sb("xc", [P, TILES, P])
        xw = sb("xw", [P, TILES, P])
        xb = sb("xb", [P, TILES, P])
        ug = [sb(f"ug{u}", [P, TILES, P]) for u in range(2)]
        mT = [sb(f"mT{u}", [P, WID, COLS]) for u in range(2)]
        t3 = [sb(f"t3_{u}", [P, TILES, P]) for u in range(2)]
        state = sb("state", [P, TILES, 6])
        mve = sb("mve", [P, TILES, 2])
        ve, nme = sb("ve", [P, TILES]), sb("nme", [P, TILES])
        rse = [sb(f"rse{u}", [P, TILES]) for u in range(2)]
        bse = [sb(f"bse{u}", [P, TILES]) for u in range(2)]
        xe = [sb(f"xe{u}", [P, TILES, P]) for u in range(2)]
        xh = [sb(f"xh_m{u}", [P, TILES, P], F32R) for u in range(4)]
        xl = [sb(f"xl_m{u}", [P, TILES, P], F32R) for u in range(4)]
        logit = sb("logit", [P, TILES, EXPERTS])
        logit2 = sb("logit2", [P, TILES, EXPERTS])
        is_max = sb("is_max", [P, TILES, EXPERTS])
        order = sb("order", [P, TILES, EXPERTS])
        pick = [sb(f"pick{i}", [P, TILES, EXPERTS]) for i in range(2)]
        share = [sb(f"share{i}", [P, TILES, EXPERTS]) for i in range(2)]
        top = [sb(f"top{i}", [P, TILES]) for i in range(2)]
        first = sb("first", [P, TILES])
        gap = sb("gap", [P, TILES])
        th = sb("th_m", [P, TILES])
        wgt = [sb(f"wgt{i}", [P, TILES]) for i in range(2)]
        gate = [sb(f"gate{u}", [P, TILES, EXPERTS]) for u in range(2)]
        gateT = [sb(f"gateT{u}", [TILES * EXPERTS, P]) for u in range(2)]
        acc = [sb(f"acc{u}", [P, TILES, P]) for u in range(2)]

        psC = ps("psC", [P, 2, 512])
        psD = ps("psD", [P, 2, 512])
        psE = [ps(f"psE{i}", [P, 2, 512]) for i in range(2)]

        w_in, fold, fold_v, ready = sem("w_in3"), sem("fold3"), sem("fold_v3"), sem("ready3")
        t2_in = [sem(f"t2_in{u}") for u in range(4)]
        statc_s, mvc_s, nmc_s, vc_s, rsc_s, bsc_s, t2e_s, xc_s, xw_s, xb_s, ug_s = (
            sem(n) for n in ("statc_s", "mvc_s", "nmc_s", "vc_s", "rsc_s", "bsc_s", "t2e_s", "xc_s", "xw_s", "xb_s",
                             "ug_s"))
        mix_mm, mT_s, we_mm, t3_s = sem("mix_mm"), sem("mT_s"), sem("we_mm"), sem("t3_s")
        state_s, mve_s, nme_s, ve_s, rse_s, bse_s, xe_s, xeT_mm, xh_s, xl_s = (
            sem(n) for n in ("state_s", "mve_s", "nme_s", "ve_s", "rse_s", "bse_s", "xe_s", "xeT_mm", "xh_sm", "xl_s"))
        route_mm, logit_s, route_s, th_s, gateT_mm, gateT_s, eb_mm, acc_s = (
            sem(n) for n in ("route_mm", "logit_s", "route_s", "th_s", "gateT_mm", "gateT_s", "eb_mm", "acc_s"))
        ex_mm, ex_s = sem("ex_mm"), sem("ex_s")
        out_s = [sem(f"out_s{u}") for u in range(2)]
        passed_pool, passed_dve, passed_pe = sem("passed_pool3"), sem("passed_dve3"), sem("passed_pe3")

        def view(d):
            return d.rearrange("(h g n v) c -> h g n v c", h=HALVES, g=8, v=FX)

        t2_v, out_v = view(t2_d), view(out_d)
        FIRST, LAST, LOOP0, LOOP1, U = -3, NM, 4, 60, 4
        PAIRS = TILES // 2
        flat = "p t c -> p (t c)"

        def place(v, m, q, h):
            n = m * 4 - q * 4
            s = slice(n, n + FX) if isinstance(n, int) else bass.ds(n, FX)
            return v[h, :, s, q * WID:(q + 1) * WID, :]

        def upto(engine, s, n, per=1):
            need(engine, s, min(n, NM) if isinstance(n, int) else n, per)

        block = ctx.enter_context(nc.Block())

        @block.sync
        def _(sp):
            loads = [(ident[:], io["ident"]), (ln_w[:], io["ln_w"]), (ln_b[:], io["ln_b"]), (be[:], io["be"]),
                     (w1[:], io["W1"].rearrange("(t p) g -> p t g", t=2)),
                     (w2[:], io["W2e"].rearrange("(t p) g -> p t g", t=2)),
                     (w3t[:], io["W3eT"].rearrange("(t p) g -> p t g", t=2)),
                     (b12[:], io["b12"]), (b3[:], io["b3"]), (wet[:], io["WeT"]), (rw[:], io["rw"]),
                     (rb[:], io["rb"]), (dec[:], io["dec"]), (ew[:], io["ew"]), (eb[:], io["eb"])]
            for dst, src in loads:
                sp.dma_start(dst, src).then_inc(w_in, 16)

            def body(m, u):
                if inside(m + 4, NM):
                    upto(sp, xc_s, m + 1)
                    upto(sp, t2e_s, m + 1)
                    for h in range(HALVES):
                        sp.dma_start(t2[u][:, h * WID:(h + 1) * WID, :], place(t2_v, m + 4, u, h)
                                     ).then_inc(t2_in[u], 16)
                if inside(m - 1, NM):
                    q = (u - 1) % 4
                    upto(sp, ex_s, m, TILES * EXPERTS)
                    for h in range(HALVES):
                        sp.dma_start(place(out_v, m - 1, q, h), acc[q % 2][:, h * WID:(h + 1) * WID, :]
                                     ).then_inc(out_s[q % 2], 16)

            pipeline(sp, body, FIRST - 1, LAST + 1, LOOP0, LOOP1, U)
            for u in range(2):
                sp.wait_ge(out_s[u], 32 * NM // 2)

        @block.gpsimd
        def _(pool):
            pool.memset(mhalf[:], -0.5).then_inc(ready, 1)
            pool.memset(minus[:], -1.0).then_inc(ready, 1)
            pool.wait_ge(ready, 2)
            pool.wait_ge(fold_v, FOLDED)

            def factors(n, mv, mv_s, mul, add, nm, nm_s, v, v_s, rs, rs_s, bs, bs_s, used_s):
                upto(pool, mv_s, n + 1)
                upto(pool, bs_s, n)
                pool.tensor_tensor(nm[:], mv[:, :, 0], minus[:], ALU.mult).then_inc(nm_s, 1)
                upto(pool, rs_s, n)
                settle(pool, passed_pool)
                pool.tensor_scalar(v[:], mv[:, :, 1], mul, add, ALU.mult, ALU.add).then_inc(v_s, 1)
                upto(pool, v_s, n + 1)
                upto(pool, used_s, n - 1)
                pool.tensor_tensor(rs[:], v[:], mhalf[:], ALU.pow).then_inc(rs_s, 1)
                upto(pool, rs_s, n + 1)
                upto(pool, nm_s, n + 1)
                pool.tensor_tensor(bs[:], nm[:], rs[:], ALU.mult).then_inc(bs_s, 1)

            def body(m, u):
                a, b = (u + 1) % 2, u % 2
                if inside(m + 3, NM):
                    factors(m + 3, mvc, mvc_s, TWICE_MUL, TWICE_ADD, nmc, nmc_s, vc, vc_s, rsc[a], rsc_s, bsc[a],
                            bsc_s, xc_s)
                if inside(m + 2, NM):
                    factors(m + 2, mve, mve_s, 1.0, EPS_LN, nme, nme_s, ve, ve_s, rse[b], rse_s, bse[b], bse_s, xe_s)
                if inside(m + 3, NM):
                    upto(pool, xw_s, m + 4)
                    upto(pool, ug_s, m + 3)
                    pool.tensor_tensor(xb[:], xw[:], ln_b[:].unsqueeze(1).to_broadcast([P, TILES, P]),
                                       ALU.add).then_inc(xb_s, 1)
                    upto(pool, t3_s, m + 2)
                    for h in range(HALVES):
                        hs = slice(h * WID, (h + 1) * WID)
                        last = pool.tensor_tensor(t2e[a][:, hs, :], t2[(u + 3) % 4][:, hs, :],
                                                  out_b[:, h, :].unsqueeze(1).to_broadcast([P, WID, P]), ALU.add)
                    last.then_inc(t2e_s, 1)

            pipeline(pool, body, FIRST, LAST, LOOP0, LOOP1, U)

        @block.vector
        def _(dve):
            dve.wait_ge(w_in, 15 * 16)
            for i in range(4):
                dve.tensor_copy(b12w[:, i, :], b12[:, i:i + 1].to_broadcast([P, P]))
            dve.tensor_copy(rwh[:], rw[:])
            dve.tensor_copy(ewh[:], ew[:]).then_inc(fold_v, 1)
            dve.wait_ge(fold_v, 1)
            dve.tensor_tensor(rwl[:], rw[:], rwh[:].bitcast(F32), ALU.subtract)
            dve.tensor_tensor(ewl[:], ew[:], ewh[:].bitcast(F32), ALU.subtract)
            dve.wait_ge(fold, 1)
            dve.tensor_copy(w32[:].rearrange("p t g -> p (t g)"), psC[:, 0, :]).then_inc(fold_v, 1)
            dve.wait_ge(fold, 2)
            dve.tensor_copy(mix[:].rearrange("p t g -> p (t g)"), psD[:, 0, :])
            dve.tensor_tensor(mix_b[:], psD[:, 1, 0:COLS], b3[:], ALU.add).then_inc(fold_v, 1)
            dve.wait_ge(fold, 3)
            dve.tensor_tensor(out_b[:], psC[:, 0, 0:COLS].rearrange("p (h c) -> p h c", h=HALVES),
                              be[:].unsqueeze(1).to_broadcast([P, HALVES, P]), ALU.add).then_inc(fold_v, 1)
            dve.wait_ge(fold_v, FOLDED)

            def route(m, a, n):
                wide = [P, TILES, EXPERTS]
                over = lambda v: v[:].unsqueeze(2).to_broadcast(wide)
                if n:
                    dve.wait_ge(route_s, m * ROUTE + n)
                if n in (0, 6):
                    i = n // 6
                    if n == 0:
                        upto(dve, logit_s, m + 1)
                    ins = dve.tensor_reduce(top[i][:], (logit2 if i else logit)[:], AX.X, ALU.max)
                elif n in (1, 8):
                    i = n // 8
                    ins = dve.tensor_tensor(is_max[:], (logit2 if i else logit)[:], over(top[i]), ALU.is_equal)
                elif n in (2, 9):
                    ins = dve.tensor_tensor(order[:], is_max[:], dec[:].unsqueeze(1).to_broadcast(wide), ALU.mult)
                elif n in (3, 10):
                    ins = dve.tensor_reduce(first[:], order[:], AX.X, ALU.max)
                elif n in (4, 11):
                    ins = dve.tensor_tensor(pick[n // 11][:], order[:], over(first), ALU.is_equal)
                elif n == 5:
                    ins = dve.scalar_tensor_tensor(logit2[:], pick[0][:], -3e38, logit[:], ALU.mult, ALU.add)
                elif n == GAP - 1:
                    upto(dve, th_s, m)
                    ins = dve.tensor_tensor(gap[:], top[0][:], top[1][:], ALU.subtract)
                elif n == 12:
                    upto(dve, th_s, m + 1)
                    for i, sign in ((0, 0.5), (1, -0.5)):
                        ins = dve.tensor_scalar(wgt[i][:], th[:], sign, 0.5, ALU.mult, ALU.add)
                elif n == 13:
                    for i in range(2):
                        ins = dve.tensor_tensor(share[i][:], pick[i][:], over(wgt[i]), ALU.mult)
                else:
                    upto(dve, gateT_mm, m - 1)
                    ins = dve.tensor_tensor(gate[a][:], share[0][:], share[1][:], ALU.add)
                ins.then_inc(route_s, 1)

            def body(m, u):
                a, b = (u + 1) % 2, u % 2
                for p in range(PAIRS):
                    routes = p == 2 and inside(m + 1, NM)
                    if routes and not inside(m, NM):
                        for n in range(ROUTE):
                            route(m + 1, a, n)
                    if inside(m, NM):
                        for e in range(EXPERTS):
                            for i in range(2):
                                t = 2 * p + i
                                if routes and 2 * e + i < ROUTE:
                                    route(m + 1, a, 2 * e + i)
                                if e % 4 == 0:
                                    dve.wait_ge(ex_mm, (m * PAIRS + p) * 4 + (2 if e else 0) + i + 1)
                                if p == 0 and e == 0 and i == 0:
                                    upto(dve, acc_s, m + 1)
                                    upto(dve, route_s, m + 1, ROUTE)
                                if e:
                                    dve.wait_ge(ex_s, (m * PAIRS + p) * 2 * EXPERTS + 2 * (e - 1) + i + 1)
                                dve.scalar_tensor_tensor(
                                    acc[b][:, t, :], psE[i][:, e // 4, (e % 4) * P:(e % 4 + 1) * P],
                                    gate[b][:, t, e:e + 1], acc[b][:, t, :], ALU.mult, ALU.add).then_inc(ex_s, 1)
                    if p == 0 and inside(m + 3, NM):
                        q = (u + 3) % 4
                        dve.wait_ge(t2_in[q], (m + 3 - q) * 8 + 32)
                        upto(dve, mvc_s, m + 3)
                        for t in range(TILES):
                            last = dve.bn_stats(statc[:, t, :], t2[q][:, t, :])
                        last.then_inc(statc_s, 1)
                        upto(dve, statc_s, m + 4)
                        upto(dve, vc_s, m + 3)
                        upto(dve, nmc_s, m + 3)
                        settle(dve, passed_dve)
                        for t in range(TILES):
                            last = dve.bn_aggr(mvc[:, t, :], statc[:, t, :])
                        last.then_inc(mvc_s, 1)
                    if p == 0 and inside(m + 1, NM):
                        upto(dve, xh_s, m + 2)
                        dve.tensor_tensor(xl[(u + 1) % 4][:].rearrange(flat), psC[:].rearrange("p k n -> p (k n)"),
                                          xh[(u + 1) % 4][:].bitcast(F32).rearrange(flat), ALU.subtract).then_inc(xl_s, 1)
                    if p == 1 and inside(m + 1, NM):
                        upto(dve, route_mm, m + 2)
                        dve.tensor_tensor(logit[:], psD[:, 0, 0:TILES * EXPERTS].rearrange("p (t e) -> p t e", t=TILES),
                                          rb[:].unsqueeze(1).to_broadcast([P, TILES, EXPERTS]), ALU.add).then_inc(logit_s, 1)
                    if p == 1 and inside(m + 2, NM):
                        upto(dve, we_mm, m + 3)
                        upto(dve, t2e_s, m + 3)
                        dve.tensor_tensor(t3[b][:].rearrange(flat), psD[:].rearrange("p k n -> p (k n)"),
                                          t2e[b][:].rearrange(flat), ALU.add).then_inc(t3_s, 1)
                        upto(dve, t3_s, m + 3)
                        upto(dve, mve_s, m + 2)
                        for t in range(TILES):
                            last = dve.bn_stats(state[:, t, :], t3[b][:, t, :])
                        last.then_inc(state_s, 1)
                        upto(dve, state_s, m + 3)
                        upto(dve, ve_s, m + 2)
                        upto(dve, nme_s, m + 2)
                        settle(dve, passed_dve)
                        for t in range(TILES):
                            last = dve.bn_aggr(mve[:, t, :], state[:, t, :])
                        last.then_inc(mve_s, 1)
                    if p == 2 and inside(m + 3, NM):
                        upto(dve, xc_s, m + 4)
                        upto(dve, xb_s, m + 3)
                        dve.tensor_tensor(xw[:], xc[:], ln_w[:].unsqueeze(1).to_broadcast([P, TILES, P]),
                                          ALU.mult).then_inc(xw_s, 1)
                    if p == 3 and inside(m + 1, NM):
                        upto(dve, eb_mm, m + 2)
                        need(dve, out_s[a], m + 1 - a, 16)
                        dve.tensor_tensor(acc[a][:].rearrange(flat), psD[:].rearrange("p k n -> p (k n)"),
                                          t3[a][:].rearrange(flat), ALU.add).then_inc(acc_s, 1)

            pipeline(dve, body, FIRST, LAST, LOOP0, LOOP1, U)

        @block.scalar
        def _(act):
            def body(m, u):
                a, b = (u + 1) % 2, u % 2
                if inside(m + 2, NM):
                    upto(act, mix_mm, m + 3)
                    upto(act, we_mm, m + 1)
                    for i in range(2):
                        last = act.activation(mT[b][:, 2 * i:2 * i + 2].rearrange("p w g -> p (w g)"), psC[:, i, :],
                                              ACT.Identity)
                    last.then_inc(mT_s, 1)
                if inside(m + 3, NM):
                    upto(act, bsc_s, m + 4)
                    upto(act, xw_s, m + 3)
                    for t in range(TILES):
                        last = act.activation(xc[:, t, :], t2[(u + 3) % 4][:, t, :], ACT.Identity,
                                              bias=bsc[a][:, t:t + 1], scale=rsc[a][:, t:t + 1])
                    last.then_inc(xc_s, 1)
                if inside(m + 2, NM):
                    upto(act, bse_s, m + 3)
                    upto(act, xeT_mm, m + 1)
                    for t in range(TILES):
                        last = act.activation(xe[b][:, t, :], t3[b][:, t, :], ACT.Identity,
                                              bias=bse[b][:, t:t + 1], scale=rse[b][:, t:t + 1])
                    last.then_inc(xe_s, 1)
                if inside(m + 1, NM):
                    act.wait_ge(route_s, (m + 1) * ROUTE + GAP)
                    act.activation(th[:], gap[:], ACT.Tanh, scale=0.5).then_inc(th_s, 1)
                if inside(m + 3, NM):
                    upto(act, xb_s, m + 4)
                    upto(act, mix_mm, m + 2)
                    act.activation(ug[a][:], xb[:], ACT.Gelu).then_inc(ug_s, 1)
                if inside(m + 1, NM):
                    upto(act, gateT_mm, m + 2)
                    upto(act, eb_mm, m)
                    act.activation(gateT[a][:], psD[0:TILES * EXPERTS, 0, 0:P], ACT.Identity).then_inc(gateT_s, 1)
                if inside(m + 2, NM):
                    upto(act, xeT_mm, m + 3)
                    upto(act, ex_mm, m - 1, 4 * PAIRS)
                    for i in range(2):
                        last = act.activation(xh[(u + 2) % 4][:, i * WID:(i + 1) * WID].rearrange(flat), psC[:, i, :],
                                              ACT.Identity)
                    last.then_inc(xh_s, 1)

            pipeline(act, body, FIRST, LAST, LOOP0, LOOP1, U)

        @block.tensor
        def _(pe):
            pe.wait_ge(w_in, 15 * 16)
            pe.wait_ge(fold_v, 1)
            for o in range(2):
                for t in range(2):
                    last = pe.matmul(psC[:, 0, o * COLS:(o + 1) * COLS], w2[:, t, o * P:(o + 1) * P], w3t[:, t, :],
                                     start=t == 0, stop=t == 1)
            last.then_inc(fold, 1)
            pe.wait_ge(fold_v, 2)
            for o in range(2):
                for t in range(2):
                    pe.matmul(psD[:, 0, o * COLS:(o + 1) * COLS], w1[:, t, o * P:(o + 1) * P], w32[:, t, :],
                              start=t == 0, stop=t == 1)
            for i in range(4):
                last = pe.matmul(psD[:, 1, 0:COLS], b12w[:, i, :], (w32 if i < 2 else w3t)[:, i % 2, :],
                                 start=i == 0, stop=i == 3)
            last.then_inc(fold, 1)
            pe.wait_ge(fold_v, 3)
            for h in range(HALVES):
                last = pe.matmul(psC[:, 0, h * P:(h + 1) * P], mix_b[:, h * P:(h + 1) * P], wet[:], start=True, stop=True)
            last.then_inc(fold, 1)
            pe.wait_ge(fold_v, FOLDED)

            def split3(out, x_h, x_l, w_h, w_l):
                pe.matmul(out, x_h, w_h, start=True, stop=False)
                pe.matmul(out, x_h, w_l, start=False, stop=False)
                return pe.matmul(out, x_l, w_h, start=False, stop=True)

            def body(m, u):
                a, b = (u + 1) % 2, u % 2
                for p in range(PAIRS):
                    if inside(m, NM):
                        for half in range(2):
                            for i in range(2):
                                t = 2 * p + i
                                if not (isinstance(m, int) and m == 0 and p == 0):
                                    pe.wait_ge(ex_s, ((m * PAIRS + p) - 1) * 2 * EXPERTS + 8 * half + 7 + i)
                                ws = slice(half * 512, (half + 1) * 512)
                                split3(psE[i][:, half, :], xh[u][:, t, :], xl[u][:, t, :], ewh[:, ws],
                                       ewl[:, ws]).then_inc(ex_mm, 1)
                    if p == 0 and inside(m + 2, NM):
                        upto(pe, ug_s, m + 3)
                        upto(pe, xl_s, m + 2)
                        for w in range(WID):
                            for h in range(HALVES):
                                last = pe.matmul(psC[:, w // 2, (w % 2) * COLS:(w % 2 + 1) * COLS],
                                                 ug[b][:, h * WID + w, :], mix[:, h, :], start=h == 0, stop=h == 1)
                        last.then_inc(mix_mm, 1)
                    if p == 1 and inside(m + 1, NM):
                        upto(pe, xl_s, m + 2)
                        upto(pe, acc_s, m + 1)
                        q = (u + 1) % 4
                        for t in range(TILES):
                            last = split3(psD[:, 0, t * EXPERTS:(t + 1) * EXPERTS], xh[q][:, t, :], xl[q][:, t, :],
                                          rwh[:], rwl[:])
                        last.then_inc(route_mm, 1)
                    if p == 1 and inside(m + 2, NM):
                        upto(pe, mT_s, m + 3)
                        upto(pe, logit_s, m + 2)
                        for h in range(HALVES):
                            for w in range(WID):
                                last = pe.matmul(psD[:, h, w * P:(w + 1) * P], mT[b][:, w, h * P:(h + 1) * P], wet[:],
                                                 start=True, stop=True)
                        last.then_inc(we_mm, 1)
                    if p == 3 and inside(m + 1, NM):
                        upto(pe, route_s, m + 2, ROUTE)
                        upto(pe, t3_s, m + 3)
                        settle(pe, passed_pe)
                        pe.transpose(psD[0:TILES * EXPERTS, 0, 0:P], gate[a][:].rearrange("p t e -> p (t e)"),
                                     ident[:]).then_inc(gateT_mm, 1)
                    if p == 3 and inside(m + 2, NM):
                        upto(pe, xe_s, m + 3)
                        upto(pe, mT_s, m + 3)
                        for t in range(TILES):
                            last = pe.transpose(psC[:, t // 4, (t % 4) * P:(t % 4 + 1) * P], xe[b][:, t, :], ident[:])
                        last.then_inc(xeT_mm, 1)
                    if p == 3 and inside(m + 1, NM):
                        upto(pe, gateT_s, m + 2)
                        for h in range(2):
                            last = pe.matmul(psD[:, h, :], gateT[a][:], eb[:, h * 512:(h + 1) * 512], start=True, stop=True)
                        last.then_inc(eb_mm, 1)

            pipeline(pe, body, FIRST, LAST, LOOP0, LOOP1, U)


def metaformer(nc, io, out_d):
    zt_d = nc.dram_tensor("zt_scratch", [P, TOK], F32, kind="Internal").ap()
    bias_d = nc.dram_tensor("bias_scratch", [ROWS, HEADS, COLS], F32, kind="Internal").ap()
    t1_d = nc.dram_tensor("t1_scratch", [TOK, P], F32, kind="Internal").ap()
    t2_d = nc.dram_tensor("t2_scratch", [TOK, P], F32, kind="Internal").ap()
    wx_d = nc.dram_tensor("wx_scratch", [P, WARM + TOK], F32, kind="Internal").ap()
    with nc.sbuf_tensor("bn_sb", [P, 2], F32) as bn_sb:
        norm_pass(nc, io, zt_d, bias_d)
        attention_pass(nc, io, zt_d, bias_d, t1_d, wx_d, bn_sb)
        recurrence_pass(nc, io, t1_d, wx_d, t2_d, bn_sb)
        mixer_pass(nc, io, t2_d, out_d)


def layouts(a):
    f = np.float32
    rows = lambda v: np.ascontiguousarray(np.broadcast_to(v, (P, v.shape[-1])))
    io = {"x": a["x"].reshape(TOK, P)}
    for n in ("Wq", "Wk", "Wv", "Wg", "Wo"):
        io[n] = a["L0_conv_" + n]
    io["WbPad"] = np.zeros((P, DH), f)
    io["WbPad"][:, :HEADS] = a["L0_conv_Wb"]
    io["ln_cols"] = np.stack([a["L0_conv_ln_scale"], a["L0_conv_ln_bias"]], axis=1)
    io["WT"], io["VT"] = a["L0_ffn_W"].T, a["L0_ffn_V"].T
    io["bn_cols"] = np.stack([a["L0_ffn_gamma"], a["L0_ffn_beta"]], axis=1)
    io["ln_w"], io["ln_b"], io["be"] = rows(a["L1_conv_ln_w"]), rows(a["L1_conv_ln_b"]), rows(a["L1_conv_be"])
    io["W1"] = a["L1_conv_W1"]
    w2 = np.zeros((8, 2, 8, 2, 8, 2, 8, 2), f)
    w3t = np.zeros((2, 8, 2, 8, 2, 8, 2, 8), f)
    for i in range(2):
        for j in range(2):
            w2[:, i, :, j, :, i, :, j] = a["L1_conv_W2"].reshape(8, 8, 8, 8)
    for i in range(8):
        for j in range(8):
            w3t[:, i, :, j, :, i, :, j] = a["L1_conv_W3"].T.reshape(2, 2, 2, 2)
    io["W2e"], io["W3eT"] = w2.reshape(COLS, COLS), w3t.reshape(COLS, COLS)
    b2 = np.broadcast_to(a["L1_conv_b2"].reshape(8, 1, 8, 1), (8, 2, 8, 2)).reshape(COLS)
    b3 = np.broadcast_to(a["L1_conv_b3"].reshape(2, 1, 2, 1), (2, 8, 2, 8)).reshape(COLS)
    io["b12"] = np.stack([a["L1_conv_b1"][:P], a["L1_conv_b1"][P:], b2[:P], b2[P:]], axis=1)
    io["b3"] = rows(b3)
    io["WeT"] = a["L1_conv_We"].T
    io["rw"], io["rb"] = a["L1_ffn_router_w"], rows(a["L1_ffn_router_b"])
    io["ew"] = a["L1_ffn_expert_w"].transpose(1, 0, 2).reshape(P, EXPERTS * P)
    eb = np.zeros((TILES, EXPERTS, TILES, P), f)
    for t in range(TILES):
        eb[t, :, t, :] = a["L1_ffn_expert_b"]
    io["eb"] = eb.reshape(TILES * EXPERTS, TILES * P)
    io["ident"] = np.eye(P, dtype=f)
    io["dec"] = rows(np.arange(EXPERTS, 0, -1).astype(f))
    return {n: np.ascontiguousarray(v) for n, v in io.items()}


def kernel(**inputs):
    import concourse.bacc as bacc
    from concourse.bass_utils import run_bass_kernel_spmd

    arrays = layouts({n: np.asarray(v) for n, v in inputs.items()})
    nc = bacc.Bacc("TRN2", target_bir_lowering=False, num_devices=1)
    io = {n: nc.dram_tensor("in_" + n, v.shape, F32, kind="ExternalInput").ap() for n, v in arrays.items()}
    out = nc.dram_tensor("out", (TOK, P), F32, kind="ExternalOutput").ap()
    metaformer(nc, io, out)
    r = run_bass_kernel_spmd(nc, [{"in_" + n: v for n, v in arrays.items()}], core_ids=[0])
    return r.results[0]["out"].reshape(1, ROWS, COLS, P)
```

```python
from contextlib import ExitStack

import numpy as np

import concourse.bass as bass
from concourse import mybir

F32 = mybir.dt.float32
F32R = mybir.dt.float32r
I32 = mybir.dt.int32
ACT = mybir.ActivationFunctionType
ALU = mybir.AluOpType
AX = mybir.AxisListType

P = 128
ROWS = 256
COLS = 256
TOK = ROWS * COLS
NT = COLS // P
HEADS, DH = 4, 32
EXPERTS = 8
EPS_LN, EPS_LNC, EPS_BN = 1e-5, 1e-6, 1e-5
TWICE_MUL, TWICE_ADD = 1.0 + EPS_LN, EPS_LN * EPS_LNC


SEG = 32
WARM = 16
LANES = TOK // SEG
G = 4
BATCH = G * P
NB = LANES // BATCH
STEPS = WARM + SEG
BLK = 8
NBLK = SEG // BLK
QUADS = BLK // 4
TOL = 2.0 ** -20


def need(engine, sem, rows, per=1):
    if isinstance(rows, int):
        if rows > 0:
            engine.wait_ge(sem, min(rows, ROWS) * per)
    else:
        engine.wait_ge(sem, rows * per if per > 1 else rows)


def settle(engine, passed):
    engine.sem_inc(passed, 1)


def inside(row, count=ROWS):
    return not isinstance(row, int) or 0 <= row < count


def split3(pe, out, x_h, x_l, w_h, w_l):
    pe.matmul(out, x_h, w_h, start=True, stop=False)
    pe.matmul(out, x_h, w_l, start=False, stop=False)
    return pe.matmul(out, x_l, w_h, start=False, stop=True)


def pipeline(engine, body, first, last, loop_from, loop_to, unroll):
    for k in range(first, loop_from):
        body(k, k % unroll)
    with engine.Fori(0, (loop_to - loop_from) // unroll) as turn:
        for u in range(unroll):
            body(turn * unroll + (loop_from + u), (loop_from + u) % unroll)
    for k in range(loop_to, last):
        body(k, k % unroll)


QR = 4
QT = QR * NT


def norm_pass(nc, io, zt_d, bias_d):
    ctx = ExitStack()
    with ctx:
        def sb(name, shape, dt=F32):
            return ctx.enter_context(nc.sbuf_tensor(name, shape, dt))

        def sem(name):
            return ctx.enter_context(nc.semaphore(name))

        ident = sb("ident0", [P, P])
        wb = sb("wb", [P, DH])
        ln_cols = sb("ln_cols", [P, 2])
        mhalf = sb("mhalf0", [P, QT])
        x_t = [sb(f"x0_{u}", [P, QT, P]) for u in range(4)]
        stat = sb("stat0", [P, QT, 6])
        mv = [sb(f"mv0_{u}", [P, QT, 2]) for u in range(2)]
        v = sb("v0", [P, QT])
        rs = [sb(f"rs0_{u}", [P, QT]) for u in range(2)]
        xh = [sb(f"xh0_{u}", [P, QT, P]) for u in range(2)]
        zt = [sb(f"zt0_{u}", [P, QR * COLS]) for u in range(2)]
        bias = [sb(f"bias0_{u}", [P, COLS]) for u in range(2)]
        psT = [ctx.enter_context(nc.psum_tensor(f"psT0_{i}", [P, 2, 512], F32)) for i in range(2)]
        psB = [ctx.enter_context(nc.psum_tensor(f"psB0_{i}", [P, 512], F32)) for i in range(2)]

        w_in, setup, passed_pool, passed_dve = sem("w_in0"), sem("setup0"), sem("passed_pool0"), sem("passed_dve0")
        x_in = [sem(f"x_in0_{u}") for u in range(4)]
        stat_s, mv_s, v_s, rs_s, xh_s, tr_mm, zt_s, b_mm, b_s = (
            sem(n + "0") for n in ("stat_s", "mv_s", "v_s", "rs_s", "xh_s", "tr_mm", "zt_s", "b_mm", "b_s"))
        zt_out = [sem(f"zt_out0_{u}") for u in range(2)]
        b_out = [sem(f"b_out0_{u}") for u in range(2)]
        x_v = io["x"].rearrange("(m j p) c -> m p j c", j=QT, p=P)
        zt_v = zt_d.rearrange("p (m t) -> m p t", t=QR * COLS)
        b_v = bias_d.rearrange("(m r) h k -> m r h k", r=QR)
        N0 = ROWS // QR
        FIRST, LAST, LOOP0, LOOP1, U = -2, N0, 4, 60, 4

        def upto(engine, s, n, per=1):
            need(engine, s, min(n, N0) if isinstance(n, int) else n, per)

        block = ctx.enter_context(nc.Block())

        @block.sync
        def _(sp):
            for dst, src in ((ident[:], io["ident"]), (wb[:], io["WbPad"]), (ln_cols[:], io["ln_cols"])):
                sp.dma_start(dst, src).then_inc(w_in, 16)

            def body(m, u):
                if inside(m + 3, N0):
                    upto(sp, xh_s, m)
                    sp.dma_start(x_t[(u + 3) % 4][:], x_v[m + 3]).then_inc(x_in[(u + 3) % 4], 16)
                if inside(m, N0):
                    upto(sp, zt_s, m + 1)
                    sp.dma_start(zt_v[m], zt[u % 2][:]).then_inc(zt_out[u % 2], 16)
                    upto(sp, b_s, m + 1)
                    for r in range(QR):
                        sp.dma_start(b_v[m, r], bias[u % 2][DH * r:DH * r + HEADS, :]).then_inc(b_out[u % 2], 16)

            pipeline(sp, body, FIRST - 1, LAST, LOOP0, LOOP1, U)
            for u in range(2):
                sp.wait_ge(zt_out[u], 16 * N0 // 2)
                sp.wait_ge(b_out[u], 16 * QR * N0 // 2)

        @block.gpsimd
        def _(pool):
            pool.memset(mhalf[:], -0.5).then_inc(setup, 1)
            pool.wait_ge(setup, 1)

            def body(m, u):
                b = u % 2
                if inside(m + 2, N0):
                    upto(pool, mv_s, m + 3)
                    upto(pool, rs_s, m + 2)
                    settle(pool, passed_pool)
                    pool.tensor_scalar(v[:], mv[b][:, :, 1], TWICE_MUL, TWICE_ADD, ALU.mult, ALU.add).then_inc(v_s, 1)
                    upto(pool, v_s, m + 3)
                    upto(pool, xh_s, m + 1)
                    pool.tensor_tensor(rs[b][:], v[:], mhalf[:], ALU.pow).then_inc(rs_s, 1)

            pipeline(pool, body, FIRST, LAST, LOOP0, LOOP1, U)

        @block.vector
        def _(dve):
            def body(m, u):
                b, q = u % 2, (u + 2) % 4
                if inside(m + 2, N0):
                    dve.wait_ge(x_in[q], (m + 2 - q) * 4 + 16)
                    upto(dve, mv_s, m + 2)
                    for t in range(QT):
                        last = dve.bn_stats(stat[:, t, :], x_t[q][:, t, :])
                    last.then_inc(stat_s, 1)
                if inside(m, N0):
                    upto(dve, b_mm, m + 1)
                    upto(dve, b_out[b], m - b, 16 * QR // 2)
                    dve.tensor_scalar(bias[b][:], psB[b][:, 0:COLS], -1.0, None, ALU.mult).then_inc(b_s, 1)
                if inside(m + 2, N0):
                    upto(dve, stat_s, m + 3)
                    upto(dve, v_s, m + 1)
                    upto(dve, xh_s, m + 1)
                    settle(dve, passed_dve)
                    for t in range(QT):
                        last = dve.bn_aggr(mv[b][:, t, :], stat[:, t, :])
                    last.then_inc(mv_s, 1)
                    upto(dve, rs_s, m + 3)
                    upto(dve, mv_s, m + 3)
                    upto(dve, tr_mm, m + 1)
                    for t in range(QT):
                        last = dve.tensor_scalar(xh[b][:, t, :], x_t[q][:, t, :], mv[b][:, t, 0:1], rs[b][:, t:t + 1],
                                                 ALU.subtract, ALU.mult)
                    last.then_inc(xh_s, 1)

            pipeline(dve, body, FIRST, LAST, LOOP0, LOOP1, U)

        @block.scalar
        def _(act):
            act.wait_ge(w_in, 48)

            def body(m, u):
                a = (u + 1) % 2
                if inside(m + 1, N0):
                    upto(act, tr_mm, m + 2)
                    upto(act, zt_out[a], m + 1 - a, 8)
                    upto(act, b_mm, m)
                    for i in range(2):
                        last = act.activation(zt[a][:, i * 512:(i + 1) * 512], psT[a][:, i, :], ACT.Identity,
                                              bias=ln_cols[:, 1:2], scale=ln_cols[:, 0:1])
                    last.then_inc(zt_s, 1)

            pipeline(act, body, FIRST, LAST, LOOP0, LOOP1, U)

        @block.tensor
        def _(pe):
            pe.wait_ge(w_in, 48)

            def body(m, u):
                a = (u + 1) % 2
                if inside(m + 1, N0):
                    upto(pe, xh_s, m + 2)
                    upto(pe, zt_s, m)
                    for t in range(QT):
                        last = pe.transpose(psT[a][:, t // 4, (t % 4) * P:(t % 4 + 1) * P], xh[a][:, t, :], ident[:])
                    last.then_inc(tr_mm, 1)
                if inside(m, N0):
                    upto(pe, zt_s, m + 1)
                    upto(pe, b_s, m - 1)
                    for r in range(QR):
                        last = pe.matmul(psB[u % 2][DH * r:DH * (r + 1), 0:COLS], wb[:],
                                         zt[u % 2][:, r * COLS:(r + 1) * COLS], start=True, stop=True)
                    last.then_inc(b_mm, 1)

            pipeline(pe, body, FIRST, LAST, LOOP0, LOOP1, U)


def attention_pass(nc, io, zt_d, bias_d, t1_d, wx_d, bn_sb):
    ctx = ExitStack()
    with ctx:
        def sb(name, shape, dt=F32):
            return ctx.enter_context(nc.sbuf_tensor(name, shape, dt))

        def ps(name, shape):
            return ctx.enter_context(nc.psum_tensor(name, shape, F32))

        sems = []

        def sem(name):
            sems.append(nc.alloc_semaphore(name))
            return sems[-1]

        w_s = sb("w_s", [P, 4, P])
        wo_s = sb("wo_s", [P, P])
        wt_s = sb("wt_s", [P, P])
        ident = sb("ident", [P, P])
        half = sb("half", [P, DH])
        mhalf = sb("mhalf", [P, NT])
        bias = sb("bias", [P, NT, HEADS, COLS])
        pad = sb("pad", [P, WARM])

        x_t = [sb(f"x_t{u}", [P, NT, P]) for u in range(4)]
        zT = [sb(f"zT{u}", [P, COLS]) for u in range(4)]
        zh = [sb(f"zh{u}", [P, COLS], F32R) for u in range(4)]
        zl = [sb(f"zl{u}", [P, COLS], F32R) for u in range(4)]
        w_h, w_l = sb("w_h", [P, 4, P], F32R), sb("w_l", [P, 4, P], F32R)
        qk = [sb(f"qk{u}", [P, 2 * COLS]) for u in range(2)]
        qk_h = [sb(f"qk_h{u}", [P, 2 * COLS], F32R) for u in range(2)]
        qk_l = [sb(f"qk_l{u}", [P, 2 * COLS], F32R) for u in range(2)]
        vv = [sb(f"vv{u}", [P, NT, P]) for u in range(2)]
        th = [sb(f"th{u}", [P, COLS]) for u in range(2)]
        score = [sb(f"score{u}", [P, NT, HEADS, COLS]) for u in range(2)]
        least = [sb(f"least{u}", [P, NT, HEADS]) for u in range(2)]
        prob = [sb(f"prob{u}", [P, NT, HEADS, COLS]) for u in range(2)]
        total = [sb(f"total{u}", [P, NT * HEADS]) for u in range(2)]
        rtotal = [sb(f"rtotal{u}", [P, NT * HEADS]) for u in range(2)]
        spread = [sb(f"spread{u}", [P, NT, P]) for u in range(2)]
        probT = [sb(f"probT{u}", [P, HEADS, NT, COLS]) for u in range(2)]
        gated = [sb(f"gated{u}", [P, COLS]) for u in range(2)]
        og = [sb(f"og{u}", [P, COLS]) for u in range(2)]
        t1 = [sb(f"t1_{u}", [P, NT, P]) for u in range(2)]
        stat2 = [sb(f"stat2_{u}", [P, NT, 6]) for u in range(2)]
        mv2 = [sb(f"mv2_{u}", [P, NT, 2]) for u in range(2)]
        v2 = [sb(f"v2_{u}", [P, NT]) for u in range(2)]
        rs2 = [sb(f"rs2_{u}", [P, NT]) for u in range(2)]
        yh = [sb(f"yh{u}", [P, NT, P]) for u in range(2)]
        yT = [sb(f"yT{u}", [P, COLS]) for u in range(2)]
        wx = [sb(f"wx{u}", [P, COLS]) for u in range(2)]
        wx_stat = sb("wx_stat", [P, ROWS, 6])

        psS = [ps(f"psS{i}", [P, 512]) for i in range(2)]
        psT = [ps(f"psT{i}", [P, 512]) for i in range(2)]
        psQK, psVG = ps("psQK", [P, 512]), ps("psVG", [P, 512])
        psO = ps("psO", [P, 512])
        psM = ps("psM", [P, 512])

        w_in, setup_d, pad_out, passed_pool, passed_dve = (
            sem(n) for n in ("w_in", "setup_d", "pad_out", "passed_pool", "passed_dve"))
        x_in = [sem(f"x_in{u}") for u in range(4)]
        z_in = [sem(f"z_in{u}") for u in range(4)]
        qk_mm, qk_s, vg_mm, vg_s, s_mm, score_s, prob_s, tr_mm, probT_s = (
            sem(n) for n in ("qk_mm", "qk_s", "vg_mm", "vg_s", "s_mm", "score_s", "prob_s", "tr_mm", "probT_s"))
        w_split, zh_s, zl_s, qkh_s, qkl_s = (sem(n) for n in ("w_split", "zh_s", "zl_s", "qkh_s", "qkl_s"))
        rtotal_s, spread_s, pv_mm, rt_mm, gated_s, og_s, out_mm = (
            sem(n) for n in ("rtotal_s", "spread_s", "pv_mm", "rt_mm", "gated_s", "og_s", "out_mm"))
        t1_s, stat2_s, mv2_s, v2_s, rs2_s, yh_s, yT_mm, yT_s, wx_mm, wx_s, wstat_s = (
            sem(n) for n in ("t1_s", "stat2_s", "mv2_s", "v2_s", "rs2_s", "yh_s", "yT_mm", "yT_s",
                             "wx_mm", "wx_s", "wstat_s"))
        t1_out = [sem(f"t1_out{u}") for u in range(2)]
        wx_out = [sem(f"wx_out{u}") for u in range(2)]

        x_v = io["x"].rearrange("(r j p) c -> r p j c", j=NT, p=P)
        z_v = zt_d.rearrange("p (r t) -> r p t", t=COLS)
        t1_v = t1_d.rearrange("(r j p) c -> r p j c", j=NT, p=P)
        wx_v = wx_d[:, WARM:WARM + TOK].rearrange("p (r t) -> r p t", t=COLS)

        FIRST, LAST, LOOP0, LOOP1, U = -3, ROWS + 3, 4, 248, 4
        UNITS = 4
        block = ctx.enter_context(nc.Block())

        @block.sync
        def _(sp):
            loads = [(w_s[:, i, :], io[n]) for i, n in enumerate(("Wq", "Wk", "Wv", "Wg"))]
            loads += [(wo_s[:], io["Wo"]), (wt_s[:], io["WT"]), (ident[:], io["ident"])]
            loads += [(bias[:, t], bias_d[t * P:(t + 1) * P]) for t in range(NT)]
            for dst, src in loads:
                sp.dma_start(dst, src).then_inc(w_in, 16)
            sp.wait_ge(setup_d, 3)
            sp.dma_start(wx_d[:, 0:WARM], pad[:]).then_inc(pad_out, 16)

            def body(k, u):
                if inside(k + 4):
                    need(sp, zl_s, k + 1)
                    sp.dma_start(zT[u][:], z_v[k + 4]).then_inc(z_in[u], 16)
                if inside(k + 1):
                    need(sp, t1_s, k - 2)
                    sp.dma_start(x_t[(u + 1) % 4][:], x_v[k + 1]).then_inc(x_in[(u + 1) % 4], 16)
                if inside(k - 3):
                    need(sp, wx_s, k - 2)
                    sp.dma_start(wx_v[k - 3], wx[(u - 3) % 2][:]).then_inc(wx_out[(u - 3) % 2], 16)
                if inside(k - 2):
                    need(sp, t1_s, k - 1)
                    sp.dma_start(t1_v[k - 2], t1[u % 2][:]).then_inc(t1_out[u % 2], 16)

            pipeline(sp, body, FIRST - 1, LAST, LOOP0, LOOP1, U)
            sp.wait_ge(pad_out, 16)
            for u in range(2):
                sp.wait_ge(t1_out[u], 16 * ROWS // 2)
                sp.wait_ge(wx_out[u], 16 * ROWS // 2)

        @block.gpsimd
        def _(pool):
            pool.memset(mhalf[:], -0.5).then_inc(setup_d, 1)
            pool.memset(half[:], 0.5).then_inc(setup_d, 1)
            pool.memset(pad[:], 0.0).then_inc(setup_d, 1)
            pool.wait_ge(setup_d, 3)

            def body(k, u):
                a, b = (u + 1) % 2, u % 2
                if inside(k - 1):
                    need(pool, rtotal_s, k)
                    need(pool, rt_mm, k - 2)
                    pool.tensor_tensor(
                        spread[a][:].rearrange("p t (h d) -> p (t h) d", h=HEADS),
                        rtotal[a][:].unsqueeze(2).to_broadcast([P, NT * HEADS, DH]),
                        half[:].unsqueeze(1).to_broadcast([P, NT * HEADS, DH]), ALU.mult).then_inc(spread_s, 1)
                if inside(k + 3):
                    q = (u + 3) % 4
                    pool.wait_ge(z_in[q], (k + 3 - q) * 4 + 16)
                    need(pool, vg_mm, k)
                    settle(pool, passed_pool)
                    pool.tensor_copy(zh[q][:], zT[q][:]).then_inc(zh_s, 1)
                    need(pool, zh_s, k + 4)
                    pool.tensor_tensor(zl[q][:], zT[q][:], zh[q][:].bitcast(F32), ALU.subtract).then_inc(zl_s, 1)
                if inside(k + 1):
                    need(pool, qk_s, k + 2)
                    need(pool, s_mm, k, UNITS)
                    settle(pool, passed_pool)
                    pool.tensor_copy(qk_h[a][:], qk[a][:]).then_inc(qkh_s, 1)
                    need(pool, qkh_s, k + 2)
                    pool.tensor_tensor(qk_l[a][:], qk[a][:], qk_h[a][:].bitcast(F32), ALU.subtract).then_inc(qkl_s, 1)
                if inside(k - 2):
                    need(pool, mv2_s, k - 1)
                    need(pool, rs2_s, k - 3)
                    settle(pool, passed_pool)
                    pool.tensor_scalar(v2[b][:], mv2[b][:, :, 1], 1.0, EPS_LN, ALU.mult, ALU.add).then_inc(v2_s, 1)
                    need(pool, v2_s, k - 1)
                    need(pool, yh_s, k - 3)
                    pool.tensor_tensor(rs2[b][:], v2[b][:], mhalf[:], ALU.pow).then_inc(rs2_s, 1)

            pipeline(pool, body, FIRST, LAST, LOOP0, LOOP1, U)

        @block.vector
        def _(dve):
            dve.wait_ge(w_in, 9 * 16)
            dve.tensor_copy(w_h[:], w_s[:]).then_inc(w_split, 1)
            dve.wait_ge(w_split, 1)
            dve.tensor_tensor(w_l[:], w_s[:], w_h[:].bitcast(F32), ALU.subtract).then_inc(w_split, 1)

            def body(k, u):
                a, b = (u + 1) % 2, u % 2
                if inside(k - 1):
                    need(dve, prob_s, k, UNITS)
                    need(dve, spread_s, k - 2)
                    dve.reciprocal(rtotal[a][:], total[a][:]).then_inc(rtotal_s, 1)
                for n in range(UNITS):
                    if inside(k):
                        dve.wait_ge(s_mm, k * UNITS + n + 1)
                        need(dve, prob_s, k - 1, UNITS)
                        settle(dve, passed_dve)
                        for t in range(NT):
                            last = dve.tensor_tensor_reduce(
                                out=score[b][:, t, n, :], in0=psS[n % 2][:, t * COLS:(t + 1) * COLS],
                                in1=bias[:, t, n, :], scale=1.0, scalar=3e38, op0=ALU.add, op1=ALU.min,
                                accum_out=least[b][:, t, n:n + 1])
                        last.then_inc(score_s, 1)
                    if inside(k - 1):
                        dve.wait_ge(tr_mm, (k - 1) * UNITS + n + 1)
                        need(dve, pv_mm, k - 2)
                        dve.tensor_copy(probT[a][:, n].rearrange("p t q -> p (t q)"), psT[n % 2][:]).then_inc(probT_s, 1)
                    if inside(k - 2):
                        if n == 1:
                            need(dve, out_mm, k - 1)
                            dve.wait_ge(x_in[(u - 2) % 4], (k - 2 - (u - 2) % 4) * 4 + 16)
                            need(dve, yh_s, k - 3)
                            need(dve, t1_out[b], k - 2 - b, 8)
                            dve.tensor_tensor(t1[b][:], psM[:, 0:COLS].rearrange("p (j c) -> p j c", j=NT),
                                              x_t[(u - 2) % 4][:], ALU.add).then_inc(t1_s, 1)
                        if n == 2:
                            need(dve, t1_s, k - 1)
                            need(dve, mv2_s, k - 3)
                            for j in range(NT):
                                last = dve.bn_stats(stat2[b][:, j, :], t1[b][:, j, :])
                            last.then_inc(stat2_s, 1)
                        if n == 3:
                            need(dve, stat2_s, k - 1)
                            need(dve, v2_s, k - 3)
                            need(dve, yh_s, k - 3)
                            settle(dve, passed_dve)
                            for j in range(NT):
                                last = dve.bn_aggr(mv2[b][:, j, :], stat2[b][:, j, :])
                            last.then_inc(mv2_s, 1)
                if inside(k - 3):
                    need(dve, wx_s, k - 2)
                    dve.bn_stats(wx_stat[:, bass.ds(k - 3, 1), :], wx[a][:]).then_inc(wstat_s, 1)
                if inside(k - 2):
                    need(dve, rs2_s, k - 1)
                    need(dve, mv2_s, k - 1)
                    need(dve, yT_mm, k - 3)
                    for j in range(NT):
                        last = dve.tensor_scalar(yh[b][:, j, :], t1[b][:, j, :], mv2[b][:, j, 0:1],
                                                 rs2[b][:, j:j + 1], ALU.subtract, ALU.mult)
                    last.then_inc(yh_s, 1)
                if inside(k - 1):
                    need(dve, rt_mm, k)
                    need(dve, vg_s, k)
                    need(dve, og_s, k - 2)
                    dve.scalar_tensor_tensor(gated[a][:], th[a][:], 1.0, psO[:, 0:COLS], ALU.add,
                                             ALU.mult).then_inc(gated_s, 1)
                    need(dve, gated_s, k)
                    need(dve, out_mm, k - 2)
                    dve.tensor_tensor(og[a][:], gated[a][:], psO[:, COLS:2 * COLS], ALU.mult).then_inc(og_s, 1)

            pipeline(dve, body, FIRST, LAST, LOOP0, LOOP1, U)
            dve.wait_ge(wstat_s, ROWS)
            dve.bn_aggr(bn_sb[:, 0:2], wx_stat[:].rearrange("p r s -> p (r s)")).then_inc(wstat_s, 1)

        @block.scalar
        def _(act):
            def body(k, u):
                a, b = (u + 1) % 2, u % 2
                if inside(k):
                    for n in range(UNITS):
                        act.wait_ge(score_s, k * UNITS + n + 1)
                        need(act, tr_mm, k - 1, UNITS)
                        need(act, rtotal_s, k - 1)
                        for t in range(NT):
                            last = act.activation(prob[b][:, t, n, :], score[b][:, t, n, :], ACT.Exp,
                                                  bias=least[b][:, t, n:n + 1], scale=-1.0,
                                                  accum_out=total[b][:, t * HEADS + n:t * HEADS + n + 1])
                        last.then_inc(prob_s, 1)
                if inside(k + 2):
                    need(act, qk_mm, k + 3)
                    need(act, qkl_s, k + 1)
                    act.activation(qk[b][:, 0:COLS], psQK[:, 0:COLS], ACT.Identity, scale=-(DH ** -0.5))
                    act.activation(qk[b][:, COLS:2 * COLS], psQK[:, COLS:2 * COLS], ACT.Identity).then_inc(qk_s, 1)
                if inside(k):
                    need(act, vg_mm, k + 1)
                    need(act, pv_mm, k - 1)
                    need(act, gated_s, k - 1)
                    act.activation(vv[b][:].rearrange("p t c -> p (t c)"), psVG[:, 0:COLS], ACT.Identity)
                    act.activation(th[b][:], psVG[:, COLS:2 * COLS], ACT.Tanh, scale=0.5).then_inc(vg_s, 1)
                if inside(k - 2):
                    need(act, yT_mm, k - 1)
                    need(act, wx_mm, k - 3)
                    act.activation(yT[b][:], psM[:, 0:COLS], ACT.Identity).then_inc(yT_s, 1)
                    need(act, wx_mm, k - 1)
                    need(act, wstat_s, k - 3)
                    need(act, wx_out[b], k - 2 - b, 8)
                    act.activation(wx[b][:], psM[:, COLS:2 * COLS], ACT.Identity).then_inc(wx_s, 1)

            pipeline(act, body, FIRST, LAST, LOOP0, LOOP1, U)

        @block.tensor
        def _(pe):
            pe.wait_ge(w_in, 9 * 16)
            pe.wait_ge(w_split, 2)

            def body(k, u):
                a, b = (u + 1) % 2, u % 2
                if inside(k):
                    need(pe, qkl_s, k + 1)
                for n in range(UNITS):
                    if inside(k):
                        if n >= 2 or not isinstance(k, int) or k > 0:
                            pe.wait_ge(score_s, k * UNITS + n - 1)
                        hs = slice(DH * n, DH * (n + 1))
                        for t in range(NT):
                            ts = slice(t * P, (t + 1) * P)
                            last = split3(pe, psS[n % 2][:, t * COLS:(t + 1) * COLS], qk_h[b][hs, ts], qk_l[b][hs, ts],
                                          qk_h[b][hs, COLS:2 * COLS], qk_l[b][hs, COLS:2 * COLS])
                        last.then_inc(s_mm, 1)
                    if inside(k - 1):
                        if n == 0:
                            need(pe, prob_s, k, UNITS)
                        if n >= 2 or not isinstance(k, int) or k > 1:
                            pe.wait_ge(probT_s, (k - 1) * UNITS + n - 1)
                        for j in range(NT):
                            for t in range(NT):
                                last = pe.transpose(psT[n % 2][:, j * COLS + t * P:j * COLS + (t + 1) * P],
                                                    prob[a][:, t, n, j * P:(j + 1) * P], ident[:])
                        last.then_inc(tr_mm, 1)
                    if n == 1 and inside(k - 2):
                        need(pe, og_s, k - 1)
                        need(pe, wx_s, k - 2)
                        for j in range(NT):
                            last = pe.matmul(psM[:, j * P:(j + 1) * P], og[b][:, j * P:(j + 1) * P], wo_s[:],
                                             start=True, stop=True)
                        last.then_inc(out_mm, 1)
                if inside(k + 2):
                    q = (u + 2) % 4
                    need(pe, zl_s, k + 3)
                    need(pe, qk_s, k + 2)
                    split3(pe, psQK[:, 0:COLS], w_h[:, 0, :], w_l[:, 0, :], zh[q][:], zl[q][:])
                    split3(pe, psQK[:, COLS:2 * COLS], w_h[:, 1, :], w_l[:, 1, :], zh[q][:], zl[q][:]).then_inc(qk_mm, 1)
                if inside(k):
                    need(pe, vg_s, k)
                    for j in range(NT):
                        js = slice(j * P, (j + 1) * P)
                        split3(pe, psVG[:, js], zh[u % 4][:, js], zl[u % 4][:, js], w_h[:, 2, :], w_l[:, 2, :])
                    split3(pe, psVG[:, COLS:2 * COLS], w_h[:, 3, :], w_l[:, 3, :], zh[u % 4][:], zl[u % 4][:]
                           ).then_inc(vg_mm, 1)
                if inside(k - 1):
                    need(pe, probT_s, k, UNITS)
                    need(pe, og_s, k - 1)
                    for j in range(NT):
                        for h in range(HEADS):
                            hs = slice(DH * h, DH * (h + 1))
                            last = pe.matmul(psO[hs, 0:COLS], vv[a][:, j, hs], probT[a][:, h, j, :],
                                             start=j == 0, stop=j == NT - 1)
                    last.then_inc(pv_mm, 1)
                if inside(k - 2):
                    need(pe, yh_s, k - 1)
                    for j in range(NT):
                        last = pe.transpose(psM[:, j * P:(j + 1) * P], yh[b][:, j, :], ident[:])
                    last.then_inc(yT_mm, 1)
                if inside(k - 1):
                    need(pe, spread_s, k)
                    for t in range(NT):
                        last = pe.transpose(psO[:, COLS + t * P:COLS + (t + 1) * P], spread[a][:, t, :], ident[:])
                    last.then_inc(rt_mm, 1)
                if inside(k - 2):
                    need(pe, yT_s, k - 1)
                    pe.matmul(psM[:, COLS:2 * COLS], wt_s[:], yT[b][:], start=True, stop=True).then_inc(wx_mm, 1)

            pipeline(pe, body, FIRST, LAST, LOOP0, LOOP1, U)

    nc.all_engine_barrier()
    nc.clear_and_free_semaphores(sems)
    nc.all_engine_barrier()


def recurrence_pass(nc, io, t1_d, wx_d, t2_d, bn_sb):
    ctx = ExitStack()
    with ctx:
        def sb(name, shape, dt=F32):
            return ctx.enter_context(nc.sbuf_tensor(name, shape, dt))

        def ps(name, shape):
            return ctx.enter_context(nc.psum_tensor(name, shape, F32))

        def sem(name):
            return ctx.enter_context(nc.semaphore(name))

        vt_s = sb("vt_s", [P, P])
        ident = sb("ident_r", [P, P])
        gb = sb("gb", [P, 2])
        mhalf = sb("mhalf_r", [P, 1])
        var_e = sb("var_e", [P, 1])
        rstd = sb("rstd", [P, 1])
        am = sb("am", [P, 1])
        bn_a = sb("bn_a", [P, 1])
        bn_b = sb("bn_b", [P, 1])
        wxb = [sb(f"wxb{i}", [P, WARM + BATCH * SEG]) for i in range(2)]
        y = [sb(f"y{g}", [P, BLK, P]) for g in range(G)]
        pre = [sb(f"pre{g}", [P, 2, P]) for g in range(G)]
        t1b = [[sb(f"t1b{g}{i}", [P, BLK, P]) for i in range(2)] for g in range(G)]
        warm_mask = sb("warm_mask", [P, LANES])
        end_mask = sb("end_mask", [P, 1])
        starts = sb("starts", [P, LANES])
        ends = sb("ends", [P, 1 + LANES])
        guess = [sb(f"guess{g}", [P, P]) for g in range(G)]
        off = warm_mask
        off_max = sb("off_max", [P, 1])
        off_bad = sb("off_bad", [P, 1])
        ones = sb("ones_r", [P, 1])
        again = sb("again", [1, 1], I32)

        psY = [ps(f"psY{g}", [P, 512]) for g in range(G)]
        psT = [ps(f"psTr{g}", [P, 4, P]) for g in range(G)]

        c_in, c_ready, bn_c, bn_p = sem("c_in"), sem("c_ready"), sem("bn_c"), sem("bn_p")
        wx_in = [sem(f"wx_in{i}") for i in range(2)]
        wx_free = sem("wx_free")
        mm = [sem(f"mm{g}") for g in range(G)]
        pre_s = [sem(f"pre_s{g}") for g in range(G)]
        y_s = [sem(f"y_s{g}") for g in range(G)]
        guess_s = [sem(f"guess_s{g}") for g in range(G)]
        start_s = [sem(f"start_s{g}") for g in range(G)]
        begin_s = [sem(f"begin_s{g}") for g in range(G)]
        tr = [sem(f"tr{g}") for g in range(G)]
        t2_s = [sem(f"t2_s{g}") for g in range(G)]
        t1_in = [[sem(f"t1_in{g}{i}") for i in range(2)] for g in range(G)]
        t2_out = [[sem(f"t2_out{g}{i}") for i in range(2)] for g in range(G)]
        off_s, bad_s, sum_mm, again_s, seen = sem("off_s"), sem("bad_s"), sem("sum_mm"), sem("again_s"), sem("seen")
        passed_r = {e: sem("passed_" + e + "2") for e in ("sp", "act", "pe", "dve")}
        CREDIT_OUT, CREDIT_T2 = 16, 1

        t1_v = t1_d.rearrange("(b g p k s) c -> b g k p s c", g=G, p=P, k=NBLK, s=BLK)
        t2_v = t2_d.rearrange("(b g p k s) c -> b g k p s c", g=G, p=P, k=NBLK, s=BLK)
        block = ctx.enter_context(nc.Block())

        def passes(engine, one_pass, passed):
            with engine.register("n_pass") as n_pass, engine.register("go_on") as go_on:
                engine.reg_mov(n_pass, 0)
                engine.reg_mov(go_on, 1)
                with engine.While(lambda: go_on):
                    n = engine.snap(n_pass)
                    one_pass(n)
                    engine.wait_ge(again_s, n + 1)
                    settle(engine, passed)
                    engine.reg_load(go_on, again[0:1, 0:1])
                    engine.drain().then_inc(seen, 1)
                    engine.reg_add(n_pass, n_pass, 1)

        @block.sync
        def _(sp):
            for dst, src in ((vt_s[:], io["VT"]), (ident[:], io["ident"]), (gb[:], io["bn_cols"])):
                sp.dma_start(dst, src).then_inc(c_in, 16)
            for g in range(G):
                for i in range(2):
                    sp.nop().then_inc(t2_out[g][i], CREDIT_OUT)

            def one_pass(n):
                def load_t1(b, k, g):
                    sp.wait_ge(t2_out[g][k % 2], (n * NB + b) * (8 * NBLK) + (k // 2) * 16 + CREDIT_OUT)
                    sp.dma_start(t1b[g][k % 2][:], t1_v[b, g, k]).then_inc(t1_in[g][k % 2], 16)

                def load_wx(b):
                    sp.wait_ge(wx_free, n * NB + b + 1)
                    sp.dma_start(wxb[b % 2][:], wx_d[:, b * (BATCH * SEG):(b + 1) * (BATCH * SEG) + WARM]
                                 ).then_inc(wx_in[b % 2], 16)

                load_wx(0)
                for b in range(NB):
                    for k in range(2):
                        for g in range(G):
                            load_t1(b, k, g)
                    if b + 1 < NB:
                        load_wx(b + 1)
                    for k in range(NBLK):
                        for g in range(G):
                            sp.wait_ge(t2_s[g], ((n * NB + b) * NBLK + (k + 1)) * QUADS + CREDIT_T2)
                            sp.dma_start(t2_v[b, g, k], t1b[g][k % 2][:]).then_inc(t2_out[g][k % 2], 16)
                        if k + 2 < NBLK:
                            for g in range(G):
                                load_t1(b, k + 2, g)
                for g in range(G):
                    for i in range(2):
                        sp.wait_ge(t2_out[g][i], (n + 1) * (NB * NBLK * 8) + CREDIT_OUT)

            passes(sp, one_pass, passed_r["sp"])

        @block.gpsimd
        def _(pool):
            pool.memset(mhalf[:], -0.5).then_inc(bn_p, 1)
            pool.tensor_scalar(var_e[:], bn_sb[:, 1:2], 1.0, EPS_BN, ALU.mult, ALU.add).then_inc(bn_p, 1)
            pool.wait_ge(bn_p, 2)
            pool.tensor_tensor(rstd[:], var_e[:], mhalf[:], ALU.pow).then_inc(bn_p, 1)

        @block.vector
        def _(dve):
            dve.nop().then_inc(wx_free, 2)
            for g in range(G):
                dve.nop().then_inc(t2_s[g], CREDIT_T2)
            dve.memset(ones[:], 1.0)
            dve.memset(warm_mask[:], 1.0).then_inc(bn_c, 1)
            dve.memset(end_mask[:], 0.0)
            dve.memset(ends[:], 0.0).then_inc(bn_c, 1)
            dve.wait_ge(bn_c, 1)
            dve.memset(warm_mask[:, 0:1], 0.0)
            for g in range(G):
                last = dve.memset(y[g][:, BLK - 1, :], 0.0)
            last.then_inc(bn_c, 1)
            dve.wait_ge(c_in, 48)
            dve.wait_ge(bn_p, 3)
            dve.tensor_tensor(bn_a[:], gb[:, 0:1], rstd[:], ALU.mult).then_inc(bn_c, 1)
            dve.wait_ge(bn_c, 4)
            dve.tensor_tensor(am[:], bn_a[:], bn_sb[:, 0:1], ALU.mult).then_inc(bn_c, 1)
            dve.wait_ge(bn_c, 5)
            dve.tensor_tensor(bn_b[:], gb[:, 1:2], am[:], ALU.subtract).then_inc(c_ready, 1)
            dve.wait_ge(c_ready, 1)

            def one_pass(n):
                with dve.Fori(0, NB // 2) as pair:
                    for i in range(2):
                        b = pair * 2 + i
                        nb = n * NB + b
                        base = nb * STEPS
                        wv = wxb[i][:]
                        dve.wait_ge(wx_in[i], n * (NB // 2 * 16) + pair * 16 + 16)

                        def step(s, j, g, now):
                            dve.wait_ge(mm[g], base + now + 1)
                            dve.scalar_tensor_tensor(
                                pre[g][:, j % 2, :],
                                wv[:, bass.ds(s + g * P * SEG, P, SEG)] if not isinstance(s, int)
                                else wv[:, s + g * P * SEG:s + g * P * SEG + (P - 1) * SEG + 1:SEG],
                                bn_a[:, 0:1], psY[g][:, 0:P], ALU.mult, ALU.add).then_inc(pre_s[g], 1)

                        for j in range(WARM):
                            for g in range(G):
                                step(j, j, g, j)
                        for g in range(G):
                            lanes = bass.ds(b * BATCH + g * P, P)
                            dve.wait_ge(y_s[g], base + WARM)
                            dve.tensor_tensor(guess[g][:], y[g][:, BLK - 1, :], warm_mask[:, lanes],
                                              ALU.mult).then_inc(guess_s[g], 1)
                        for g in range(G):
                            lanes = bass.ds(b * BATCH + g * P, P)
                            dve.wait_ge(guess_s[g], nb + 1)
                            dve.scalar_tensor_tensor(starts[:, lanes], ends[:, lanes], end_mask[:, 0:1], guess[g][:],
                                                     ALU.mult, ALU.add).then_inc(start_s[g], 1)
                        for g in range(G):
                            lanes = bass.ds(b * BATCH + g * P, P)
                            dve.wait_ge(start_s[g], nb + 1)
                            dve.tensor_scalar(y[g][:, BLK - 1, :], starts[:, lanes], 1.0, None,
                                              ALU.mult).then_inc(begin_s[g], 1)
                        for j in range(SEG):
                            if j % BLK == 0:
                                for g in range(G):
                                    dve.wait_ge(t1_in[g][j // BLK % 2], nb * (8 * NBLK) + (j // BLK // 2 * 16 + 16))
                            for g in range(G):
                                step(WARM + j, j, g, WARM + j)
                                if j % 4 == 1 and j > 4:
                                    add_states(nb, j // 4 - 1, g)
                        for g in range(G):
                            add_states(nb, SEG // 4 - 1, g)
                        for g in range(G):
                            dve.wait_ge(y_s[g], base + STEPS)
                            last = dve.tensor_scalar(ends[:, bass.ds(b * BATCH + g * P + 1, P)], y[g][:, BLK - 1, :], 1.0,
                                                     None, ALU.mult)
                        last.then_inc(wx_free, 1)
                dve.wait_ge(wx_free, (n + 1) * NB + 2)
                dve.tensor_tensor(off[:], starts[:], ends[:, 0:LANES], ALU.subtract).then_inc(off_s, 1)
                dve.wait_ge(off_s, n * 3 + 1)
                dve.tensor_tensor(off[:], off[:], off[:], ALU.mult).then_inc(off_s, 1)
                dve.wait_ge(off_s, n * 3 + 2)
                dve.tensor_reduce(off_max[:], off[:], AX.X, ALU.max).then_inc(off_s, 1)
                dve.wait_ge(off_s, n * 3 + 3)
                dve.tensor_scalar(off_bad[:], off_max[:], TOL * TOL, None, ALU.is_gt).then_inc(bad_s, 1)
                dve.memset(warm_mask[:], 0.0)
                dve.memset(end_mask[:], 1.0)
                dve.wait_ge(sum_mm, n + 1)
                dve.tensor_copy(again[0:1, 0:1], psY[0][0:1, 0:1]).then_inc(again_s, 1)
                dve.wait_ge(seen, n * 4 + 3)

            def add_states(nb, quad, g):
                dve.wait_ge(tr[g], nb * (SEG // 4) + (quad + 1))
                part = t1b[g][quad // QUADS % 2][:, 4 * (quad % QUADS):4 * (quad % QUADS) + 4, :]
                dve.tensor_tensor(part, psT[g][:], part, ALU.add).then_inc(t2_s[g], 1)

            passes(dve, one_pass, passed_r["dve"])

        @block.scalar
        def _(act):
            act.wait_ge(c_ready, 1)

            def one_pass(n):
                with act.Fori(0, NB) as b:
                    base = (n * NB + b) * STEPS
                    with act.Fori(0, STEPS, BLK) as s0:
                        for j in range(BLK):
                            for g in range(G):
                                act.wait_ge(pre_s[g], base + s0 + (j + 1))
                                act.activation(y[g][:, j, :], pre[g][:, j % 2, :], ACT.Sigmoid,
                                               bias=bn_b[:, 0:1]).then_inc(y_s[g], 1)

            passes(act, one_pass, passed_r["act"])

        @block.tensor
        def _(pe):
            pe.wait_ge(c_in, 48)
            pe.wait_ge(bn_c, 3)

            def one_pass(n):
                with pe.Fori(0, NB) as b:
                    nb = n * NB + b
                    base = nb * STEPS

                    def step(j, g):
                        pe.matmul(psY[g][:, 0:P], vt_s[:], y[g][:, (j - 1) % BLK, :], start=True,
                                  stop=True).then_inc(mm[g], 1)

                    def transposes(quad, g):
                        pe.wait_ge(t2_s[g], nb * (SEG // 4) + (quad + CREDIT_T2))
                        for q in range(4):
                            last = pe.transpose(psT[g][:, q, :], y[g][:, 4 * (quad % QUADS) + q, :], ident[:])
                        last.then_inc(tr[g], 1)

                    pe.wait_ge(wx_free, nb + 2)
                    for j in range(WARM):
                        for g in range(G):
                            if j:
                                pe.wait_ge(y_s[g], base + j)
                            step(j, g)
                    for j in range(SEG):
                        for g in range(G):
                            if j == 0:
                                pe.wait_ge(begin_s[g], nb + 1)
                            pe.wait_ge(y_s[g], base + (WARM + j))
                            step(j, g)
                            if j % 4 == 0 and j:
                                transposes(j // 4 - 1, g)
                    for g in range(G):
                        pe.wait_ge(y_s[g], base + STEPS)
                        transposes(SEG // 4 - 1, g)
                pe.wait_ge(bad_s, n + 1)
                pe.matmul(psY[0][0:1, 0:1], off_bad[:], ones[:], start=True, stop=True).then_inc(sum_mm, 1)

            passes(pe, one_pass, passed_r["pe"])


HALVES = 2
WID = 4
TILES = HALVES * WID
NM = ROWS // WID
FOLDED = 4
ROUTE, GAP = 15, 8
SUMS = 3
FX = 16


def mixer_pass(nc, io, t2_d, out_d):
    ctx = ExitStack()
    with ctx:
        def sb(name, shape, dt=F32):
            return ctx.enter_context(nc.sbuf_tensor(name, shape, dt))

        def ps(name, shape):
            return ctx.enter_context(nc.psum_tensor(name, shape, F32))

        def sem(name):
            return ctx.enter_context(nc.semaphore(name))

        ident = sb("ident_m", [P, P])
        ln_w, ln_b, be = sb("ln_w", [P, P]), sb("ln_b", [P, P]), sb("be", [P, P])
        w1 = sb("w1", [P, 2, COLS])
        w2 = sb("w2", [P, 2, COLS])
        w3t = sb("w3t", [P, 2, COLS])
        b12 = sb("b12", [P, 4])
        b12w = sb("b12w", [P, 4, P])
        b3 = sb("b3", [P, COLS])
        w32 = sb("w32", [P, 2, COLS])
        mix = sb("mix", [P, 2, COLS])
        mix_b = sb("mix_b", [P, COLS])
        out_b = sb("out_b", [P, HALVES, P])
        wet = sb("wet", [P, P])
        rw, rb, dec = sb("rw", [P, EXPERTS]), sb("rb", [P, EXPERTS]), sb("dec", [P, EXPERTS])
        rwhl = sb("rwhl", [P, 2, EXPERTS], F32R)
        ew = sb("ew", [P, EXPERTS * P])
        ewh, ewl = sb("ewh", [P, EXPERTS * P], F32R), sb("ewl", [P, EXPERTS * P], F32R)
        eb = sb("eb", [TILES * EXPERTS, TILES * P])
        ebh, ebl = sb("ebh", [TILES * EXPERTS, TILES * P], F32R), sb("ebl", [TILES * EXPERTS, TILES * P], F32R)
        mhalf, minus = sb("mhalf_m", [P, TILES]), sb("minus_m", [P, TILES])

        t2 = [sb(f"t2_{u}", [P, TILES, P]) for u in range(4)]
        t2e = [sb(f"t2e{u}", [P, TILES, P]) for u in range(2)]
        statc = sb("statc", [P, TILES, 6])
        mvc = sb("mvc", [P, TILES, 2])
        vc, nmc = sb("vc", [P, TILES]), sb("nmc", [P, TILES])
        rsc = [sb(f"rsc{u}", [P, TILES]) for u in range(2)]
        bsc = [sb(f"bsc{u}", [P, TILES]) for u in range(2)]
        xc = sb("xc", [P, TILES, P])
        xw = sb("xw", [P, TILES, P])
        xb = sb("xb", [P, TILES, P])
        ug = [sb(f"ug{u}", [P, TILES, P]) for u in range(2)]
        mT = [sb(f"mT{u}", [P, WID, COLS]) for u in range(2)]
        t3 = [sb(f"t3_{u}", [P, TILES, P]) for u in range(2)]
        state = sb("state", [P, TILES, 6])
        mve = sb("mve", [P, TILES, 2])
        ve, nme = sb("ve", [P, TILES]), sb("nme", [P, TILES])
        rse = [sb(f"rse{u}", [P, TILES]) for u in range(2)]
        bse = [sb(f"bse{u}", [P, TILES]) for u in range(2)]
        xe = [sb(f"xe{u}", [P, TILES, P]) for u in range(2)]
        xh = [sb(f"xh_m{u}", [P, TILES, P], F32R) for u in range(2)]
        xl = [sb(f"xl_m{u}", [P, TILES, P], F32R) for u in range(2)]
        logit = sb("logit", [P, TILES, EXPERTS])
        logit_h = sb("logit_h", [P, TILES, EXPERTS])
        logit2 = sb("logit2", [P, TILES, EXPERTS])
        is_max = sb("is_max", [P, TILES, EXPERTS])
        order = sb("order", [P, TILES, EXPERTS])
        pick = [sb(f"pick{i}", [P, TILES, EXPERTS]) for i in range(2)]
        share = [sb(f"share{i}", [P, TILES, EXPERTS]) for i in range(2)]
        top = [sb(f"top{i}", [P, TILES]) for i in range(2)]
        first = sb("first", [P, TILES])
        gap = sb("gap", [P, TILES])
        th = sb("th_m", [P, TILES])
        wgt = [sb(f"wgt{i}", [P, TILES]) for i in range(2)]
        gate = [sb(f"gate{u}", [P, TILES, EXPERTS]) for u in range(2)]
        gateTh = [sb(f"gateTh{u}", [TILES * EXPERTS, P], F32R) for u in range(2)]
        gateTl = [sb(f"gateTl{u}", [TILES * EXPERTS, P], F32R) for u in range(2)]
        acc = [sb(f"acc{u}", [P, TILES, P]) for u in range(2)]
        scaled = [sb(f"scaled{h}", [P, TILES // 2, EXPERTS // 2, P]) for h in range(HALVES)]

        psC = ps("psC", [P, 2, 512])
        psD = ps("psD", [P, 2, 512])
        psE = [ps(f"psE{i}", [P, 2, 512]) for i in range(2)]

        passed_pool, passed_dve, passed_pe = sem("passed_pool3"), sem("passed_dve3"), sem("passed_pe3")
        w_in, fold, fold_v = sem("w_in3"), sem("fold3"), sem("fold_v3")
        t2_in = [sem(f"t2_in{u}") for u in range(4)]
        statc_s, mvc_s, nmc_s, vc_s, rsc_s, bsc_s, t2e_s, xc_s, xw_s, xb_s, ug_s = (
            sem(n) for n in ("statc_s", "mvc_s", "nmc_s", "vc_s", "rsc_s", "bsc_s", "t2e_s", "xc_s", "xw_s", "xb_s",
                             "ug_s"))
        mix_mm, mT_s, we_mm, t3_s = sem("mix_mm"), sem("mT_s"), sem("we_mm"), sem("t3_s")
        state_s, mve_s, nme_s, ve_s, rse_s, bse_s, xe_s, xeT_mm, xh_s, xl_s = (
            sem(n) for n in ("state_s", "mve_s", "nme_s", "ve_s", "rse_s", "bse_s", "xe_s", "xeT_mm", "xh_sm", "xl_s"))
        route_mm, logit_s, route_s, th_s, gateT_mm, gateTh_s, eb_mm, acc_s = (
            sem(n) for n in ("route_mm", "logit_s", "route_s", "th_s", "gateT_mm", "gateTh_s", "eb_mm", "acc_s"))
        gateTl_s = sem("gateTl_s")
        ex_mm, ex_s, scaled_s, sum_s = sem("ex_mm"), sem("ex_s"), sem("scaled_s"), sem("sum_s")
        out_s = [sem(f"out_s{u}") for u in range(2)]

        def view(d):
            return d.rearrange("(h g n v) c -> h g n v c", h=HALVES, g=8, v=FX)

        t2_v, out_v = view(t2_d), view(out_d)
        FIRST, LAST, LOOP0, LOOP1, U = -3, NM, 4, 60, 4
        PAIRS = TILES // 2
        flat = "p t c -> p (t c)"

        def place(v, m, q, h):
            n = m * 4 - q * 4
            s = slice(n, n + FX) if isinstance(n, int) else bass.ds(n, FX)
            return v[h, :, s, q * WID:(q + 1) * WID, :]

        def upto(engine, s, n, per=1):
            need(engine, s, min(n, NM) if isinstance(n, int) else n, per)

        block = ctx.enter_context(nc.Block())

        @block.sync
        def _(sp):
            loads = [(ident[:], io["ident"]), (ln_w[:], io["ln_w"]), (ln_b[:], io["ln_b"]), (be[:], io["be"]),
                     (w1[:], io["W1"].rearrange("(t p) g -> p t g", t=2)),
                     (w2[:], io["W2e"].rearrange("(t p) g -> p t g", t=2)),
                     (w3t[:], io["W3eT"].rearrange("(t p) g -> p t g", t=2)),
                     (b12[:], io["b12"]), (b3[:], io["b3"]), (wet[:], io["WeT"]), (rw[:], io["rw"]),
                     (rb[:], io["rb"]), (dec[:], io["dec"]), (ew[:], io["ew"]), (eb[:], io["eb"])]
            for dst, src in loads:
                sp.dma_start(dst, src).then_inc(w_in, 16)

            def body(m, u):
                if inside(m + 4, NM):
                    upto(sp, xc_s, m + 1)
                    upto(sp, t2e_s, m + 1)
                    for h in range(HALVES):
                        sp.dma_start(t2[u][:, h * WID:(h + 1) * WID, :], place(t2_v, m + 4, u, h)
                                     ).then_inc(t2_in[u], 16)
                if inside(m - 1, NM):
                    q = (u - 1) % 4
                    for h in range(HALVES):
                        sp.wait_ge(sum_s, (m - 1) * 2 * SUMS + (h + 1) * SUMS)
                        sp.dma_start(place(out_v, m - 1, q, h), acc[q % 2][:, h * WID:(h + 1) * WID, :]
                                     ).then_inc(out_s[q % 2], 16)

            pipeline(sp, body, FIRST - 1, LAST + 1, LOOP0, LOOP1, U)
            for u in range(2):
                sp.wait_ge(out_s[u], 32 * NM // 2)

        @block.gpsimd
        def _(pool):
            pool.wait_ge(fold_v, FOLDED)

            def factors(n, mv, mv_s, mul, add, nm, nm_s, v, v_s, rs, rs_s, bs, bs_s, used_s):
                upto(pool, mv_s, n + 1)
                upto(pool, bs_s, n)
                pool.tensor_tensor(nm[:], mv[:, :, 0], minus[:], ALU.mult).then_inc(nm_s, 1)
                upto(pool, rs_s, n)
                settle(pool, passed_pool)
                pool.tensor_scalar(v[:], mv[:, :, 1], mul, add, ALU.mult, ALU.add).then_inc(v_s, 1)
                upto(pool, v_s, n + 1)
                upto(pool, used_s, n - 1)
                pool.tensor_tensor(rs[:], v[:], mhalf[:], ALU.pow).then_inc(rs_s, 1)
                upto(pool, rs_s, n + 1)
                upto(pool, nm_s, n + 1)
                pool.tensor_tensor(bs[:], nm[:], rs[:], ALU.mult).then_inc(bs_s, 1)

            def sum_half(n, v, h):
                x, hs, before = scaled[h], slice(h * WID, (h + 1) * WID), n * 2 * SUMS + h * SUMS
                pool.wait_ge(scaled_s, n * TILES + (h + 1) * TILES // 2)
                pool.tensor_tensor(x[:, :, 0:2, :], x[:, :, 0:2, :], x[:, :, 2:4, :], ALU.add).then_inc(sum_s, 1)
                pool.wait_ge(sum_s, before + 1)
                pool.tensor_tensor(x[:, :, 0, :], x[:, :, 0, :], x[:, :, 1, :], ALU.add).then_inc(sum_s, 1)
                pool.wait_ge(sum_s, before + 2)
                pool.wait_ge(ex_s, n * 4 * TILES + (h + 1) * 2 * TILES)
                pool.tensor_tensor(acc[v][:, hs, :], acc[v][:, hs, :], x[:, :, 0, :], ALU.add).then_inc(sum_s, 1)

            def body(m, u):
                a, b = (u + 1) % 2, u % 2
                if inside(m + 2, NM):
                    upto(pool, xw_s, m + 3)
                    upto(pool, ug_s, m + 2)
                    pool.tensor_tensor(xb[:], xw[:], ln_b[:].unsqueeze(1).to_broadcast([P, TILES, P]),
                                       ALU.add).then_inc(xb_s, 1)
                if inside(m - 1, NM):
                    sum_half(m - 1, a, 1)
                if inside(m + 3, NM):
                    q = (u + 3) % 4
                    pool.wait_ge(t2_in[q], (m + 3 - q) * 8 + 32)
                    upto(pool, t3_s, m + 2)
                    for h in range(HALVES):
                        hs = slice(h * WID, (h + 1) * WID)
                        last = pool.tensor_tensor(t2e[a][:, hs, :], t2[q][:, hs, :],
                                                  out_b[:, h, :].unsqueeze(1).to_broadcast([P, WID, P]), ALU.add)
                    last.then_inc(t2e_s, 1)
                if inside(m + 3, NM):
                    factors(m + 3, mvc, mvc_s, TWICE_MUL, TWICE_ADD, nmc, nmc_s, vc, vc_s, rsc[a], rsc_s, bsc[a],
                            bsc_s, xc_s)
                if inside(m, NM):
                    sum_half(m, b, 0)
                if inside(m + 2, NM):
                    factors(m + 2, mve, mve_s, 1.0, EPS_LN, nme, nme_s, ve, ve_s, rse[b], rse_s, bse[b], bse_s, xe_s)

            pipeline(pool, body, FIRST, LAST + 1, LOOP0, LOOP1, U)

        @block.vector
        def _(dve):
            dve.wait_ge(w_in, 15 * 16)
            for i in range(4):
                dve.tensor_copy(b12w[:, i, :], b12[:, i:i + 1].to_broadcast([P, P]))
            dve.memset(mhalf[:], -0.5)
            dve.memset(minus[:], -1.0)
            dve.tensor_copy(rwhl[:, 0, :], rw[:])
            dve.tensor_copy(ebh[:], eb[:])
            dve.tensor_copy(ewh[:], ew[:]).then_inc(fold_v, 1)
            dve.wait_ge(fold_v, 1)
            dve.tensor_tensor(rwhl[:, 1, :], rw[:], rwhl[:, 0, :].bitcast(F32), ALU.subtract)
            dve.tensor_tensor(ebl[:], eb[:], ebh[:].bitcast(F32), ALU.subtract)
            dve.tensor_tensor(ewl[:], ew[:], ewh[:].bitcast(F32), ALU.subtract)
            dve.wait_ge(fold, 1)
            dve.tensor_copy(w32[:].rearrange("p t g -> p (t g)"), psC[:, 0, :]).then_inc(fold_v, 1)
            dve.wait_ge(fold, 2)
            dve.tensor_copy(mix[:].rearrange("p t g -> p (t g)"), psD[:, 0, :])
            dve.tensor_tensor(mix_b[:], psD[:, 1, 0:COLS], b3[:], ALU.add).then_inc(fold_v, 1)
            dve.wait_ge(fold, 3)
            dve.tensor_tensor(out_b[:], psC[:, 0, 0:COLS].rearrange("p (h c) -> p h c", h=HALVES),
                              be[:].unsqueeze(1).to_broadcast([P, HALVES, P]), ALU.add).then_inc(fold_v, 1)
            dve.wait_ge(fold_v, FOLDED)

            def route(m, a, n):
                wide = [P, TILES, EXPERTS]
                over = lambda v: v[:].unsqueeze(2).to_broadcast(wide)
                if n:
                    dve.wait_ge(route_s, m * ROUTE + n)
                if n in (0, 6):
                    i = n // 6
                    if n == 0:
                        upto(dve, logit_s, m + 1, 2)
                    ins = dve.tensor_reduce(top[i][:], (logit2 if i else logit)[:], AX.X, ALU.max)
                elif n in (1, 8):
                    i = n // 8
                    ins = dve.tensor_tensor(is_max[:], (logit2 if i else logit)[:], over(top[i]), ALU.is_equal)
                elif n in (2, 9):
                    ins = dve.tensor_tensor(order[:], is_max[:], dec[:].unsqueeze(1).to_broadcast(wide), ALU.mult)
                elif n in (3, 10):
                    ins = dve.tensor_reduce(first[:], order[:], AX.X, ALU.max)
                elif n in (4, 11):
                    ins = dve.tensor_tensor(pick[n // 11][:], order[:], over(first), ALU.is_equal)
                elif n == 5:
                    ins = dve.scalar_tensor_tensor(logit2[:], pick[0][:], -3e38, logit[:], ALU.mult, ALU.add)
                elif n == GAP - 1:
                    upto(dve, th_s, m)
                    ins = dve.tensor_tensor(gap[:], top[0][:], top[1][:], ALU.subtract)
                elif n == 12:
                    upto(dve, th_s, m + 1)
                    for i, sign in ((0, 0.5), (1, -0.5)):
                        ins = dve.tensor_scalar(wgt[i][:], th[:], sign, 0.5, ALU.mult, ALU.add)
                elif n == 13:
                    for i in range(2):
                        ins = dve.tensor_tensor(share[i][:], pick[i][:], over(wgt[i]), ALU.mult)
                else:
                    upto(dve, gateT_mm, m - 1)
                    upto(dve, scaled_s, m - 1, TILES)
                    ins = dve.tensor_tensor(gate[a][:], share[0][:], share[1][:], ALU.add)
                ins.then_inc(route_s, 1)

            def body(m, u):
                a, b = (u + 1) % 2, u % 2
                steps = iter(range(ROUTE if inside(m + 1, NM) else 0))

                def route_next():
                    for n in steps:
                        route(m + 1, a, n)
                        break

                for p in range(PAIRS):
                    if inside(m, NM):
                        for e in range(4):
                            for i in range(2):
                                t = 2 * p + i
                                if e == 0:
                                    dve.wait_ge(ex_mm, (m * PAIRS + p) * 4 + i + 1)
                                if p == 0 and e == 0 and i == 0:
                                    upto(dve, acc_s, m + 1)
                                    upto(dve, route_s, m + 1, ROUTE)
                                if e:
                                    dve.wait_ge(ex_s, (m * PAIRS + p) * 8 + 2 * (e - 1) + i + 1)
                                dve.scalar_tensor_tensor(
                                    acc[b][:, t, :], psE[i][:, 0, e * P:(e + 1) * P],
                                    gate[b][:, t, e:e + 1], acc[b][:, t, :], ALU.mult, ALU.add).then_inc(ex_s, 1)
                                if p == 2:
                                    route_next()
                    if p == 0 and inside(m + 1, NM):
                        upto(dve, xh_s, m + 2)
                        dve.tensor_tensor(xl[a][:].rearrange(flat), psC[:].rearrange("p k n -> p (k n)"),
                                          xh[a][:].bitcast(F32).rearrange(flat), ALU.subtract).then_inc(xl_s, 1)
                    if p == 1 and inside(m + 1, NM):
                        upto(dve, route_mm, m + 2)
                        parts = psD[:, 0, 0:TILES * 2 * EXPERTS].rearrange("p (t i e) -> p t i e", t=TILES, i=2)
                        dve.tensor_tensor(logit_h[:], parts[:, :, 0, :],
                                          rb[:].unsqueeze(1).to_broadcast([P, TILES, EXPERTS]), ALU.add
                                          ).then_inc(logit_s, 1)
                        dve.wait_ge(logit_s, (m + 1) * 2 + 1)
                        dve.tensor_tensor(logit[:], parts[:, :, 1, :], logit_h[:], ALU.add).then_inc(logit_s, 1)
                    if p == 1 and inside(m + 3, NM):
                        q = (u + 3) % 4
                        dve.wait_ge(t2_in[q], (m + 3 - q) * 8 + 32)
                        upto(dve, mvc_s, m + 3)
                        for t in range(TILES):
                            last = dve.bn_stats(statc[:, t, :], t2[q][:, t, :])
                            if t == TILES - 1:
                                last.then_inc(statc_s, 1)
                            route_next()
                        upto(dve, statc_s, m + 4)
                        upto(dve, vc_s, m + 3)
                        upto(dve, nmc_s, m + 3)
                        settle(dve, passed_dve)
                        for t in range(TILES):
                            last = dve.bn_aggr(mvc[:, t, :], statc[:, t, :])
                        last.then_inc(mvc_s, 1)
                    if p == 2:
                        for _ in range(ROUTE):
                            route_next()
                    if p == 2 and inside(m + 2, NM):
                        upto(dve, we_mm, m + 3)
                        upto(dve, t2e_s, m + 3)
                        dve.tensor_tensor(t3[b][:].rearrange(flat), psD[:].rearrange("p k n -> p (k n)"),
                                          t2e[b][:].rearrange(flat), ALU.add).then_inc(t3_s, 1)
                        upto(dve, t3_s, m + 3)
                        upto(dve, mve_s, m + 2)
                        for t in range(TILES):
                            last = dve.bn_stats(state[:, t, :], t3[b][:, t, :])
                        last.then_inc(state_s, 1)
                        upto(dve, state_s, m + 3)
                        upto(dve, ve_s, m + 2)
                        upto(dve, nme_s, m + 2)
                        settle(dve, passed_dve)
                        for t in range(TILES):
                            last = dve.bn_aggr(mve[:, t, :], state[:, t, :])
                        last.then_inc(mve_s, 1)
                    if p == 2 and inside(m + 1, NM):
                        upto(dve, gateTh_s, m + 2)
                        upto(dve, eb_mm, m)
                        dve.tensor_tensor(gateTl[a][:], psD[0:TILES * EXPERTS, 0, 0:P], gateTh[a][:].bitcast(F32),
                                          ALU.subtract).then_inc(gateTl_s, 1)
                    if p == 3 and inside(m + 3, NM):
                        upto(dve, xc_s, m + 4)
                        upto(dve, xb_s, m + 3)
                        dve.tensor_tensor(xw[:], xc[:], ln_w[:].unsqueeze(1).to_broadcast([P, TILES, P]),
                                          ALU.mult).then_inc(xw_s, 1)
                    if p == 3 and inside(m + 1, NM):
                        upto(dve, eb_mm, m + 2)
                        need(dve, out_s[a], m + 1 - a, 16)
                        dve.tensor_tensor(acc[a][:].rearrange(flat), psD[:].rearrange("p k n -> p (k n)"),
                                          t3[a][:].rearrange(flat), ALU.add).then_inc(acc_s, 1)

            pipeline(dve, body, FIRST, LAST, LOOP0, LOOP1, U)

        @block.scalar
        def _(act):
            def scale_pair(m, b, p):
                for i in range(2):
                    t = 2 * p + i
                    act.wait_ge(ex_mm, (m * PAIRS + p) * 4 + 2 + i + 1)
                    if t == 0:
                        upto(act, route_s, m + 1, ROUTE)
                    if t % WID == 0 and not (isinstance(m, int) and m == 0):
                        act.wait_ge(sum_s, (m - 1) * 2 * SUMS + (t // WID + 1) * SUMS)
                    for e in range(4):
                        last = act.activation(scaled[t // WID][:, t % WID, e, :], psE[i][:, 1, e * P:(e + 1) * P],
                                              ACT.Identity, scale=gate[b][:, t, 4 + e:5 + e])
                    last.then_inc(scaled_s, 1)

            def body(m, u):
                a, b = (u + 1) % 2, u % 2
                if inside(m, NM):
                    scale_pair(m, b, 0)
                if inside(m + 1, NM):
                    upto(act, xeT_mm, m + 2)
                    upto(act, ex_mm, m, 4 * PAIRS)
                    upto(act, route_mm, m)
                    for i in range(2):
                        last = act.activation(xh[a][:, i * WID:(i + 1) * WID].rearrange(flat), psC[:, i, :],
                                              ACT.Identity)
                    last.then_inc(xh_s, 1)
                if inside(m + 2, NM):
                    upto(act, xb_s, m + 3)
                    upto(act, mix_mm, m + 1)
                    act.activation(ug[b][:], xb[:], ACT.Gelu).then_inc(ug_s, 1)
                if inside(m, NM):
                    scale_pair(m, b, 1)
                if inside(m + 2, NM):
                    upto(act, mix_mm, m + 3)
                    upto(act, we_mm, m + 1)
                    for i in range(2):
                        last = act.activation(mT[b][:, 2 * i:2 * i + 2].rearrange("p w g -> p (w g)"), psC[:, i, :],
                                              ACT.Identity)
                    last.then_inc(mT_s, 1)
                if inside(m + 1, NM):
                    act.wait_ge(route_s, (m + 1) * ROUTE + GAP)
                    act.activation(th[:], gap[:], ACT.Tanh, scale=0.5).then_inc(th_s, 1)
                if inside(m + 3, NM):
                    upto(act, bsc_s, m + 4)
                    upto(act, xw_s, m + 3)
                    for t in range(TILES):
                        last = act.activation(xc[:, t, :], t2[(u + 3) % 4][:, t, :], ACT.Identity,
                                              bias=bsc[a][:, t:t + 1], scale=rsc[a][:, t:t + 1])
                    last.then_inc(xc_s, 1)
                if inside(m, NM):
                    scale_pair(m, b, 2)
                if inside(m + 1, NM):
                    upto(act, gateT_mm, m + 2)
                    upto(act, eb_mm, m)
                    act.activation(gateTh[a][:], psD[0:TILES * EXPERTS, 0, 0:P], ACT.Identity).then_inc(gateTh_s, 1)
                if inside(m, NM):
                    scale_pair(m, b, 3)
                if inside(m + 2, NM):
                    upto(act, bse_s, m + 3)
                    upto(act, xeT_mm, m + 1)
                    for t in range(TILES):
                        last = act.activation(xe[b][:, t, :], t3[b][:, t, :], ACT.Identity,
                                              bias=bse[b][:, t:t + 1], scale=rse[b][:, t:t + 1])
                    last.then_inc(xe_s, 1)

            pipeline(act, body, FIRST, LAST, LOOP0, LOOP1, U)

        @block.tensor
        def _(pe):
            pe.wait_ge(w_in, 15 * 16)
            pe.wait_ge(fold_v, 1)
            for o in range(2):
                for t in range(2):
                    last = pe.matmul(psC[:, 0, o * COLS:(o + 1) * COLS], w2[:, t, o * P:(o + 1) * P], w3t[:, t, :],
                                     start=t == 0, stop=t == 1)
            last.then_inc(fold, 1)
            pe.wait_ge(fold_v, 2)
            for o in range(2):
                for t in range(2):
                    pe.matmul(psD[:, 0, o * COLS:(o + 1) * COLS], w1[:, t, o * P:(o + 1) * P], w32[:, t, :],
                              start=t == 0, stop=t == 1)
            for i in range(4):
                last = pe.matmul(psD[:, 1, 0:COLS], b12w[:, i, :], (w32 if i < 2 else w3t)[:, i % 2, :],
                                 start=i == 0, stop=i == 3)
            last.then_inc(fold, 1)
            pe.wait_ge(fold_v, 3)
            for h in range(HALVES):
                last = pe.matmul(psC[:, 0, h * P:(h + 1) * P], mix_b[:, h * P:(h + 1) * P], wet[:], start=True, stop=True)
            last.then_inc(fold, 1)
            pe.wait_ge(fold_v, FOLDED)

            def transpose_gates(m, a):
                upto(pe, route_s, m + 2, ROUTE)
                upto(pe, t3_s, m + 3)
                settle(pe, passed_pe)
                pe.transpose(psD[0:TILES * EXPERTS, 0, 0:P], gate[a][:].rearrange("p t e -> p (t e)"),
                             ident[:]).then_inc(gateT_mm, 1)

            def body(m, u):
                a, b = (u + 1) % 2, u % 2
                for p in range(PAIRS):
                    for half in range(2):
                        if inside(m, NM):
                            for i in range(2):
                                t = 2 * p + i
                                if not (isinstance(m, int) and m == 0 and p == 0):
                                    if half == 0:
                                        pe.wait_ge(ex_s, (m * PAIRS + p) * 8 - 1 + i)
                                    else:
                                        pe.wait_ge(scaled_s, (m * PAIRS + p) * 2 - 1 + i)
                                ws = slice(half * 512, (half + 1) * 512)
                                split3(pe, psE[i][:, half, :], xh[b][:, t, :], xl[b][:, t, :], ewh[:, ws],
                                       ewl[:, ws]).then_inc(ex_mm, 1)
                        if (p, half) == (3, 0) and inside(m + 1, NM):
                            transpose_gates(m, a)
                    if p == 0 and inside(m + 1, NM):
                        upto(pe, xe_s, m + 2)
                        upto(pe, mT_s, m + 2)
                        for t in range(TILES):
                            last = pe.transpose(psC[:, t // 4, (t % 4) * P:(t % 4 + 1) * P], xe[a][:, t, :], ident[:])
                        last.then_inc(xeT_mm, 1)
                    if p == 1 and inside(m + 1, NM):
                        upto(pe, xl_s, m + 2)
                        upto(pe, acc_s, m + 1)
                        for t in range(TILES):
                            both = psD[:, 0, t * 2 * EXPERTS:(t + 1) * 2 * EXPERTS]
                            w_parts = rwhl[:].rearrange("p i e -> p (i e)")
                            pe.matmul(both, xh[a][:, t, :], w_parts, start=True, stop=False)
                            last = pe.matmul(both, xl[a][:, t, :], w_parts, start=False, stop=True)
                        last.then_inc(route_mm, 1)
                    if p == 1 and inside(m + 2, NM):
                        upto(pe, ug_s, m + 3)
                        upto(pe, xl_s, m + 2)
                        for w in range(WID):
                            for h in range(HALVES):
                                last = pe.matmul(psC[:, w // 2, (w % 2) * COLS:(w % 2 + 1) * COLS],
                                                 ug[b][:, h * WID + w, :], mix[:, h, :], start=h == 0, stop=h == 1)
                        last.then_inc(mix_mm, 1)
                    if p == 2 and inside(m + 2, NM):
                        upto(pe, mT_s, m + 3)
                        upto(pe, logit_s, m + 2, 2)
                        for h in range(HALVES):
                            for w in range(WID):
                                last = pe.matmul(psD[:, h, w * P:(w + 1) * P], mT[b][:, w, h * P:(h + 1) * P], wet[:],
                                                 start=True, stop=True)
                        last.then_inc(we_mm, 1)
                    if p == 3 and inside(m + 1, NM):
                        upto(pe, gateTl_s, m + 2)
                        for h in range(2):
                            hs = slice(h * 512, (h + 1) * 512)
                            last = split3(pe, psD[:, h, :], gateTh[a][:], gateTl[a][:], ebh[:, hs], ebl[:, hs])
                        last.then_inc(eb_mm, 1)

            pipeline(pe, body, FIRST, LAST, LOOP0, LOOP1, U)


def metaformer(nc, io, out_d):
    zt_d = nc.dram_tensor("zt_scratch", [P, TOK], F32, kind="Internal").ap()
    bias_d = nc.dram_tensor("bias_scratch", [ROWS, HEADS, COLS], F32, kind="Internal").ap()
    t1_d = nc.dram_tensor("t1_scratch", [TOK, P], F32, kind="Internal").ap()
    t2_d = nc.dram_tensor("t2_scratch", [TOK, P], F32, kind="Internal").ap()
    wx_d = nc.dram_tensor("wx_scratch", [P, WARM + TOK], F32, kind="Internal").ap()
    with nc.sbuf_tensor("bn_sb", [P, 2], F32) as bn_sb:
        norm_pass(nc, io, zt_d, bias_d)
        attention_pass(nc, io, zt_d, bias_d, t1_d, wx_d, bn_sb)
        recurrence_pass(nc, io, t1_d, wx_d, t2_d, bn_sb)
        mixer_pass(nc, io, t2_d, out_d)


def layouts(a):
    f = np.float32
    rows = lambda v: np.ascontiguousarray(np.broadcast_to(v, (P, v.shape[-1])))
    io = {"x": a["x"].reshape(TOK, P)}
    for n in ("Wq", "Wk", "Wv", "Wg", "Wo"):
        io[n] = a["L0_conv_" + n]
    io["WbPad"] = np.zeros((P, DH), f)
    io["WbPad"][:, :HEADS] = a["L0_conv_Wb"]
    io["ln_cols"] = np.stack([a["L0_conv_ln_scale"], a["L0_conv_ln_bias"]], axis=1)
    io["WT"], io["VT"] = a["L0_ffn_W"].T, a["L0_ffn_V"].T
    io["bn_cols"] = np.stack([a["L0_ffn_gamma"], a["L0_ffn_beta"]], axis=1)
    io["ln_w"], io["ln_b"], io["be"] = rows(a["L1_conv_ln_w"]), rows(a["L1_conv_ln_b"]), rows(a["L1_conv_be"])
    io["W1"] = a["L1_conv_W1"]
    w2 = np.zeros((8, 2, 8, 2, 8, 2, 8, 2), f)
    w3t = np.zeros((2, 8, 2, 8, 2, 8, 2, 8), f)
    for i in range(2):
        for j in range(2):
            w2[:, i, :, j, :, i, :, j] = a["L1_conv_W2"].reshape(8, 8, 8, 8)
    for i in range(8):
        for j in range(8):
            w3t[:, i, :, j, :, i, :, j] = a["L1_conv_W3"].T.reshape(2, 2, 2, 2)
    io["W2e"], io["W3eT"] = w2.reshape(COLS, COLS), w3t.reshape(COLS, COLS)
    b2 = np.broadcast_to(a["L1_conv_b2"].reshape(8, 1, 8, 1), (8, 2, 8, 2)).reshape(COLS)
    b3 = np.broadcast_to(a["L1_conv_b3"].reshape(2, 1, 2, 1), (2, 8, 2, 8)).reshape(COLS)
    io["b12"] = np.stack([a["L1_conv_b1"][:P], a["L1_conv_b1"][P:], b2[:P], b2[P:]], axis=1)
    io["b3"] = rows(b3)
    io["WeT"] = a["L1_conv_We"].T
    io["rw"], io["rb"] = a["L1_ffn_router_w"], rows(a["L1_ffn_router_b"])
    io["ew"] = a["L1_ffn_expert_w"].transpose(1, 0, 2).reshape(P, EXPERTS * P)
    eb = np.zeros((TILES, EXPERTS, TILES, P), f)
    for t in range(TILES):
        eb[t, :, t, :] = a["L1_ffn_expert_b"]
    io["eb"] = eb.reshape(TILES * EXPERTS, TILES * P)
    io["ident"] = np.eye(P, dtype=f)
    io["dec"] = rows(np.arange(EXPERTS, 0, -1).astype(f))
    return {n: np.ascontiguousarray(v) for n, v in io.items()}


def kernel(**inputs):
    import concourse.bacc as bacc
    from concourse.bass_utils import run_bass_kernel_spmd

    arrays = layouts({n: np.asarray(v) for n, v in inputs.items()})
    nc = bacc.Bacc("TRN2", target_bir_lowering=False, num_devices=1)
    io = {n: nc.dram_tensor("in_" + n, v.shape, F32, kind="ExternalInput").ap() for n, v in arrays.items()}
    out = nc.dram_tensor("out", (TOK, P), F32, kind="ExternalOutput").ap()
    metaformer(nc, io, out)
    r = run_bass_kernel_spmd(nc, [{"in_" + n: v for n, v in arrays.items()}], core_ids=[0])
    return r.results[0]["out"].reshape(1, ROWS, COLS, P)
```
